# Optimizing a Trainium2 kernel written in Bass

```python
import numpy as np
import jax
import jax.numpy as jnp

def _softmax(x, axis=-1):
    return jax.nn.softmax(x, axis=axis)

def _gelu(x):
    return jax.nn.gelu(x, approximate=True)

def _silu(x):
    return jax.nn.silu(x)

def _sigmoid(x):
    return jax.nn.sigmoid(x)

def _layernorm(x, axis=-1, eps=1e-05):
    m = jnp.mean(x, axis=axis, keepdims=True)
    v = jnp.var(x, axis=axis, keepdims=True)
    return (x - m) / jnp.sqrt(v + eps)

def _scatter_add(tgt, idx, src, axis=0):
    return tgt.at[idx].add(src)

def _segment_sum(src, seg, n):
    return jax.ops.segment_sum(src, seg, n)
kernel_name = 'mk_gnn_preln_d4_gnn_r32_5a6da7'

def setup_inputs(seed: int=0):
    np.random.seed(seed)
    _w = jnp.asarray

    def _rec_inputs():
        import jax
        import jax.numpy as jnp
        _gk = jax.random.key(seed)
        x = -0.000202 + 1 * jax.random.normal(jax.random.fold_in(_gk, 1), (50000, 128), jnp.float32)
        src = jax.random.randint(jax.random.fold_in(_gk, 2), (25000,), 0, 50000, jnp.int32)
        dst = jnp.minimum((50000 * jax.random.uniform(jax.random.fold_in(_gk, 3), (25000,)) ** 2.0).astype(jnp.int32), 49999)
        _o = jnp.argsort(dst, stable=True)
        src = src[_o]
        dst = dst[_o]
        edge_attr_4 = 0.000398945 + 1.00003 * jax.random.normal(jax.random.fold_in(_gk, 12), (25000, 4), jnp.float32)
        return (x, src, dst, edge_attr_4)
    x, src, dst, edge_attr_4 = _rec_inputs()

    def _L0_gnn_setup():
        import jax, jax.numpy as jnp
        import numpy as np
        N = 50000
        E = 25000
        H = 128
        key = jax.random.key(seed)
        k1, k2, k3, k4, k5 = jax.random.split(key, 5)
        s = 1.0 / np.sqrt(H).astype(np.float32)
        x = jax.random.normal(k1, (N, H), dtype=jnp.float32)
        edge_index = jax.random.randint(k2, (2, E), 0, N, dtype=jnp.int64)
        a_i = jax.random.normal(k3, (H,), dtype=jnp.float32) * s
        a_j = jax.random.normal(k4, (H,), dtype=jnp.float32) * s
        W = jax.random.normal(k5, (H, H), dtype=jnp.float32) * s
        return {'x': x, 'edge_index': edge_index, 'a_i': a_i, 'a_j': a_j, 'W': W}
    _L0_gnn_all = _L0_gnn_setup()
    _L0_gnn_in = {k: v for k, v in _L0_gnn_all.items() if k in ('a_i', 'a_j', 'W')}
    del _L0_gnn_all

    def _L1_gnn_setup():
        import jax, jax.numpy as jnp
        import numpy as np
        N = 3125
        E = 50000
        IN_DIM = 128
        OUT_DIM = 128
        EDGE_DIM = 4
        LN_EPS = 1e-05
        key = jax.random.key(seed)
        ks = jax.random.split(key, 12)
        s_in = 1.0 / np.sqrt(IN_DIM)
        s_ed = 1.0 / np.sqrt(EDGE_DIM)
        s_out = 1.0 / np.sqrt(OUT_DIM)
        s_cat = 1.0 / np.sqrt(IN_DIM + OUT_DIM)
        return {'x': jax.random.normal(ks[0], (N, IN_DIM), jnp.float32), 'edge_index': jax.random.randint(ks[1], (2, E), 0, N, jnp.int32), 'edge_attr': jax.random.normal(ks[2], (E, EDGE_DIM), jnp.float32), 'agg_W': jax.random.uniform(ks[3], (IN_DIM, OUT_DIM), jnp.float32, -s_in, s_in), 'agg_b': jnp.zeros((OUT_DIM,), jnp.float32), 'edge_W1': jax.random.uniform(ks[4], (EDGE_DIM, OUT_DIM), jnp.float32, -s_ed, s_ed), 'edge_b1': jnp.zeros((OUT_DIM,), jnp.float32), 'edge_W2': jax.random.uniform(ks[5], (OUT_DIM, 1), jnp.float32, -s_out, s_out), 'edge_b2': jnp.zeros((1,), jnp.float32), 'upd_W1': jax.random.uniform(ks[6], (IN_DIM + OUT_DIM, OUT_DIM), jnp.float32, -s_cat, s_cat), 'upd_b1': jnp.zeros((OUT_DIM,), jnp.float32), 'upd_W2': jax.random.uniform(ks[7], (OUT_DIM, OUT_DIM), jnp.float32, -s_out, s_out), 'upd_b2': jnp.zeros((OUT_DIM,), jnp.float32), 'ln_g': jnp.ones((OUT_DIM,), jnp.float32), 'ln_b': jnp.zeros((OUT_DIM,), jnp.float32), 'res_W': jax.random.uniform(ks[8], (IN_DIM, OUT_DIM), jnp.float32, -s_in, s_in)}
    _L1_gnn_all = _L1_gnn_setup()
    _L1_gnn_in = {k: v for k, v in _L1_gnn_all.items() if k in ('agg_W', 'agg_b', 'edge_W1', 'edge_b1', 'edge_W2', 'edge_b2', 'upd_W1', 'upd_b1', 'upd_W2', 'upd_b2', 'ln_g', 'ln_b', 'res_W')}
    del _L1_gnn_all

    def _L2_gnn_setup():
        import jax, jax.numpy as jnp
        import numpy as np
        N_NODES = 3125
        N_EDGES = 20000
        D = 128
        key = jax.random.key(seed)
        k1, k2, k3 = jax.random.split(key, 3)
        x = jax.random.normal(k1, (N_NODES, D), dtype=jnp.float32)
        W = jax.random.normal(k2, (D, D), dtype=jnp.float32) * (1.0 / np.sqrt(D))
        edge_index = jax.random.randint(k3, (2, N_EDGES), 0, N_NODES, dtype=jnp.int64)
        return {'x': x, 'W': W, 'edge_index': edge_index}
    _L2_gnn_all = _L2_gnn_setup()
    _L2_gnn_in = {k: v for k, v in _L2_gnn_all.items() if k in ('W',)}
    del _L2_gnn_all

    def _L3_gnn_setup():
        import jax, jax.numpy as jnp
        import numpy as np
        N_NODES = 1250
        N_EDGES = 20000
        D_IN = 128
        D_HID = 256
        D_OUT = 128
        key = jax.random.key(seed)
        ks = jax.random.split(key, 6)
        feat = jax.random.normal(ks[0], (N_NODES, D_IN), dtype=jnp.float32)
        src = jax.random.randint(ks[1], (N_EDGES,), 0, N_NODES)
        dst = jax.random.randint(ks[2], (N_EDGES,), 0, N_NODES)
        eps = jnp.zeros((1,), dtype=jnp.float32)
        W1 = jax.random.normal(ks[3], (D_IN, D_HID), dtype=jnp.float32) * (1.0 / np.sqrt(D_IN))
        b1 = jnp.zeros((D_HID,), dtype=jnp.float32)
        W2 = jax.random.normal(ks[4], (D_HID, D_OUT), dtype=jnp.float32) * (1.0 / np.sqrt(D_HID))
        b2 = jnp.zeros((D_OUT,), dtype=jnp.float32)
        return {'feat': feat, 'src': src, 'dst': dst, 'eps': eps, 'W1': W1, 'b1': b1, 'W2': W2, 'b2': b2}
    _L3_gnn_all = _L3_gnn_setup()
    _L3_gnn_in = {k: v for k, v in _L3_gnn_all.items() if k in ('eps', 'W1', 'b1', 'W2', 'b2')}
    del _L3_gnn_all
    return {'x': x, 'src': src, 'dst': dst, 'edge_attr_4': edge_attr_4, 'L0_gnn_a_i': _L0_gnn_in['a_i'], 'L0_gnn_a_j': _L0_gnn_in['a_j'], 'L0_gnn_W': _L0_gnn_in['W'], 'L1_gnn_agg_W': _L1_gnn_in['agg_W'], 'L1_gnn_agg_b': _L1_gnn_in['agg_b'], 'L1_gnn_edge_W1': _L1_gnn_in['edge_W1'], 'L1_gnn_edge_b1': _L1_gnn_in['edge_b1'], 'L1_gnn_edge_W2': _L1_gnn_in['edge_W2'], 'L1_gnn_edge_b2': _L1_gnn_in['edge_b2'], 'L1_gnn_upd_W1': _L1_gnn_in['upd_W1'], 'L1_gnn_upd_b1': _L1_gnn_in['upd_b1'], 'L1_gnn_upd_W2': _L1_gnn_in['upd_W2'], 'L1_gnn_upd_b2': _L1_gnn_in['upd_b2'], 'L1_gnn_ln_g': _L1_gnn_in['ln_g'], 'L1_gnn_ln_b': _L1_gnn_in['ln_b'], 'L1_gnn_res_W': _L1_gnn_in['res_W'], 'L2_gnn_W': _L2_gnn_in['W'], 'L3_gnn_eps': _L3_gnn_in['eps'], 'L3_gnn_W1': _L3_gnn_in['W1'], 'L3_gnn_b1': _L3_gnn_in['b1'], 'L3_gnn_W2': _L3_gnn_in['W2'], 'L3_gnn_b2': _L3_gnn_in['b2']}

def reference(x, src, dst, edge_attr_4, L0_gnn_a_i, L0_gnn_a_j, L0_gnn_W, L1_gnn_agg_W, L1_gnn_agg_b, L1_gnn_edge_W1, L1_gnn_edge_b1, L1_gnn_edge_W2, L1_gnn_edge_b2, L1_gnn_upd_W1, L1_gnn_upd_b1, L1_gnn_upd_W2, L1_gnn_upd_b2, L1_gnn_ln_g, L1_gnn_ln_b, L1_gnn_res_W, L2_gnn_W, L3_gnn_eps, L3_gnn_W1, L3_gnn_b1, L3_gnn_W2, L3_gnn_b2):
    import jax
    import jax.numpy as jnp

    def _L0_gnn_ref(x, edge_index, a_i, a_j, W):
        import jax, jax.numpy as jnp
        import numpy as np
        N = 50000
        E = 25000
        H = 128
        n = x.shape[0]
        idx_j = edge_index[0]
        idx_i = edge_index[1]
        si = x @ a_i
        sj = x @ a_j
        e = jax.nn.leaky_relu(si[idx_i] + sj[idx_j], negative_slope=0.01)
        seg_max = jax.ops.segment_max(e, idx_i, num_segments=n)
        e_exp = jnp.exp(e - seg_max[idx_i])
        denom = jax.ops.segment_sum(e_exp, idx_i, num_segments=n)
        alpha = e_exp / denom[idx_i]
        m = x + x @ W
        out = jax.ops.segment_sum(alpha[:, None] * m[idx_i], idx_j, num_segments=n)
        return jax.nn.gelu(out, approximate=False)

    def _L1_gnn_ref(x, edge_index, edge_attr, agg_W, agg_b, edge_W1, edge_b1, edge_W2, edge_b2, upd_W1, upd_b1, upd_W2, upd_b2, ln_g, ln_b, res_W):
        import jax, jax.numpy as jnp
        import numpy as np
        N = 3125
        E = 50000
        IN_DIM = 128
        OUT_DIM = 128
        EDGE_DIM = 4
        LN_EPS = 1e-05
        n = x.shape[0]
        src, dst = (edge_index[0], edge_index[1])
        e_h = jax.nn.silu(edge_attr @ edge_W1 + edge_b1)
        e_w = jax.nn.sigmoid(e_h @ edge_W2 + edge_b2)
        x_agg = jax.nn.silu(x[src] @ agg_W + agg_b) * e_w
        out = jax.ops.segment_sum(x_agg, dst, num_segments=n)
        cnt = jax.ops.segment_sum(jnp.ones((dst.shape[0],), x.dtype), dst, num_segments=n)
        out = out / jnp.maximum(cnt, 1.0)[:, None]
        h = jnp.concatenate([x, out], axis=-1)
        h = jax.nn.silu(h @ upd_W1 + upd_b1) @ upd_W2 + upd_b2
        h = h + x @ res_W
        mu = jnp.mean(h, axis=-1, keepdims=True)
        var = jnp.mean(jnp.square(h - mu), axis=-1, keepdims=True)
        h = (h - mu) * jax.lax.rsqrt(var + LN_EPS) * ln_g + ln_b
        return h

    def _L2_gnn_ref(x, W, edge_index):
        import jax, jax.numpy as jnp
        import numpy as np
        N_NODES = 3125
        N_EDGES = 20000
        D = 128
        h = jnp.matmul(x, W.T)
        src, dst = (edge_index[0], edge_index[1])
        out = jax.ops.segment_sum(h[src], dst, num_segments=x.shape[0])
        return out

    def _L3_gnn_ref(feat, src, dst, eps, W1, b1, W2, b2):
        import jax, jax.numpy as jnp
        import numpy as np
        N_NODES = 1250
        N_EDGES = 20000
        D_IN = 128
        D_HID = 256
        D_OUT = 128
        n = feat.shape[0]
        msgs = feat[src]
        summed = jax.ops.segment_sum(msgs, dst, num_segments=n)
        deg = jax.ops.segment_sum(jnp.ones((src.shape[0],), feat.dtype), dst, num_segments=n)
        neigh = summed / jnp.maximum(deg, 1.0)[:, None]
        rst = (1.0 + eps[0]) * feat + neigh
        h = jax.nn.relu(rst @ W1 + b1)
        h = jax.nn.relu(h @ W2 + b2)
        return h
    edge_index = jnp.stack([src, dst])
    h = jnp.maximum(_layernorm(x, axis=-1), 0.0)
    x = x + _L0_gnn_ref(h, edge_index, L0_gnn_a_i, L0_gnn_a_j, L0_gnn_W)
    h = jnp.maximum(_layernorm(x, axis=-1), 0.0)
    x = x + _L1_gnn_ref(h, edge_index, edge_attr_4, L1_gnn_agg_W, L1_gnn_agg_b, L1_gnn_edge_W1, L1_gnn_edge_b1, L1_gnn_edge_W2, L1_gnn_edge_b2, L1_gnn_upd_W1, L1_gnn_upd_b1, L1_gnn_upd_W2, L1_gnn_upd_b2, L1_gnn_ln_g, L1_gnn_ln_b, L1_gnn_res_W)
    h = jnp.maximum(_layernorm(x, axis=-1), 0.0)
    x = x + _L2_gnn_ref(h, L2_gnn_W, edge_index)
    h = jnp.maximum(_layernorm(x, axis=-1), 0.0)
    x = x + _L3_gnn_ref(h, src, dst, L3_gnn_eps, L3_gnn_W1, L3_gnn_b1, L3_gnn_W2, L3_gnn_b2)
    return x

_drawn_inputs = setup_inputs


def setup_inputs(seed=0):
    import zlib

    import numpy as np

    out = dict(_drawn_inputs(seed))
    spreads = {'L1_gnn_agg_b': (0.0, 0.8),
     'L1_gnn_edge_b1': (0.0, 2.0),
     'L1_gnn_upd_b1': (0.0, 0.1),
     'L1_gnn_upd_b2': (0.0, 0.1),
     'L1_gnn_ln_g': (1.0, 0.2),
     'L1_gnn_ln_b': (0.0, 0.1),
     'L3_gnn_b1': (0.0, 0.292),
     'L3_gnn_b2': (0.0, 0.1)}
    factors = {'edge_attr_4': 8.0,
     'L0_gnn_a_i': 9.415,
     'L1_gnn_agg_W': 5.118,
     'L1_gnn_edge_W1': 8.0,
     'L1_gnn_edge_W2': 8.0}
    for name, (base, spread) in spreads.items():
        noise = np.random.default_rng([zlib.crc32(name.encode()), seed]).standard_normal(out[name].shape)
        drawn = base * np.exp(spread * noise) if base else spread * noise
        out[name] = jnp.asarray(drawn.astype(out[name].dtype))
    for name, factor in factors.items():
        out[name] = (out[name] * factor).astype(out[name].dtype)
    return out
```

```python
from contextlib import ExitStack

import concourse.bass as bass
from concourse import mybir

F32 = mybir.dt.float32
BF16 = mybir.dt.bfloat16
I32 = mybir.dt.int32
ALU = mybir.AluOpType
ACT = mybir.ActivationFunctionType

N = 50000
E = 25000
D = 128
P = 125
ET = E // P
K = 4
EG = ET // K
NG = N // (P * K)
GC = P * K
EPS = 1e-5
BIG = 1e38
DUMP = 2 * K * P
SKIP = 1 << 24
FILL = 16


def ds(start, size):
    return bass.ds(start, size)


class Steps:

    def __init__(self, eng, sem, base, held=None):
        self.eng, self.sem, self.base, self.n, self.held = eng, sem, base, 0, held

    def __call__(self, ins):
        ins.then_inc(self.sem, 1)
        self.n += 1
        self.eng.wait_ge(self.sem, self.base + self.n)


STATS = 14
MAGIC = 0x5F3759DF


class Stats:

    def __init__(self, t_, name, n):
        self.n = n
        self.st, self.mv = t_(name + "_st", [P, n, 6]), t_(name + "_mv", [P, n, 2])
        self.v, self.a, self.y, self.nmr = (t_(f"{name}_{s}", [P, n]) for s in ("v", "a", "y", "nmr"))
        self.mean, self.rstd = self.mv[:, :, 0], self.y


def row_stats(dve, step, rows, s):
    for k in range(s.n):
        last = dve.bn_stats(s.st[:, k, :], rows(k))
    step(last)
    dve.sem_inc(step.held, 1)
    for k in range(s.n):
        last = dve.bn_aggr(s.mv[:, k, :], s.st[:, k, :])
    step(last)
    v, a, y = s.v[:, :], s.a[:, :], s.y[:, :]
    step(dve.tensor_scalar(v, s.mv[:, :, 1], EPS, None, ALU.add))
    step(dve.tensor_scalar(a.bitcast(I32), v.bitcast(I32), 1, None, ALU.logical_shift_right))
    step(dve.tensor_scalar(y.bitcast(I32), a.bitcast(I32), -1.0, float(MAGIC), ALU.mult, ALU.add))
    for _ in range(3):
        step(dve.scalar_tensor_tensor(a, y, -0.5, y, ALU.mult, ALU.mult))
        step(dve.tensor_tensor(a, a, v, ALU.mult))
        step(dve.scalar_tensor_tensor(y, a, 1.5, y, ALU.add, ALU.mult))


def program(nc, a, out):
    with ExitStack() as whole:
        bank = [whole.enter_context(nc.psum_tensor(f"bank{i}", [128, 512], F32)) for i in range(8)]

        made = {}

        def sem(name):
            if name not in made:
                made[name] = whole.enter_context(nc.semaphore(name))
            return made[name]

        def sb(name, shape, dt=F32, ctx=whole):
            return ctx.enter_context(nc.sbuf_tensor(name, shape, dt))

        def dram(name, rows):
            return nc.dram_tensor(name, (rows, D), F32, kind="Internal").ap()

        agg0 = dram("agg0", N + DUMP)
        agg1 = dram("agg1", N)
        x1 = dram("x1", N)
        x2 = dram("x2", N)
        x3 = dram("x3", N + DUMP)

        ident = sb("ident", [128, 128])
        dst_t = sb("dst_t", [P, ET], I32)
        src_t = sb("src_t", [P, ET], I32)
        key_t = sb("key_t", [P, ET])
        prev_t = sb("prev_t", [P, ET])
        end_t = sb("end_t", [P, ET], I32)
        add_t = sb("add_t", [P, ET], I32)
        ew_t = sb("ew_t", [P, ET])

        node_rows = lambda ap, g: ap[ds(g * GC, GC), :].rearrange("(p k) d -> p k d", k=K)

        prepare(nc, a, sem, sb, bank, ident, dst_t, src_t, key_t, prev_t, end_t, add_t)
        with ExitStack() as ctx:
            esb = lambda name, shape, dt=F32: sb(name, shape, dt, ctx)
            h_dst = esb("h_dst", [P, ET * D])
            si = esb("si", [P, ET])
            sj = esb("sj", [P, ET])
            alpha = esb("alpha", [P, ET])
            src_p = esb("src_p", [P, ET], I32)
            dst_p = esb("dst_p", [P, ET], I32)
            edge_rows(nc, a, sem, sb, bank, agg0, agg1, x3, h_dst, si, sj, src_p, dst_p, ew_t)
            softmax(nc, sem, sb, bank, ident, si, sj, dst_p, alpha)
            scatter_by_source(nc, a, sem, sb, bank, agg0, h_dst, alpha, src_p)
        layer0_nodes(nc, a, sem, sb, bank, ident, agg0, x1, node_rows)
        edges(nc, a, sem, sb, bank, 1, ident, x1, agg1, src_t, key_t, prev_t, end_t, ew_t)
        layer1_nodes(nc, a, sem, sb, bank, ident, x1, agg1, x2, x3, node_rows)
        edges(nc, a, sem, sb, bank, 2, ident, x2, x3, src_t, key_t, prev_t, add_t, ew_t)
        edges(nc, a, sem, sb, bank, 3, ident, x3, agg1, src_t, key_t, prev_t, end_t, ew_t)
        layer3_nodes(nc, a, sem, sb, bank, ident, x3, agg1, out, node_rows)


def prepare(nc, a, sem, sb, bank, ident, dst_t, src_t, key_t, prev_t, end_t, add_t):
    with ExitStack() as ctx:
        loaded, made, step_s = sem("p_loaded"), sem("p_made"), sem("p_step")
        nxt = sb("nxt", [P, ET], F32, ctx)
        nxt_i = sb("nxt_i", [P, ET], I32, ctx)
        prev_i = sb("prev_i", [P, ET], I32, ctx)
        spare = sb("spare", [P, ET], F32, ctx)
        isend = sb("isend", [P, ET], F32, ctx)
        tmp = sb("tmp", [P, ET], F32, ctx)
        with nc.Block() as block:
            @block.sync
            def _(sp):
                sp.dma_start(dst_t[:, :], a["dst_t"]).then_inc(loaded, 16)
                sp.dma_start(src_t[:, :], a["src_t"]).then_inc(loaded, 16)
                sp.dma_start(nxt_i[0:P - 1, :], a["dst_t"][1:P, :]).then_inc(loaded, 16)
                sp.dma_start(nxt_i[P - 1:P, 0:ET - 1], a["dst_t"][0:1, 1:ET]).then_inc(loaded, 16)
                sp.dma_start(nxt_i[P - 1:P, ET - 1:ET], a["dst_t"][P - 1:P, ET - 1:ET]).then_inc(loaded, 16)
                sp.dma_start(prev_i[:, 1:ET], a["dst_t"][P - 1:P, 0:ET - 1].broadcast_to([P, ET - 1])).then_inc(loaded, 16)

            @block.gpsimd
            def _(pool):
                pool.memset(ident[:, :], 0.0).then_inc(made, 1)
                pool.wait_ge(made, 1)
                pool.affine_select(out=ident[:, :], in_=ident[:, :], compare_op=ALU.not_equal, fill=1.0,
                                   base=0, pattern=[[-1, 128]], channel_multiplier=1).then_inc(made, 1)
                pool.iota(spare[:, :], pattern=[[0, ET // (2 * K)], [P, 2 * K]], base=N,
                          channel_multiplier=1, allow_small_or_imprecise_dtypes=True).then_inc(made, 1)

            @block.vector
            def _(dve):
                step = Steps(dve, step_s, 0)
                dve.wait_ge(loaded, 96)
                step(dve.tensor_copy(key_t[:, :], dst_t[:, :]))
                step(dve.tensor_copy(nxt[:, :], nxt_i[:, :]))
                dve.tensor_copy(prev_t[:, 1:ET], prev_i[:, 1:ET])
                step(dve.memset(prev_t[:, 0:1], -1.0))
                dve.wait_ge(made, 3)
                step(dve.tensor_scalar(tmp[:, :], prev_t[:, :], 1.0, ident[0:P, P - 1:P], ALU.add, ALU.mult))
                step(dve.tensor_scalar(prev_t[:, :], tmp[:, :], 1.0, None, ALU.subtract))
                step(dve.tensor_tensor(isend[:, :], key_t[:, :], nxt[:, :], ALU.not_equal))
                step(dve.tensor_tensor(isend[:, ET - 1:ET], isend[:, ET - 1:ET], ident[0:P, P - 1:P], ALU.max))
                step(dve.scalar_tensor_tensor(tmp[:, :], key_t[:, :], float(SKIP), isend[:, :], ALU.subtract, ALU.mult))
                step(dve.tensor_scalar(end_t[:, :], tmp[:, :], float(SKIP), None, ALU.add))
                step(dve.tensor_tensor(tmp[:, :], key_t[:, :], spare[:, :], ALU.subtract))
                step(dve.tensor_tensor(nxt[:, :], tmp[:, :], isend[:, :], ALU.mult))
                step(dve.tensor_tensor(add_t[:, :], nxt[:, :], spare[:, :], ALU.add))


def edge_rows(nc, a, sem, sb, bank, agg0, agg1, x3, h_dst, si, sj, src_p, dst_p, ew_t):
    with ExitStack() as ctx:
        t_ = lambda name, shape, dt=F32: sb("a_" + name, shape, dt, ctx)
        zeros = t_("zeros", [P, FILL * D])
        xg = [t_(f"xg{b}", [P, 2 * K, D]) for b in range(2)]
        hs = [t_(f"hs{b}", [P, K, D]) for b in range(2)]
        cur = [t_(f"cur{b}", [P, 2 * K], I32) for b in range(2)]
        ln = [Stats(t_, f"ln{b}", 2 * K) for b in range(2)]
        junk = t_("junk", [P, 2 * K, D])
        sc = [t_(f"sc{b}", [P, 2 * K]) for b in range(2)]
        ai = t_("ai", [P, D])
        aj = t_("aj", [P, D])
        w1 = t_("w1", [4, D])
        b1 = t_("b1", [D, 1])
        w2 = t_("w2", [D, 1])
        b2 = t_("b2", [P, 1])
        at = [t_(f"at{b}", [4, GC]) for b in range(2)]
        hid = [t_(f"hid{b}", [D, GC]) for b in range(2)]
        consts, zeroed, filled = sem("a_consts"), sem("a_zeroed"), sem("a_filled")
        gathered = [sem(f"a_gathered{b}") for b in range(2)]
        attr = [sem(f"a_attr{b}") for b in range(2)]
        staged, x_free, stats, relued, dots = (sem("a_" + s) for s in ("staged", "x_free", "stats", "relued", "dots"))
        step_s, hid_mm, hid_done, ew_mm = (sem("a_" + s) for s in ("step", "hid_mm", "hid_done", "ew_mm"))
        order = held = sem("passed")
        with nc.Block() as block:
            @block.sync
            def _(sp):
                sp.dma_start(src_p[:, :], a["src"].rearrange("(p t) -> p t", t=ET)).then_inc(consts, 16)
                sp.dma_start(dst_p[:, :], a["dst"].rearrange("(p t) -> p t", t=ET)).then_inc(consts, 16)
                sp.dma_start(ai[:, :], a["L0_gnn_a_i"].rearrange("(o d) -> o d", o=1).broadcast_to([P, D])).then_inc(consts, 16)
                sp.dma_start(aj[:, :], a["L0_gnn_a_j"].rearrange("(o d) -> o d", o=1).broadcast_to([P, D])).then_inc(consts, 16)
                sp.dma_start(w1[:, :], a["L1_gnn_edge_W1"]).then_inc(consts, 16)
                sp.dma_start(b1[:, :], a["L1_gnn_edge_b1"].rearrange("(d o) -> d o", o=1)).then_inc(consts, 16)
                sp.dma_start(w2[:, :], a["L1_gnn_edge_W2"]).then_inc(consts, 16)
                sp.dma_start(b2[:, :], a["L1_gnn_edge_b2"].rearrange("(o d) -> o d", o=1).broadcast_to([P, 1])).then_inc(consts, 16)
                for b in range(2):
                    sp.dma_start(at[b][:, :], a["attr"][:, b * GC:(b + 1) * GC]).then_inc(attr[b], 16)
                sp.wait_ge(zeroed, 1)
                rows = P * FILL
                with sp.Fori(0, N // rows) as i:
                    for agg in (agg0, agg1):
                        sp.dma_start(agg[ds(i * rows, rows), :].rearrange("(p r) d -> p (r d)", r=FILL), zeros[:, :]).then_inc(filled, 16)
                for agg in (agg0, x3):
                    sp.dma_start(agg[N:N + DUMP, :].rearrange("(p r) d -> p (r d)", r=DUMP // P), zeros[:, 0:DUMP // P * D]).then_inc(filled, 16)
                with sp.Fori(1, EG // 2) as i:
                    for b in range(2):
                        sp.wait_ge(hid_mm, 2 * i + b - 1)
                        sp.dma_start(at[b][:, :], a["attr"][:, ds((2 * i + b) * GC, GC)]).then_inc(attr[b], 16)
                sp.wait_ge(filled, (N // rows * 2 + 2) * 16)

            @block.gpsimd
            def _(pool):
                pool.memset(zeros[:, :], 0.0).then_inc(zeroed, 1)
                pool.wait_ge(consts, 128)
                with pool.Fori(0, EG // 2) as i:
                    for b in range(2):
                        j = 2 * i + b
                        pool.wait_ge(x_free, j + 1)
                        pool.sem_inc(order, 1)
                        pool.tensor_copy(cur[b][:, 0:K], dst_p[:, ds(j * K, K)]).then_inc(staged, 1)
                        pool.tensor_copy(cur[b][:, K:2 * K], src_p[:, ds(j * K, K)]).then_inc(staged, 1)
                        pool.wait_ge(staged, 2 * j + 2)
                        pool.sem_inc(order, 1)
                        for k in range(2 * K):
                            pool.indirect_dma_start(
                                out=xg[b][:, k, :], out_offset=None, in_=a["x"][:, :],
                                in_offset=bass.IndirectOffsetOnAxis(ap=cur[b][:, k:k + 1], axis=0)).then_inc(gathered[b], 16)

            @block.vector
            def _(dve):
                dve.sem_inc(dots, 2)
                dve.wait_ge(consts, 128)

                def scores(j, b):
                    step = Steps(dve, step_s, j * (STATS + 1), held)
                    dve.wait_ge(gathered[b], 16 * 2 * K * ((j - b) // 2 + 1) if isinstance(j, int) else 64 * (j - b + 2))
                    row_stats(dve, step, lambda k: xg[b][:, k, :], ln[b])
                    step(dve.scalar_tensor_tensor(ln[b].nmr[:, :], ln[b].mean, -1.0, ln[b].rstd[:, :], ALU.mult, ALU.mult))
                    dve.sem_inc(stats, 1)

                def dot(j, b):
                    dve.wait_ge(relued, 2 * K * (j + 1))
                    for k in range(K):
                        dve.scalar_tensor_tensor(junk[:, k, :], h_dst[:, ds((j * K + k) * D, D)], 1.0, ai[:, :],
                                                 ALU.mult, ALU.mult, accum_out=sc[b][:, k:k + 1])
                        last = dve.scalar_tensor_tensor(junk[:, K + k, :], hs[b][:, k, :], 1.0, aj[:, :],
                                                        ALU.mult, ALU.mult, accum_out=sc[b][:, K + k:K + k + 1])
                    last.then_inc(dots, 1)
                    dve.wait_ge(dots, j + 3)
                    dve.tensor_copy(si[:, ds(j * K, K)], sc[b][:, 0:K])
                    dve.tensor_copy(sj[:, ds(j * K, K)], sc[b][:, K:2 * K])

                scores(0, 0)
                with dve.Fori(0, EG // 2 - 1) as i:
                    scores(2 * i + 1, 1)
                    dot(2 * i, 0)
                    scores(2 * i + 2, 0)
                    dot(2 * i + 1, 1)
                scores(EG - 1, 1)
                dot(EG - 2, 0)
                dot(EG - 1, 1)

            @block.scalar
            def _(act):
                act.sem_inc(x_free, 2)
                act.wait_ge(consts, 128)
                with act.Fori(0, EG // 2) as i:
                    for b in range(2):
                        j = 2 * i + b
                        act.wait_ge(stats, j + 1)
                        act.wait_ge(dots, j + 1)
                        for k in range(2 * K):
                            o = h_dst[:, ds((j * K + k) * D, D)] if k < K else hs[b][:, k - K, :]
                            last = act.activation(o, xg[b][:, k, :], ACT.Relu, bias=ln[b].nmr[:, k:k + 1],
                                                  scale=ln[b].rstd[:, k:k + 1]).then_inc(relued, 1)
                        act.wait_ge(relued, 2 * K * (j + 1))
                        act.sem_inc(x_free, 1)
                        act.wait_ge(hid_mm, j + 1)
                        act.activation(hid[b][:, :], bank[b][:, 0:GC], ACT.Silu, bias=b1[:, 0:1]).then_inc(hid_done, 1)
                act.wait_ge(ew_mm, EG)
                act.activation(ew_t[:, :], bank[2][0:P, 0:ET], ACT.Sigmoid, bias=b2[:, 0:1])

            @block.tensor
            def _(pe):
                pe.wait_ge(consts, 128)

                def hidden(j, b):
                    pe.wait_ge(attr[b], 16 * ((j - b) // 2 + 1) if isinstance(j, int) else 8 * (j - b + 2))
                    pe.matmul(bank[b][:, 0:GC], w1[:, :], at[b][:, :], start=True, stop=True).then_inc(hid_mm, 1)

                def weigh(j, b):
                    pe.wait_ge(hid_done, j + 1)
                    for k in range(K):
                        last = pe.matmul(bank[2][0:P, ds(j * K + k, 1)], hid[b][:, k * P:(k + 1) * P], w2[:, :],
                                         start=True, stop=True)
                    last.then_inc(ew_mm, 1)

                hidden(0, 0)
                hidden(1, 1)
                with pe.Fori(0, EG // 2 - 1) as i:
                    for b in range(2):
                        weigh(2 * i + b, b)
                        hidden(2 * i + b + 2, b)
                weigh(EG - 2, 0)
                weigh(EG - 1, 1)


def softmax(nc, sem, sb, bank, ident, si, sj, dst_p, alpha):
    with ExitStack() as ctx:
        t_ = lambda name, shape: sb("s_" + name, shape, F32, ctx)
        key, e, same, gate, f, f2, bk, w = (t_(n, [P, ET]) for n in ("key", "e", "same", "gate", "f", "f2", "bk", "w"))
        gate_b = t_("gate_b", [P, ET])
        cols = t_("cols", [P, 1])
        row = {n: t_("row_" + n, [1, 128]) for n in
               ("k0", "kl", "cont", "on", "g_on", "g_cont", "onb", "g_onb", "g_contb", "edge", "run", "enter", "rev")}
        step_s, rows_s, cols_s, e1, e2 = (sem("s_" + n) for n in ("step", "rows", "cols", "e1", "e2"))
        counts = {"step": 0, "t": 0}
        jobs = []

        with nc.Block() as block:
            @block.vector
            def _(dve):
                step = Steps(dve, step_s, 0)

                def to_row(dst_row, col):
                    step(dve.tensor_copy(cols[:, :], col))
                    dve.sem_inc(rows_s, 1)
                    jobs.append("row")
                    dve.wait_ge(cols_s, len(jobs))
                    step(dve.tensor_copy(dst_row[0:1, 0:P], bank[0][0:1, 0:P]))

                def to_col(src_row):
                    dve.sem_inc(rows_s, 1)
                    jobs.append("col")
                    dve.wait_ge(cols_s, len(jobs))
                    step(dve.tensor_copy(cols[:, :], bank[1][0:P, 0:1]))

                r = {n: x[0:1, 0:P] for n, x in row.items()}
                step(dve.tensor_copy(key[:, :], dst_p[:, :]))
                step(dve.tensor_tensor(f[:, :], si[:, :], sj[:, :], ALU.add))
                step(dve.scalar_tensor_tensor(e[:, :], f[:, :], 0.01, f[:, :], ALU.mult, ALU.max))
                dve.memset(same[:, :], 1.0)
                step(dve.tensor_tensor(gate_b[:, 1:ET], key[:, 1:ET], key[:, 0:ET - 1], ALU.is_equal))
                step(dve.tensor_copy(same[:, 1:ET], gate_b[:, 1:ET]))
                step(dve.tensor_scalar(gate[:, :], same[:, :], 1.0, BIG, ALU.subtract, ALU.mult))
                step(dve.memset(gate_b[:, :], 0.0))
                step(dve.tensor_copy(gate_b[:, 0:ET - 1], gate[:, 1:ET]))
                to_row(row["k0"], key[:, 0:1])
                to_row(row["kl"], key[:, ET - 1:ET])
                step(dve.memset(r["cont"], 0.0))
                step(dve.tensor_tensor(row["cont"][0:1, 1:P], row["k0"][0:1, 1:P], row["kl"][0:1, 0:P - 1], ALU.is_equal))
                step(dve.tensor_tensor(r["edge"], r["k0"], r["kl"], ALU.is_equal))
                step(dve.tensor_tensor(r["on"], r["edge"], r["cont"], ALU.mult))
                step(dve.tensor_scalar(r["g_on"], r["on"], 1.0, BIG, ALU.subtract, ALU.mult))
                step(dve.tensor_scalar(r["g_cont"], r["cont"], 1.0, BIG, ALU.subtract, ALU.mult))
                step(dve.memset(r["g_contb"], -BIG))
                step(dve.tensor_copy(row["g_contb"][0:1, 0:P - 1], row["g_cont"][0:1, 1:P]))
                step(dve.tensor_scalar(r["onb"], r["edge"], 1.0, BIG, ALU.subtract, ALU.mult))
                step(dve.tensor_tensor(r["g_onb"], r["g_contb"], r["onb"], ALU.min))

                def back_max(x, res):
                    step(dve.tensor_tensor_scan(f2[:, ::-1], gate_b[:, ::-1], x[:, ::-1], -BIG, ALU.add, ALU.max))
                    to_row(row["edge"], f2[:, 0:1])
                    step(dve.tensor_tensor_scan(row["run"][0:1, P - 1::-1], row["g_onb"][0:1, P - 1::-1],
                                                row["edge"][0:1, P - 1::-1], -BIG, ALU.add, ALU.max))
                    step(dve.memset(r["enter"], -BIG))
                    step(dve.tensor_tensor(row["enter"][0:1, 0:P - 1], row["run"][0:1, 1:P], row["g_contb"][0:1, 0:P - 1], ALU.add))
                    to_col(row["enter"])
                    step(dve.tensor_tensor_scan(res[:, ::-1], gate_b[:, ::-1], x[:, ::-1], cols[:, 0:1], ALU.add, ALU.max))

                step(dve.tensor_tensor_scan(f[:, :], gate[:, :], e[:, :], -BIG, ALU.add, ALU.max))
                to_row(row["edge"], f[:, ET - 1:ET])
                step(dve.tensor_tensor_scan(r["run"], r["g_on"], r["edge"], -BIG, ALU.add, ALU.max))
                step(dve.memset(r["enter"], -BIG))
                step(dve.tensor_tensor(row["enter"][0:1, 1:P], row["run"][0:1, 0:P - 1], row["g_cont"][0:1, 1:P], ALU.add))
                to_col(row["enter"])
                step(dve.tensor_tensor_scan(f[:, :], gate[:, :], e[:, :], cols[:, 0:1], ALU.add, ALU.max))
                back_max(f, bk)
                dve.tensor_tensor(f[:, :], e[:, :], bk[:, :], ALU.subtract).then_inc(e1, 1)
                dve.wait_ge(e2, 1)
                step(dve.tensor_tensor_scan(f[:, :], same[:, :], w[:, :], 0.0, ALU.mult, ALU.add))
                to_row(row["edge"], f[:, ET - 1:ET])
                step(dve.tensor_tensor_scan(r["run"], r["on"], r["edge"], 0.0, ALU.mult, ALU.add))
                step(dve.memset(r["enter"], 0.0))
                step(dve.tensor_tensor(row["enter"][0:1, 1:P], row["run"][0:1, 0:P - 1], row["cont"][0:1, 1:P], ALU.mult))
                to_col(row["enter"])
                step(dve.tensor_tensor_scan(f[:, :], same[:, :], w[:, :], cols[:, 0:1], ALU.mult, ALU.add))
                back_max(f, bk)
                step(dve.reciprocal(f[:, :], bk[:, :]))
                step(dve.tensor_tensor(alpha[:, :], w[:, :], f[:, :], ALU.mult))

            @block.scalar
            def _(act):
                act.wait_ge(e1, 1)
                act.activation(w[:, :], f[:, :], ACT.Exp).then_inc(e2, 1)

            @block.tensor
            def _(pe):
                for n, kind in enumerate(jobs):
                    pe.wait_ge(rows_s, n + 1)
                    if kind == "row":
                        pe.transpose(bank[0][0:1, 0:P], cols[:, 0:1], ident[0:P, 0:P]).then_inc(cols_s, 1)
                    else:
                        pe.transpose(bank[1][0:P, 0:1], row["enter"][0:1, 0:P], ident[0:1, 0:1]).then_inc(cols_s, 1)


def scatter_by_source(nc, a, sem, sb, bank, agg0, h_dst, alpha, src_p):
    with ExitStack() as ctx:
        t_ = lambda name, shape, dt=F32: sb("b_" + name, shape, dt, ctx)
        key = t_("key", [P, ET])
        earlier = t_("earlier", [P, K, K, P])
        keyrow = [t_(f"keyrow{b}", [P, GC], I32) for b in range(2)]
        same = [t_(f"same{b}", [P, K, GC]) for b in range(2)]
        junk = t_("junk", [P, K, GC])
        cnt = t_("cnt", [P, K])
        pick = t_("pick", [P, K])
        diff = t_("diff", [P, K])
        spare = t_("spare", [P, K])
        idx = [t_(f"idx{b}", [P, K], I32) for b in range(2)]
        msg = [t_(f"msg{b}", [P, K, D]) for b in range(2)]
        tot = [t_(f"tot{b}", [P, K, D]) for b in range(2)]
        keys_in = [sem(f"b_keys_in{b}") for b in range(2)]
        made, step_s, msgs, summed, totals, added, first = (
            sem("b_" + s) for s in ("made", "step", "msgs", "summed", "totals", "added", "first"))
        order = sem("passed")
        with nc.Block() as block:
            @block.sync
            def _(sp):
                load = lambda j, b: sp.dma_start(
                    keyrow[b][:, :], a["src_p"][ds(j * K, K), :].rearrange("(o k) p -> o (k p)", o=1).broadcast_to([P, GC])).then_inc(keys_in[b], 16)
                load(0, 0)
                load(1, 1)
                with sp.Fori(1, EG // 2) as i:
                    for b in range(2):
                        sp.wait_ge(msgs, 2 * i + b - 1)
                        load(2 * i + b, b)

            @block.gpsimd
            def _(pool):
                pool.memset(earlier[:, :, :, :], 1.0).then_inc(made, 1)
                pool.wait_ge(made, 1)
                for k in range(K):
                    last = pool.affine_select(out=earlier[:, k, :, :], in_=earlier[:, k, :, :], compare_op=ALU.is_gt, fill=0.0,
                                              base=k * P, pattern=[[-P, K], [-1, P]], channel_multiplier=1)
                last.then_inc(made, 1)
                pool.iota(spare[:, :], pattern=[[P, K]], base=N, channel_multiplier=1,
                          allow_small_or_imprecise_dtypes=True).then_inc(made, 1)

                def scatter(j, b, first=False):
                    pool.wait_ge(totals, j + 1)
                    pool.sem_inc(order, 1)
                    if not first:
                        pool.wait_ge(added, 64 * j)
                        pool.sem_inc(order, 1)
                    for k in range(K):
                        pool.indirect_dma_start(
                            out=agg0[:, :], out_offset=bass.IndirectOffsetOnAxis(ap=idx[b][:, k:k + 1], axis=0),
                            in_=tot[b][:, k, :], in_offset=None, compute_op=ALU.add).then_inc(added, 16)

                scatter(0, 0, True)
                scatter(1, 1)
                with pool.Fori(1, EG // 2) as i:
                    for b in range(2):
                        scatter(2 * i + b, b)
                pool.wait_ge(added, 64 * EG)

            @block.vector
            def _(dve):
                dve.tensor_copy(key[:, :], src_p[:, :]).then_inc(first, 1)
                dve.wait_ge(first, 1)
                dve.wait_ge(made, 3)

                def prepare_group(j, b):
                    step = Steps(dve, step_s, j * 4)
                    dve.wait_ge(keys_in[b], 16 * ((j - b) // 2 + 1) if isinstance(j, int) else 8 * (j - b + 2))
                    for k in range(K):
                        t = j * K + k
                        dve.tensor_scalar(msg[b][:, k, :], h_dst[:, ds(t * D, D)], alpha[:, ds(t, 1)], None, ALU.mult)
                        last = dve.tensor_scalar(same[b][:, k, :], keyrow[b][:, :], key[:, ds(t, 1)], None, ALU.is_equal)
                    step(last)
                    dve.sem_inc(msgs, 1)
                    for k in range(K):
                        last = dve.scalar_tensor_tensor(junk[:, k, :], same[b][:, k, :], 1.0,
                                                        earlier[:, k, :, :].rearrange("p j q -> p (j q)"),
                                                        ALU.mult, ALU.mult, accum_out=cnt[:, k:k + 1])
                    step(last)
                    dve.tensor_scalar(pick[:, :], cnt[:, :], 0.5, None, ALU.is_lt)
                    step(dve.tensor_tensor(diff[:, :], key[:, ds(j * K, K)], spare[:, :], ALU.subtract))
                    step(dve.tensor_tensor(cnt[:, :], diff[:, :], pick[:, :], ALU.mult))

                def finish_group(j, b, first=False):
                    dve.wait_ge(summed, j + 1)
                    if not first:
                        dve.wait_ge(added, 64 * (j - 1))
                    dve.tensor_copy(tot[b][:, :, :].rearrange("p k d -> p (k d)"), bank[b][0:P, 0:K * D])
                    dve.tensor_tensor(idx[b][:, :], cnt[:, :], spare[:, :], ALU.add).then_inc(totals, 1)

                for b in range(2):
                    prepare_group(b, b)
                    finish_group(b, b, True)
                with dve.Fori(1, EG // 2) as i:
                    for b in range(2):
                        prepare_group(2 * i + b, b)
                        finish_group(2 * i + b, b)

            @block.tensor
            def _(pe):
                with pe.Fori(0, EG // 2) as i:
                    for b in range(2):
                        j = 2 * i + b
                        pe.wait_ge(msgs, j + 1)
                        for o in range(K):
                            for k in range(K):
                                last = pe.matmul(bank[b][0:P, o * D:(o + 1) * D], same[b][:, k, o * P:(o + 1) * P],
                                                 msg[b][:, k, :], start=(k == 0), stop=(k == K - 1))
                        last.then_inc(summed, 1)


def layer0_nodes(nc, a, sem, sb, bank, ident, agg0, x1, node_rows):
    with ExitStack() as ctx:
        t_ = lambda name, shape, dt=F32: sb("c_" + name, shape, dt, ctx)
        R = 4
        w = t_("w", [D, D])
        wi = t_("wi", [D, D])
        ag = [t_(f"ag{b}", [P, K, D]) for b in range(R)]
        x = [t_(f"x{b}", [P, K, D]) for b in range(R)]
        at = [t_(f"at{b}", [D, GC]) for b in range(2)]
        y = [t_(f"y{b}", [P, K, D]) for b in range(2)]
        z = [t_(f"z{b}", [P, K, D]) for b in range(R)]
        loaded = [sem(f"c_loaded{b}") for b in range(R)]
        stored = [sem(f"c_stored{b}") for b in range(R)]
        w_in, w_made, turned, turned_out, mm, act_done, sums = (
            sem("c_" + s) for s in ("w_in", "w_made", "turned", "turned_out", "mm", "act_done", "sums"))
        with nc.Block() as block:
            @block.sync
            def _(sp):
                sp.dma_start(w[:, :], a["L0_gnn_W"]).then_inc(w_in, 16)
                for b in range(R):
                    sp.dma_start(ag[b][:, :, :], node_rows(agg0, b)).then_inc(loaded[b], 16)
                    sp.dma_start(x[b][:, :, :], node_rows(a["x"], b)).then_inc(loaded[b], 16)
                with sp.Fori(0, NG // R - 1) as i:
                    for b in range(R):
                        g = R * i + b
                        sp.wait_ge(sums, g + 3)
                        sp.dma_start(node_rows(x1, g), z[b][:, :, :]).then_inc(stored[b], 16)
                        sp.dma_start(ag[b][:, :, :], node_rows(agg0, g + R)).then_inc(loaded[b], 16)
                        sp.dma_start(x[b][:, :, :], node_rows(a["x"], g + R)).then_inc(loaded[b], 16)
                for b in range(R):
                    sp.wait_ge(sums, NG - R + b + 3)
                    sp.dma_start(node_rows(x1, NG - R + b), z[b][:, :, :]).then_inc(stored[b], 16)
                for b in range(R):
                    sp.wait_ge(stored[b], 16 * (NG // R))

            @block.tensor
            def _(pe):
                def turn(g, b):
                    pe.wait_ge(loaded[b], 32 * ((g - b) // R + 1) if isinstance(g, int) else 8 * (g - b + R))
                    for k in range(K):
                        last = pe.transpose(bank[b % 2][:, k * P:(k + 1) * P], ag[b][:, k, :], ident[0:P, 0:P])
                    last.then_inc(turned, 1)

                def product(g, b):
                    pe.wait_ge(turned_out, g + 1)
                    pe.wait_ge(act_done, g + 1)
                    for k in range(K):
                        last = pe.matmul(bank[2 + b % 2][0:P, k * D:(k + 1) * D], at[b % 2][:, k * P:(k + 1) * P], wi[:, :],
                                         start=True, stop=True)
                    last.then_inc(mm, 1)

                pe.wait_ge(w_made, 1)
                turn(0, 0)
                with pe.Fori(0, NG // R - 1) as i:
                    for b in range(R):
                        turn(R * i + b + 1, (b + 1) % R)
                        product(R * i + b, b)
                for b in range(R):
                    if b < R - 1:
                        turn(NG - R + b + 1, b + 1)
                    product(NG - R + b, b)

            @block.vector
            def _(dve):
                dve.wait_ge(w_in, 16)
                dve.tensor_tensor(wi[:, :], w[:, :], ident[:, :], ALU.add).then_inc(w_made, 1)
                with dve.Fori(0, NG // R) as i:
                    for b in range(R):
                        g = R * i + b
                        dve.wait_ge(turned, g + 1)
                        dve.wait_ge(act_done, g + 1)
                        dve.tensor_copy(at[b % 2][:, :], bank[b % 2][:, 0:GC]).then_inc(turned_out, 1)

            @block.scalar
            def _(act):
                act.sem_inc(act_done, 2)
                with act.Fori(0, NG // R) as i:
                    for b in range(R):
                        g = R * i + b
                        act.wait_ge(mm, g + 1)
                        act.wait_ge(sums, g + 1)
                        act.activation(y[b % 2][:, :, :].rearrange("p k d -> p (k d)"), bank[2 + b % 2][0:P, 0:K * D],
                                       ACT.Gelu).then_inc(act_done, 1)

            @block.gpsimd
            def _(pool):
                pool.sem_inc(sums, 2)

                def add_rows(g, b, first=False):
                    pool.wait_ge(act_done, g + 3)
                    if not first:
                        pool.wait_ge(stored[b], 4 * (g - b))
                    pool.tensor_tensor(z[b][:, :, :], y[b % 2][:, :, :], x[b][:, :, :], ALU.add).then_inc(sums, 1)

                for b in range(R):
                    add_rows(b, b, True)
                with pool.Fori(1, NG // R) as i:
                    for b in range(R):
                        add_rows(R * i + b, b)


def over(eng, n, unroll, body):
    for b in range(unroll):
        body(b, b)
    with eng.Fori(1, n // unroll - 1) as i:
        for b in range(unroll):
            body(unroll * i + b, b)
    for b in range(unroll):
        body(n - unroll + b, b)


def wait(eng, s, value):
    if not isinstance(value, int) or value > 0:
        eng.wait_ge(s, value)


def there(g, n):
    return not isinstance(g, int) or 0 <= g < n


def edges(nc, a, sem, sb, bank, layer, ident, x, agg, src_t, key_t, prev_t, to_t, ew_t):
    with ExitStack() as ctx:
        nm = f"e{layer}_"
        t_ = lambda name, shape, dt=F32: sb(nm + name, shape, dt, ctx)
        two = range(2)
        xg = [t_(f"xg{b}", [P, K, D]) for b in two]
        from_i = [t_(f"from_i{b}", [P, K], I32) for b in two]
        to_i = [t_(f"to_i{b}", [P, K], I32) for b in two]
        keyrow = [t_(f"keyrow{b}", [P, GC], I32) for b in two]
        same = [t_(f"same{b}", [P, K, P]) for b in two]
        carry = [t_(f"carry{b}", [P, K, P]) for b in two]
        ln = [Stats(t_, f"ln{b}", K) for b in two]
        msg = [t_(f"msg{b}", [P, K, D + 1]) for b in two]
        run = [t_(f"run{b}", [P, K, D + 1]) for b in two]
        cnt = [t_(f"cnt{b}", [P, K]) for b in two]
        res = [t_(f"res{b}", [P, K, D]) for b in two]
        if layer == 1:
            h = [t_(f"h{b}", [P, K, D]) for b in two]
            ht = [t_(f"ht{b}", [D, GC]) for b in two]
            m = [t_(f"m{b}", [P, K, D]) for b in two]
            bias = t_("bias", [1, K * D])
            ones = t_("ones", [1, P])
        if layer != 3:
            w = t_("w", [D, D])
        if layer == 2:
            rt = [t_(f"rt{b}", [D, GC]) for b in two]
        gathered, keys_in, written = ([sem(f"{nm}{s}{b}") for b in two] for s in ("gathered", "keys_in", "written"))
        order = held = sem("passed")
        ready, staged, step_s, stats, relued, matrices, run_mm, run_out, results = (
            sem(nm + s) for s in ("ready", "staged", "step", "stats", "relued", "matrices", "run_mm", "run_out", "results"))
        if layer != 3:
            consts, turned, turned_out, mm = (sem(nm + s) for s in ("consts", "turned", "turned_out", "mm"))
        if layer != 2:
            out_s = sem(nm + "out")
        if layer == 1:
            silued, msgs = sem(nm + "silued"), sem(nm + "msgs")
        run_at = lambda k: bank[4 + k % 2][0:P, 0:D + 1]
        with nc.Block() as block:
            @block.sync
            def _(sp):
                if layer == 1:
                    sp.dma_start(w[:, :], a["L1_gnn_agg_W"]).then_inc(consts, 16)
                    for k in range(K):
                        sp.dma_start(bias[:, k * D:(k + 1) * D], a["L1_gnn_agg_b"].rearrange("(o d) -> o d", o=1)).then_inc(consts, 16)
                if layer == 2:
                    sp.dma_start(w[:, :], a["w2t"]).then_inc(consts, 16)

                def load_keys(j, b):
                    wait(sp, matrices, j - 1)
                    sp.dma_start(keyrow[b][:, :], a["dst_rows"][ds(j * K, K), :].rearrange("(o k) p -> o (k p)", o=1)
                                 .broadcast_to([P, GC])).then_inc(keys_in[b], 16)
                over(sp, EG, 2, load_keys)

            @block.gpsimd
            def _(pool):
                def write(j, b):
                    pool.wait_ge(results, j + 1)
                    pool.sem_inc(order, 1)
                    pool.tensor_copy(to_i[b][:, :], to_t[:, ds(j * K, K)]).then_inc(staged, 1)
                    pool.wait_ge(staged, staged_before(j) + 1)
                    pool.sem_inc(order, 1)
                    for k in range(K):
                        if layer == 2:
                            pool.indirect_dma_start(
                                out=agg[:, :], out_offset=bass.IndirectOffsetOnAxis(ap=to_i[b][:, k:k + 1], axis=0),
                                in_=res[b][:, k, :], in_offset=None, compute_op=ALU.add).then_inc(written[b], 16)
                        else:
                            pool.indirect_dma_start(
                                out=agg[:, :], out_offset=bass.IndirectOffsetOnAxis(ap=to_i[b][:, k:k + 1], axis=0),
                                in_=res[b][:, k, :], in_offset=None, bounds_check=N - 1, oob_is_err=False).then_inc(written[b], 16)

                def staged_before(j):
                    return min(j + 3, EG) + j if isinstance(j, int) else 2 * j + 3

                def both(j, b):
                    if there(j + 2, EG):
                        gather_at(j + 2, b)
                    write(j, b)

                def gather_at(j, b):
                    wait(pool, relued, 4 * (j - 1))
                    pool.sem_inc(order, 1)
                    pool.tensor_copy(from_i[b][:, :], src_t[:, ds(j * K, K)]).then_inc(staged, 1)
                    pool.wait_ge(staged, j + 1 + max(j - 2, 0) if isinstance(j, int) else 2 * j - 1)
                    pool.sem_inc(order, 1)
                    for k in range(K):
                        pool.indirect_dma_start(
                            out=xg[b][:, k, :], out_offset=None, in_=x[0:N, :],
                            in_offset=bass.IndirectOffsetOnAxis(ap=from_i[b][:, k:k + 1], axis=0)).then_inc(gathered[b], 16)

                gather_at(0, 0)
                gather_at(1, 1)
                over(pool, EG, 2, both)
                for b in two:
                    pool.wait_ge(written[b], 32 * EG)

            @block.vector
            def _(dve):
                for b in two:
                    dve.memset(msg[b][:, :, D:D + 1], 1.0)
                    dve.memset(run[b][:, :, :], 0.0)
                if layer == 1:
                    dve.memset(ones[:, :], 1.0)
                dve.memset(cnt[0][:, :], 0.0).then_inc(ready, 1)

                def normalize(j, b):
                    step = Steps(dve, step_s, j * (STATS + 1), held)
                    dve.wait_ge(gathered[b], 32 * (j - b + 2))
                    row_stats(dve, step, lambda k: xg[b][:, k, :], ln[b])
                    dve.scalar_tensor_tensor(ln[b].nmr[:, :], ln[b].mean, -1.0, ln[b].rstd[:, :], ALU.mult, ALU.mult).then_inc(step_s, 1)
                    step.n += 1
                    dve.wait_ge(step_s, step.base + step.n)
                    dve.sem_inc(stats, 1)
                    dve.wait_ge(keys_in[b], 8 * (j - b + 2))
                    for k in range(K):
                        t = j * K + k
                        dve.tensor_scalar(same[b][:, k, :], keyrow[b][:, k * P:(k + 1) * P], key_t[:, ds(t, 1)], None, ALU.is_equal)
                        last = dve.tensor_scalar(carry[b][:, k, :], keyrow[b][:, k * P:(k + 1) * P], prev_t[:, ds(t, 1)], None, ALU.is_equal)
                    last.then_inc(matrices, 1)

                def weigh(j, b):
                    dve.wait_ge(silued, j + 1)
                    for k in range(K):
                        last = dve.tensor_scalar(msg[b][:, k, 0:D], m[b][:, k, :], ew_t[:, ds(j * K + k, 1)], None, ALU.mult)
                    last.then_inc(msgs, 1)

                def evacuate(j, b):
                    dve.wait_ge(turned, j + 1)
                    dve.tensor_copy(ht[b][:, :], bank[b][:, 0:GC]).then_inc(turned_out, 1)

                def means(j, b):
                    dve.wait_ge(run_out, K * (j + 1))
                    dve.tensor_scalar(cnt[b][:, :], run[b][:, :, D], 1.0, None, ALU.max).then_inc(out_s, 1)
                    dve.wait_ge(out_s, 2 * j + 1)
                    dve.reciprocal(cnt[b][:, :], cnt[b][:, :]).then_inc(out_s, 1)
                    dve.wait_ge(out_s, 2 * j + 2)
                    wait(dve, written[b], 32 * (j - b))
                    for k in range(K):
                        last = dve.tensor_scalar(res[b][:, k, :], run[b][:, k, 0:D], cnt[b][:, k:k + 1], None, ALU.mult)
                    last.then_inc(results, 1)

                def products(j, b):
                    dve.wait_ge(turned, j + 1)
                    dve.tensor_copy(rt[b][:, :], bank[6][:, 0:GC]).then_inc(turned_out, 1)
                    wait(dve, written[b], 32 * (j - b))
                    dve.wait_ge(mm, j + 1)
                    dve.tensor_copy(res[b][:, :, :].rearrange("p k d -> p (k d)"), bank[7][0:P, 0:K * D]).then_inc(results, 1)

                def group(j, b):
                    if layer == 1:
                        weigh(j, b)
                    if there(j + 1, EG):
                        normalize(j + 1, 1 - b)
                    if layer == 2:
                        products(j, b)
                    else:
                        means(j, b)
                    if layer == 1 and there(j + 1, EG):
                        evacuate(j + 1, 1 - b)

                normalize(0, 0)
                if layer == 1:
                    evacuate(0, 0)
                over(dve, EG, 2, group)

            @block.scalar
            def _(act):
                act.wait_ge(ready, 1)

                def relu(j, b):
                    act.wait_ge(stats, j + 1)
                    for k in range(K):
                        act.activation(h[b][:, k, :] if layer == 1 else msg[b][:, k, 0:D], xg[b][:, k, :], ACT.Relu,
                                       bias=ln[b].nmr[:, k:k + 1], scale=ln[b].rstd[:, k:k + 1]).then_inc(relued, 1)

                def silu(j, b):
                    act.wait_ge(mm, j + 1)
                    act.activation(m[b][:, :, :].rearrange("p k d -> p (k d)"), bank[2 + b][0:P, 0:K * D], ACT.Silu).then_inc(silued, 1)

                def runs_out(j, b):
                    for k in range(K):
                        act.wait_ge(run_mm, K * j + k + 1)
                        act.activation(run[b][:, k, :], run_at(k), ACT.Copy).then_inc(run_out, 1)

                def group(j, b):
                    runs_out(j, b)
                    if there(j + 1, EG):
                        relu(j + 1, 1 - b)
                        if layer == 1:
                            silu(j + 1, 1 - b)

                relu(0, 0)
                if layer == 1:
                    silu(0, 0)
                over(act, EG, 2, group)

            @block.tensor
            def _(pe):
                pe.wait_ge(ready, 1)
                if layer != 3:
                    pe.wait_ge(consts, 16 * (1 + K) if layer == 1 else 16)

                def turn(j, b):
                    pe.wait_ge(relued, K * (j + 1))
                    for k in range(K):
                        last = pe.transpose(bank[b][:, k * P:(k + 1) * P], h[b][:, k, :], ident[0:P, 0:P])
                    last.then_inc(turned, 1)

                def linear(j, b):
                    pe.matmul(bank[2 + b][0:P, 0:K * D], ones[:, :], bias[:, :], start=True, stop=False)
                    pe.wait_ge(turned_out, j + 1)
                    for k in range(K):
                        last = pe.matmul(bank[2 + b][0:P, k * D:(k + 1) * D], ht[b][:, k * P:(k + 1) * P], w[:, :],
                                         start=False, stop=(k == K - 1))
                    last.then_inc(mm, 1)

                def sum_runs(j, b):
                    pe.wait_ge(matrices, j + 1)
                    if layer == 1:
                        pe.wait_ge(msgs, j + 1)
                    else:
                        pe.wait_ge(relued, K * (j + 1))
                    for k in range(K):
                        pe.matmul(run_at(k), same[b][:, k, :], msg[b][:, k, :], start=True, stop=False)
                        before = run[b][:, k - 1, :] if k else run[1 - b][:, K - 1, :]
                        wait(pe, run_out, K * j + k)
                        pe.matmul(run_at(k), carry[b][:, k, :], before, start=False, stop=True).then_inc(run_mm, 1)

                def times_w(j, b):
                    pe.wait_ge(run_out, K * (j + 1))
                    wait(pe, results, j)
                    for k in range(K):
                        last = pe.transpose(bank[6][:, k * P:(k + 1) * P], run[b][:, k, 0:D], ident[0:P, 0:P])
                    last.then_inc(turned, 1)
                    pe.wait_ge(turned_out, j + 1)
                    for k in range(K):
                        last = pe.matmul(bank[7][0:P, k * D:(k + 1) * D], rt[b][:, k * P:(k + 1) * P], w[:, :],
                                         start=True, stop=True)
                    last.then_inc(mm, 1)

                def group(j, b):
                    sum_runs(j, b)
                    if layer == 2:
                        times_w(j, b)
                    if layer == 1 and there(j + 1, EG):
                        turn(j + 1, 1 - b)
                        linear(j + 1, 1 - b)

                if layer == 1:
                    turn(0, 0)
                    linear(0, 0)
                over(pe, EG, 2, group)


def layer1_nodes(nc, a, sem, sb, bank, ident, x1, agg1, x2, x3, node_rows):
    with ExitStack() as ctx:
        t_ = lambda name, shape, dt=F32: sb("d_" + name, shape, dt, ctx)
        R = 4
        four, two = range(R), range(2)
        wh, wa, w2, wr = (t_(n, [D, D]) for n in ("wh", "wa", "w2", "wr"))
        b1 = t_("b1", [D, 1])
        gain, shift = t_("gain", [P, K, D]), t_("shift", [P, K, D])
        b2 = t_("b2", [65, K * D])
        part = t_("part", [65, K * D])
        b2s = t_("b2s", [65, K * D], BF16)
        ones = t_("ones", [65, P], BF16)
        x = [t_(f"x{b}", [P, K, D]) for b in four]
        ag = [t_(f"ag{b}", [P, K, D]) for b in four]
        z = [t_(f"z{b}", [P, K, D]) for b in four]
        xn, yn = ([t_(f"{n}{b}", [P, K, D]) for b in two] for n in ("xn", "yn"))
        ht, at, ut = ([t_(f"{n}{b}", [D, GC]) for b in two] for n in ("ht", "at", "ut"))
        ln, lo = ([Stats(t_, f"{n}{b}", K) for b in two] for n in ("ln", "lo"))
        loaded, stored = ([sem(f"d_{s}{b}") for b in four] for s in ("loaded", "stored"))
        consts, made, made_s, in_s, out_s, normed, turned, evac, mm, silued, mo, ostats, onormed, sums = (
            sem("d_" + s) for s in ("consts", "made", "made_s", "in_s", "out_s", "normed", "turned", "evac",
                                    "mm", "silued", "mo", "ostats", "onormed", "sums"))
        held = sem("passed")
        flat = lambda ap: ap.rearrange("p k d -> p (k d)")
        with nc.Block() as block:
            @block.sync
            def _(sp):
                row = lambda n: a[n].rearrange("(o d) -> o d", o=1)
                sp.dma_start(wh[:, :], a["L1_gnn_upd_W1"][0:D, :]).then_inc(consts, 16)
                sp.dma_start(wa[:, :], a["L1_gnn_upd_W1"][D:2 * D, :]).then_inc(consts, 16)
                sp.dma_start(w2[:, :], a["L1_gnn_upd_W2"]).then_inc(consts, 16)
                sp.dma_start(wr[:, :], a["L1_gnn_res_W"]).then_inc(consts, 16)
                sp.dma_start(b1[:, :], a["L1_gnn_upd_b1"].rearrange("(d o) -> d o", o=1)).then_inc(consts, 16)
                for k in range(K):
                    sp.dma_start(gain[:, k, :], row("L1_gnn_ln_g").broadcast_to([P, D])).then_inc(consts, 16)
                    sp.dma_start(shift[:, k, :], row("L1_gnn_ln_b").broadcast_to([P, D])).then_inc(consts, 16)
                    sp.dma_start(b2[:, k * D:(k + 1) * D], row("L1_gnn_upd_b2").broadcast_to([65, D])).then_inc(consts, 16)

                def load(g, b):
                    sp.dma_start(x[b][:, :, :], node_rows(x1, g)).then_inc(loaded[b], 16)
                    sp.dma_start(ag[b][:, :, :], node_rows(agg1, g)).then_inc(loaded[b], 16)

                def move(g, b):
                    sp.wait_ge(sums, 3 * (g + 1))
                    sp.dma_start(node_rows(x2, g), z[b][:, :, :]).then_inc(stored[b], 16)
                    sp.dma_start(node_rows(x3, g), z[b][:, :, :]).then_inc(stored[b], 16)
                    if there(g + R, NG):
                        load(g + R, b)

                for b in four:
                    load(b, b)
                over(sp, NG, R, move)
                for b in four:
                    sp.wait_ge(stored[b], 32 * (NG // R))

            @block.vector
            def _(dve):
                step = Steps(dve, made_s, 0)
                dve.wait_ge(consts, 16 * (5 + 3 * K))
                dve.memset(ones[:, :], 0.0)
                step(dve.memset(b2s[:, :], 0.0))
                for p in (0, 32, 64):
                    dve.memset(ones[p:p + 1, :], 1.0)
                step(dve.tensor_copy(b2s[0:1, :], b2[0:1, :]))
                step(dve.tensor_copy(b2s[32:33, :], b2[32:33, :]))
                step(dve.tensor_tensor(part[32:33, :], b2[32:33, :], b2s[32:33, :], ALU.subtract))
                step(dve.tensor_copy(b2s[32:33, :], part[32:33, :]))
                step(dve.tensor_copy(b2s[64:65, :], b2[64:65, :]))
                step(dve.tensor_tensor(part[64:65, :], b2[64:65, :], b2s[64:65, :], ALU.subtract))
                step(dve.tensor_copy(b2s[64:65, :], part[64:65, :]))
                step(dve.tensor_tensor(part[64:65, :], part[64:65, :], b2s[64:65, :], ALU.subtract))
                dve.tensor_copy(b2s[64:65, :], part[64:65, :]).then_inc(made, 1)

                def normalize(g, b):
                    c = b % 2
                    step = Steps(dve, in_s, g * STATS, held)
                    dve.wait_ge(loaded[b], 8 * (g - b + R))
                    row_stats(dve, step, lambda k: x[b][:, k, :], ln[c])
                    wait(dve, turned, g - 1)
                    for k in range(K):
                        last = dve.tensor_scalar(xn[c][:, k, :], x[b][:, k, :], ln[c].mv[:, k, 0:1], ln[c].rstd[:, k:k + 1],
                                                 ALU.subtract, ALU.mult)
                    last.then_inc(normed, 1)

                def out_stats(g, b):
                    c = b % 2
                    step = Steps(dve, out_s, g * (STATS + 1), held)
                    dve.wait_ge(mo, g + 1)
                    row_stats(dve, step, lambda k: bank[6 + c][0:P, k * D:(k + 1) * D], lo[c])
                    step(dve.scalar_tensor_tensor(lo[c].nmr[:, :], lo[c].mean, -1.0, lo[c].rstd[:, :], ALU.mult, ALU.mult))
                    dve.sem_inc(ostats, 1)

                def group(g, b):
                    if there(g + 2, NG):
                        normalize(g + 2, (b + 2) % R)
                    out_stats(g, b)

                normalize(0, 0)
                normalize(1, 1)
                over(dve, NG, R, group)

            @block.scalar
            def _(act):
                def evacuate(g, b):
                    c = b % 2
                    act.wait_ge(turned, g + 1)
                    wait(act, mo, g - 1)
                    act.activation(ht[c][:, :], bank[c][:, 0:GC], ACT.Relu)
                    act.activation(at[c][:, :], bank[2 + c][:, 0:GC], ACT.Copy).then_inc(evac, 1)

                def silu(g, b):
                    c = b % 2
                    act.wait_ge(mm, g + 1)
                    act.activation(ut[c][:, :], bank[4 + c][:, 0:GC], ACT.Silu, bias=b1[:, 0:1]).then_inc(silued, 1)

                def out_normalize(g, b):
                    c = b % 2
                    act.wait_ge(ostats, g + 1)
                    wait(act, sums, 3 * (g - 1))
                    for k in range(K):
                        last = act.activation(yn[c][:, k, :], bank[6 + c][0:P, k * D:(k + 1) * D], ACT.Identity,
                                              bias=lo[c].nmr[:, k:k + 1], scale=lo[c].rstd[:, k:k + 1])
                    last.then_inc(onormed, 1)

                def group(g, b):
                    silu(g, b)
                    if there(g + 1, NG):
                        evacuate(g + 1, (b + 1) % R)
                    if there(g - 1, NG):
                        out_normalize(g - 1, (b - 1) % R)

                act.wait_ge(consts, 16 * (5 + 3 * K))
                evacuate(0, 0)
                over(act, NG, R, group)
                out_normalize(NG - 1, R - 1)

            @block.gpsimd
            def _(pool):
                pool.wait_ge(consts, 16 * (5 + 3 * K))

                def finish(g, b):
                    c = b % 2
                    pool.wait_ge(onormed, g + 1)
                    pool.tensor_tensor(yn[c][:, :, :], yn[c][:, :, :], gain[:, :, :], ALU.mult).then_inc(sums, 1)
                    wait(pool, stored[b], 8 * (g - b))
                    pool.tensor_tensor(z[b][:, :, :], x[b][:, :, :], shift[:, :, :], ALU.add).then_inc(sums, 1)
                    pool.wait_ge(sums, 3 * g + 2)
                    pool.tensor_tensor(z[b][:, :, :], z[b][:, :, :], yn[c][:, :, :], ALU.add).then_inc(sums, 1)
                over(pool, NG, R, finish)

            @block.tensor
            def _(pe):
                pe.wait_ge(consts, 16 * (5 + 3 * K))
                pe.wait_ge(made, 1)

                def turn(g, b):
                    c = b % 2
                    pe.wait_ge(normed, g + 1)
                    for k in range(K):
                        pe.transpose(bank[c][:, k * P:(k + 1) * P], xn[c][:, k, :], ident[0:P, 0:P])
                    for k in range(K):
                        last = pe.transpose(bank[2 + c][:, k * P:(k + 1) * P], ag[b][:, k, :], ident[0:P, 0:P])
                    last.then_inc(turned, 1)

                def hidden(g, b):
                    c = b % 2
                    pe.wait_ge(evac, g + 1)
                    pe.matmul(bank[4 + c][:, 0:GC], wh[:, :], ht[c][:, :], start=True, stop=False)
                    pe.matmul(bank[4 + c][:, 0:GC], wa[:, :], at[c][:, :], start=False, stop=True).then_inc(mm, 1)

                def outer(g, b):
                    c = b % 2
                    o = bank[6 + c]
                    wait(pe, onormed, g - 1)
                    pe.matmul(o[0:P, 0:K * D], ones[:, :], b2s[:, :], start=True, stop=False)
                    for k in range(K):
                        pe.matmul(o[0:P, k * D:(k + 1) * D], ht[c][:, k * P:(k + 1) * P], wr[:, :], start=False, stop=False)
                    pe.wait_ge(silued, g + 1)
                    for k in range(K):
                        last = pe.matmul(o[0:P, k * D:(k + 1) * D], ut[c][:, k * P:(k + 1) * P], w2[:, :],
                                         start=False, stop=(k == K - 1))
                    last.then_inc(mo, 1)

                def group(g, b):
                    hidden(g, b)
                    if there(g + 1, NG):
                        turn(g + 1, (b + 1) % R)
                    outer(g, b)

                turn(0, 0)
                over(pe, NG, R, group)


def layer3_nodes(nc, a, sem, sb, bank, ident, x3, agg3, out, node_rows):
    with ExitStack() as ctx:
        t_ = lambda name, shape, dt=F32: sb("f_" + name, shape, dt, ctx)
        R = 4
        four, two = range(R), range(2)
        w1 = t_("w1", [D, 2 * D])
        w2 = t_("w2", [D, 2, D])
        b1 = t_("b1", [D, 2])
        eps1 = t_("eps1", [D, 1])
        b2 = t_("b2", [65, K * D])
        part = t_("part", [65, K * D])
        b2s = t_("b2s", [65, K * D], BF16)
        ones = t_("ones", [65, P], BF16)
        x = [t_(f"x{b}", [P, K, D]) for b in four]
        ag = [t_(f"ag{b}", [P, K, D]) for b in four]
        z = [t_(f"z{b}", [P, K, D]) for b in four]
        xn = [t_(f"xn{b}", [P, K, D]) for b in two]
        ht, rt, ut, vt = ([t_(f"{n}{b}", [D, GC]) for b in two] for n in ("ht", "rt", "ut", "vt"))
        ln = [Stats(t_, f"ln{b}", K) for b in two]
        loaded, stored = ([sem(f"f_{s}{b}") for b in four] for s in ("loaded", "stored"))
        consts, made, made_s, in_s, normed, turned, relued, rst, mm, relued2, mo, sums = (
            sem("f_" + s) for s in ("consts", "made", "made_s", "in_s", "normed", "turned", "relued", "rst",
                                    "mm", "relued2", "mo", "sums"))
        held = sem("passed")
        n_consts = 16 * (4 + K + 1)
        with nc.Block() as block:
            @block.sync
            def _(sp):
                sp.dma_start(w1[:, :], a["L3_gnn_W1"]).then_inc(consts, 16)
                sp.dma_start(w2[:, :, :], a["L3_gnn_W2"].rearrange("(h q) d -> q h d", h=2)).then_inc(consts, 16)
                for h in two:
                    sp.dma_start(b1[:, h:h + 1], a["L3_gnn_b1"][h * D:(h + 1) * D].rearrange("(q o) -> q o", o=1)).then_inc(consts, 16)
                sp.dma_start(eps1[:, :], a["L3_gnn_eps"].rearrange("(o d) -> o d", o=1).broadcast_to([D, 1])).then_inc(consts, 16)
                for k in range(K):
                    sp.dma_start(b2[:, k * D:(k + 1) * D], a["L3_gnn_b2"].rearrange("(o d) -> o d", o=1).broadcast_to([65, D])).then_inc(consts, 16)

                def load(g, b):
                    sp.dma_start(x[b][:, :, :], node_rows(x3, g)).then_inc(loaded[b], 16)
                    sp.dma_start(ag[b][:, :, :], node_rows(agg3, g)).then_inc(loaded[b], 16)

                def move(g, b):
                    sp.wait_ge(sums, g + 1)
                    sp.dma_start(node_rows(out, g), z[b][:, :, :]).then_inc(stored[b], 16)
                    if there(g + R, NG):
                        load(g + R, b)

                for b in four:
                    load(b, b)
                over(sp, NG, R, move)
                for b in four:
                    sp.wait_ge(stored[b], 16 * (NG // R))

            @block.vector
            def _(dve):
                step = Steps(dve, made_s, 0)
                dve.wait_ge(consts, n_consts)
                dve.memset(ones[:, :], 0.0)
                step(dve.memset(b2s[:, :], 0.0))
                for p in (0, 32, 64):
                    dve.memset(ones[p:p + 1, :], 1.0)
                step(dve.tensor_scalar(eps1[:, :], eps1[:, :], 1.0, None, ALU.add))
                step(dve.tensor_copy(b2s[0:1, :], b2[0:1, :]))
                step(dve.tensor_copy(b2s[32:33, :], b2[32:33, :]))
                step(dve.tensor_tensor(part[32:33, :], b2[32:33, :], b2s[32:33, :], ALU.subtract))
                step(dve.tensor_copy(b2s[32:33, :], part[32:33, :]))
                step(dve.tensor_copy(b2s[64:65, :], b2[64:65, :]))
                step(dve.tensor_tensor(part[64:65, :], b2[64:65, :], b2s[64:65, :], ALU.subtract))
                step(dve.tensor_copy(b2s[64:65, :], part[64:65, :]))
                step(dve.tensor_tensor(part[64:65, :], part[64:65, :], b2s[64:65, :], ALU.subtract))
                dve.tensor_copy(b2s[64:65, :], part[64:65, :]).then_inc(made, 1)

                def normalize(g, b):
                    c = b % 2
                    step = Steps(dve, in_s, g * STATS, held)
                    dve.wait_ge(loaded[b], 8 * (g - b + R))
                    row_stats(dve, step, lambda k: x[b][:, k, :], ln[c])
                    wait(dve, turned, g - 1)
                    for k in range(K):
                        last = dve.tensor_scalar(xn[c][:, k, :], x[b][:, k, :], ln[c].mv[:, k, 0:1], ln[c].rstd[:, k:k + 1],
                                                 ALU.subtract, ALU.mult)
                    last.then_inc(normed, 1)

                def combine(g, b):
                    c = b % 2
                    dve.wait_ge(relued, g + 1)
                    wait(dve, mm, g - 1)
                    dve.scalar_tensor_tensor(rt[c][:, :], ht[c][:, :], eps1[:, 0:1], bank[2 + c][:, 0:GC], ALU.mult, ALU.add).then_inc(rst, 1)

                def finish(g, b):
                    c = b % 2
                    dve.wait_ge(mo, g + 1)
                    wait(dve, stored[b], 4 * (g - b))
                    dve.scalar_tensor_tensor(z[b][:, :, :].rearrange("p k d -> p (k d)"), bank[6 + c][0:P, 0:K * D], 0.0,
                                             x[b][:, :, :].rearrange("p k d -> p (k d)"), ALU.max, ALU.add).then_inc(sums, 1)

                def group(g, b):
                    if there(g + 2, NG):
                        normalize(g + 2, (b + 2) % R)
                    if there(g + 1, NG):
                        combine(g + 1, (b + 1) % R)
                    finish(g, b)

                normalize(0, 0)
                normalize(1, 1)
                combine(0, 0)
                over(dve, NG, R, group)

            @block.scalar
            def _(act):
                act.wait_ge(consts, n_consts)

                def evacuate(g, b):
                    c = b % 2
                    act.wait_ge(turned, g + 1)
                    wait(act, rst, g - 1)
                    act.activation(ht[c][:, :], bank[c][:, 0:GC], ACT.Relu).then_inc(relued, 1)

                def relu(g, b):
                    c = b % 2
                    act.wait_ge(mm, g + 1)
                    wait(act, mo, g - 1)
                    act.activation(ut[c][:, :], bank[4][:, 0:GC], ACT.Relu, bias=b1[:, 0:1])
                    act.activation(vt[c][:, :], bank[5][:, 0:GC], ACT.Relu, bias=b1[:, 1:2]).then_inc(relued2, 1)

                def group(g, b):
                    relu(g, b)
                    if there(g + 1, NG):
                        evacuate(g + 1, (b + 1) % R)

                evacuate(0, 0)
                over(act, NG, R, group)

            @block.tensor
            def _(pe):
                pe.wait_ge(consts, n_consts)
                pe.wait_ge(made, 1)

                def turn(g, b):
                    c = b % 2
                    pe.wait_ge(normed, g + 1)
                    for k in range(K):
                        pe.transpose(bank[c][:, k * P:(k + 1) * P], xn[c][:, k, :], ident[0:P, 0:P])
                    for k in range(K):
                        last = pe.transpose(bank[2 + c][:, k * P:(k + 1) * P], ag[b][:, k, :], ident[0:P, 0:P])
                    last.then_inc(turned, 1)

                def hidden(g, b):
                    c = b % 2
                    pe.wait_ge(rst, g + 1)
                    wait(pe, relued2, g)
                    pe.matmul(bank[4][:, 0:GC], w1[:, 0:D], rt[c][:, :], start=True, stop=True)
                    pe.matmul(bank[5][:, 0:GC], w1[:, D:2 * D], rt[c][:, :], start=True, stop=True).then_inc(mm, 1)

                def outer(g, b):
                    c = b % 2
                    o = bank[6 + c]
                    wait(pe, sums, g - 1)
                    pe.matmul(o[0:P, 0:K * D], ones[:, :], b2s[:, :], start=True, stop=False)
                    pe.wait_ge(relued2, g + 1)
                    for k in range(K):
                        pe.matmul(o[0:P, k * D:(k + 1) * D], ut[c][:, k * P:(k + 1) * P], w2[:, 0, :], start=False, stop=False)
                    for k in range(K):
                        last = pe.matmul(o[0:P, k * D:(k + 1) * D], vt[c][:, k * P:(k + 1) * P], w2[:, 1, :],
                                         start=False, stop=(k == K - 1))
                    last.then_inc(mo, 1)

                def group(g, b):
                    hidden(g, b)
                    if there(g + 1, NG):
                        turn(g + 1, (b + 1) % R)
                    outer(g, b)

                turn(0, 0)
                over(pe, NG, R, group)


_INS = ['x', 'src', 'dst', 'L0_gnn_a_i', 'L0_gnn_a_j', 'L0_gnn_W', 'L1_gnn_agg_W', 'L1_gnn_agg_b', 'L1_gnn_edge_W1',
        'L1_gnn_edge_b1', 'L1_gnn_edge_W2', 'L1_gnn_edge_b2', 'L1_gnn_upd_W1', 'L1_gnn_upd_b1', 'L1_gnn_upd_W2',
        'L1_gnn_upd_b2', 'L1_gnn_ln_g', 'L1_gnn_ln_b', 'L1_gnn_res_W', 'L2_gnn_W', 'L3_gnn_eps', 'L3_gnn_W1',
        'L3_gnn_b1', 'L3_gnn_W2', 'L3_gnn_b2']


def kernel(**inputs):
    import numpy as _np
    import concourse.bacc as _bacc
    from concourse import mybir as _mybir
    from concourse.bass_utils import run_bass_kernel_spmd as _run

    nc = _bacc.Bacc("TRN2", target_bir_lowering=False, num_devices=1)
    laid = {name: _np.ascontiguousarray(inputs[name]) for name in _INS}
    src, dst = laid['src'], laid['dst']
    laid['src_t'] = _np.ascontiguousarray(src.reshape(ET, P).T)
    laid['dst_t'] = _np.ascontiguousarray(dst.reshape(ET, P).T)
    laid['dst_rows'] = _np.ascontiguousarray(dst.reshape(ET, P))
    laid['src_p'] = _np.ascontiguousarray(src.reshape(P, ET).T)
    laid['attr'] = _np.ascontiguousarray(_np.asarray(inputs['edge_attr_4']).T)
    laid['w2t'] = _np.ascontiguousarray(_np.asarray(inputs['L2_gnn_W']).T)
    arrays, aps = {}, {}
    for name, v in laid.items():
        arrays[f"in_{name}"] = v
        aps[name] = nc.dram_tensor(f"in_{name}", v.shape, _mybir.dt.from_np(v.dtype), kind="ExternalInput").ap()
    out = nc.dram_tensor("out_x", (N, D), F32, kind="ExternalOutput").ap()
    program(nc, aps, out)
    r = _run(nc, [arrays], core_ids=[0])
    return r.results[0]["out_x"]
```

```python
from contextlib import ExitStack, contextmanager

import concourse.bass as bass
from concourse import mybir

F32 = mybir.dt.float32
BF16 = mybir.dt.bfloat16
I32 = mybir.dt.int32
ALU = mybir.AluOpType
ACT = mybir.ActivationFunctionType

N = 50000
E = 25000
D = 128
P = 125
ET = E // P
K = 4
EG = ET // K
NG = N // (P * K)
GC = P * K
EPS = 1e-5
BIG = 1e38
DUMP = 2 * K * P
SKIP = 1 << 24
FILL = 16


def ds(start, size):
    return bass.ds(start, size)


class Steps:

    def __init__(self, eng, sem, base, passed, between=()):
        self.eng, self.sem, self.value, self.passed, self.between = eng, sem, base, passed, list(between)

    def __call__(self, ins):
        ins.then_inc(self.sem, 1)
        self.value = self.value + 1
        if self.between:
            self.between.pop(0)()
        self.eng.wait_ge(self.sem, self.value)

    def rest(self):
        for emit in self.between:
            emit()


STATS = 14
MAGIC = 0x5F3759DF


class Stats:

    def __init__(self, t_, name, n):
        self.n = n
        self.st, self.mv = t_(name + "_st", [P, n, 6]), t_(name + "_mv", [P, n, 2])
        self.v, self.a, self.y, self.nmr = (t_(f"{name}_{s}", [P, n]) for s in ("v", "a", "y", "nmr"))
        self.mean, self.rstd = self.mv[:, :, 0], self.y


def moments(dve, s, k, rows):
    return dve.bn_stats(s.st[:, k, :], rows)


def roots(dve, step, s, last, lo, hi):
    step(last)
    dve.sem_inc(step.passed, 1)
    for k in range(lo, hi):
        last = dve.bn_aggr(s.mv[:, k, :], s.st[:, k, :])
    step(last)
    v, a, y = (x[:, lo:hi] for x in (s.v, s.a, s.y))
    step(dve.tensor_scalar(v, s.mv[:, lo:hi, 1], EPS, None, ALU.add))
    step(dve.tensor_scalar(a.bitcast(I32), v.bitcast(I32), 1, None, ALU.logical_shift_right))
    step(dve.tensor_scalar(y.bitcast(I32), a.bitcast(I32), -1.0, float(MAGIC), ALU.mult, ALU.add))
    for n in range(3):
        step(dve.scalar_tensor_tensor(a, y, -0.5, y, ALU.mult, ALU.mult))
        step(dve.tensor_tensor(a, a, v, ALU.mult))
        last = dve.scalar_tensor_tensor(y, a, 1.5, y, ALU.add, ALU.mult)
        if n < 2:
            step(last)
    return last


def minus_mean_over_root(dve, s, lo, hi):
    return dve.scalar_tensor_tensor(s.nmr[:, lo:hi], s.mv[:, lo:hi, 0], -1.0, s.y[:, lo:hi], ALU.mult, ALU.mult)


def over(eng, n, unroll, ahead, body):
    loops = (n - ahead) // unroll
    for g in range(unroll):
        body(g, g, 0)
    with eng.Fori(1, loops) as i:
        for b in range(unroll):
            body(unroll * i + b, b, i)
    for g in range(unroll * loops, n):
        body(g, g % unroll, g // unroll)


def wait(eng, s, value):
    if not isinstance(value, int) or value > 0:
        eng.wait_ge(s, value)


def there(g, n):
    return not isinstance(g, int) or 0 <= g < n


def program(nc, a, out):
    with ExitStack() as whole:
        bank = [whole.enter_context(nc.psum_tensor(f"bank{i}", [128, 512], F32)) for i in range(8)]

        def sb(name, shape, dt=F32, ctx=whole):
            return ctx.enter_context(nc.sbuf_tensor(name, shape, dt))

        def dram(name, rows):
            return nc.dram_tensor(name, (rows, D), F32, kind="Internal").ap()

        agg0 = dram("agg0", N + DUMP)
        agg1 = dram("agg1", N)
        x1 = dram("x1", N)
        x2 = dram("x2", N)
        x3 = dram("x3", N + DUMP)

        ident = sb("ident", [128, 128])
        dst_t = sb("dst_t", [P, ET], I32)
        src_t = sb("src_t", [P, ET], I32)
        key_t = sb("key_t", [P, ET])
        prev_t = sb("prev_t", [P, ET])
        end_t = sb("end_t", [P, ET], I32)
        add_t = sb("add_t", [P, ET], I32)
        ew_t = sb("ew_t", [P, ET])

        node_rows = lambda ap, g: ap[ds(g * GC, GC), :].rearrange("(p k) d -> p k d", k=K)

        with semaphores(nc, whole) as sem:
            prepare(nc, a, sem, sb, bank, ident, dst_t, src_t, key_t, prev_t, end_t, add_t)
            with ExitStack() as ctx:
                esb = lambda name, shape, dt=F32: sb(name, shape, dt, ctx)
                h_dst = esb("h_dst", [P, ET * D])
                si = esb("si", [P, ET])
                sj = esb("sj", [P, ET])
                alpha = esb("alpha", [P, ET])
                src_p = esb("src_p", [P, ET], I32)
                dst_p = esb("dst_p", [P, ET], I32)
                edge_rows(nc, a, sem, sb, bank, agg0, agg1, x3, h_dst, si, sj, src_p, dst_p, ew_t)
                softmax(nc, sem, sb, bank, ident, si, sj, dst_p, alpha)
                scatter_by_source(nc, a, sem, sb, bank, agg0, h_dst, alpha, src_p)
            layer0_nodes(nc, a, sem, sb, bank, ident, agg0, x1, node_rows)
        with semaphores(nc, whole) as sem:
            edges(nc, a, sem, sb, bank, 1, ident, x1, agg1, src_t, key_t, prev_t, end_t, ew_t)
            layer1_nodes(nc, a, sem, sb, bank, ident, x1, agg1, x2, x3, node_rows)
        with semaphores(nc, whole) as sem:
            edges(nc, a, sem, sb, bank, 2, ident, x2, x3, src_t, key_t, prev_t, add_t, ew_t)
            edges(nc, a, sem, sb, bank, 3, ident, x3, agg1, src_t, key_t, prev_t, end_t, ew_t)
            layer3_nodes(nc, a, sem, sb, bank, ident, x3, agg1, out, node_rows)


@contextmanager
def semaphores(nc, whole):
    with ExitStack() as ctx:
        known, kept = {}, {}

        def sem(name, pool=False):
            mine = kept if pool else known
            if name not in mine:
                mine[name] = (whole if pool else ctx).enter_context(nc.semaphore(name))
            return mine[name]
        yield sem
        with nc.Block() as block:
            @block.sync
            def _(sp):
                for s in known.values():
                    sp.sem_clear(s)


def prepare(nc, a, sem, sb, bank, ident, dst_t, src_t, key_t, prev_t, end_t, add_t):
    with ExitStack() as ctx:
        loaded, made, step_s = sem("p_loaded"), sem("p_made"), sem("p_step")
        nxt = sb("nxt", [P, ET], F32, ctx)
        nxt_i = sb("nxt_i", [P, ET], I32, ctx)
        prev_i = sb("prev_i", [P, ET], I32, ctx)
        spare = sb("spare", [P, ET], F32, ctx)
        isend = sb("isend", [P, ET], F32, ctx)
        tmp = sb("tmp", [P, ET], F32, ctx)
        with nc.Block() as block:
            @block.sync
            def _(sp):
                sp.dma_start(dst_t[:, :], a["dst_t"]).then_inc(loaded, 16)
                sp.dma_start(src_t[:, :], a["src_t"]).then_inc(loaded, 16)
                sp.dma_start(nxt_i[0:P - 1, :], a["dst_t"][1:P, :]).then_inc(loaded, 16)
                sp.dma_start(nxt_i[P - 1:P, 0:ET - 1], a["dst_t"][0:1, 1:ET]).then_inc(loaded, 16)
                sp.dma_start(nxt_i[P - 1:P, ET - 1:ET], a["dst_t"][P - 1:P, ET - 1:ET]).then_inc(loaded, 16)
                sp.dma_start(prev_i[:, 1:ET], a["dst_t"][P - 1:P, 0:ET - 1].broadcast_to([P, ET - 1])).then_inc(loaded, 16)

            @block.gpsimd
            def _(pool):
                pool.memset(ident[:, :], 0.0).then_inc(made, 1)
                pool.wait_ge(made, 1)
                pool.affine_select(out=ident[:, :], in_=ident[:, :], compare_op=ALU.not_equal, fill=1.0,
                                   base=0, pattern=[[-1, 128]], channel_multiplier=1).then_inc(made, 1)
                pool.iota(spare[:, :], pattern=[[0, ET // (2 * K)], [P, 2 * K]], base=N,
                          channel_multiplier=1, allow_small_or_imprecise_dtypes=True).then_inc(made, 1)

            @block.vector
            def _(dve):
                step = Steps(dve, step_s, 0, None)
                dve.wait_ge(loaded, 96)
                step(dve.tensor_copy(key_t[:, :], dst_t[:, :]))
                step(dve.tensor_copy(nxt[:, :], nxt_i[:, :]))
                dve.tensor_copy(prev_t[:, 1:ET], prev_i[:, 1:ET])
                step(dve.memset(prev_t[:, 0:1], -1.0))
                dve.wait_ge(made, 3)
                step(dve.tensor_scalar(tmp[:, :], prev_t[:, :], 1.0, ident[0:P, P - 1:P], ALU.add, ALU.mult))
                step(dve.tensor_scalar(prev_t[:, :], tmp[:, :], 1.0, None, ALU.subtract))
                step(dve.tensor_tensor(isend[:, :], key_t[:, :], nxt[:, :], ALU.not_equal))
                step(dve.tensor_tensor(isend[:, ET - 1:ET], isend[:, ET - 1:ET], ident[0:P, P - 1:P], ALU.max))
                step(dve.scalar_tensor_tensor(tmp[:, :], key_t[:, :], float(SKIP), isend[:, :], ALU.subtract, ALU.mult))
                step(dve.tensor_scalar(end_t[:, :], tmp[:, :], float(SKIP), None, ALU.add))
                step(dve.tensor_tensor(tmp[:, :], key_t[:, :], spare[:, :], ALU.subtract))
                step(dve.tensor_tensor(nxt[:, :], tmp[:, :], isend[:, :], ALU.mult))
                step(dve.tensor_tensor(add_t[:, :], nxt[:, :], spare[:, :], ALU.add))


def edge_rows(nc, a, sem, sb, bank, agg0, agg1, x3, h_dst, si, sj, src_p, dst_p, ew_t):
    with ExitStack() as ctx:
        t_ = lambda name, shape, dt=F32: sb("a_" + name, shape, dt, ctx)
        zeros = t_("zeros", [P, FILL * D])
        R = 4
        xg = [t_(f"xg{b}", [P, 2 * K, D]) for b in range(R)]
        hs = [t_(f"hs{b}", [P, K, D]) for b in range(2)]
        cur = [t_(f"cur{b}", [P, 2 * K], I32) for b in range(R)]
        ln = [Stats(t_, f"ln{b}", 2 * K) for b in range(2)]
        junk = t_("junk", [P, 2 * K, D])
        sc = [t_(f"sc{b}", [P, 2 * K]) for b in range(2)]
        ai = t_("ai", [P, D])
        aj = t_("aj", [P, D])
        w1 = t_("w1", [4, D])
        b1 = t_("b1", [D, 1])
        w2 = t_("w2", [D, 1])
        b2 = t_("b2", [P, 1])
        at = [t_(f"at{b}", [4, GC]) for b in range(2)]
        hid = [t_(f"hid{b}", [D, GC]) for b in range(2)]
        consts, zeroed, filled = sem("a_consts"), sem("a_zeroed"), sem("a_filled")
        gathered = [sem(f"a_gathered{b}", pool=True) for b in range(R)]
        attr = [sem(f"a_attr{b}") for b in range(2)]
        staged, stats, relued, dots, copied, step_s, hid_mm, hid_done, ew_mm = (
            sem("a_" + s) for s in ("staged", "stats", "relued", "dots", "copied", "step", "hid_mm", "hid_done", "ew_mm"))
        passed = sem("passed")
        fills = N // (P * FILL)
        assert fills * P * FILL == N and 2 * fills == EG
        with nc.Block() as block:
            @block.sync
            def _(sp):
                row = lambda n: a[n].rearrange("(o d) -> o d", o=1)
                sp.dma_start(src_p[:, :], a["src"].rearrange("(p t) -> p t", t=ET)).then_inc(consts, 16)
                sp.dma_start(dst_p[:, :], a["dst"].rearrange("(p t) -> p t", t=ET)).then_inc(consts, 16)
                sp.dma_start(ai[:, :], row("L0_gnn_a_i").broadcast_to([P, D])).then_inc(consts, 16)
                sp.dma_start(aj[:, :], row("L0_gnn_a_j").broadcast_to([P, D])).then_inc(consts, 16)
                sp.dma_start(w1[:, :], a["L1_gnn_edge_W1"]).then_inc(consts, 16)
                sp.dma_start(b1[:, :], a["L1_gnn_edge_b1"].rearrange("(d o) -> d o", o=1)).then_inc(consts, 16)
                sp.dma_start(w2[:, :], a["L1_gnn_edge_W2"]).then_inc(consts, 16)
                sp.dma_start(b2[:, :], row("L1_gnn_edge_b2").broadcast_to([P, 1])).then_inc(consts, 16)
                sp.wait_ge(zeroed, 1)
                for agg in (agg0, x3):
                    sp.dma_start(agg[N:N + DUMP, :].rearrange("(p r) d -> p (r d)", r=DUMP // P), zeros[:, 0:DUMP // P * D]).then_inc(filled, 16)

                def supply(j, b, i):
                    wait(sp, hid_mm, j - 1)
                    sp.dma_start(at[b][:, :], a["attr"][:, ds(j * GC, GC)]).then_inc(attr[b], 16)
                    agg = (agg0, agg1)[b]
                    sp.dma_start(agg[ds(i * P * FILL, P * FILL), :].rearrange("(p r) d -> p (r d)", r=FILL), zeros[:, :]).then_inc(filled, 16)
                over(sp, EG, 2, 1, supply)
                sp.wait_ge(filled, (2 * fills + 2) * 16)

            @block.gpsimd
            def _(pool):
                pool.memset(zeros[:, :], 0.0).then_inc(zeroed, 1)
                pool.wait_ge(consts, 128)

                def gather(j, b, i):
                    wait(pool, relued, 2 * K * (j - R + 1))
                    pool.sem_inc(passed, 1)
                    pool.tensor_copy(cur[b][:, 0:K], dst_p[:, ds(j * K, K)]).then_inc(staged, 1)
                    pool.tensor_copy(cur[b][:, K:2 * K], src_p[:, ds(j * K, K)]).then_inc(staged, 1)
                    pool.wait_ge(staged, 2 * j + 2)
                    pool.sem_inc(passed, 1)
                    for k in range(2 * K):
                        pool.indirect_dma_start(
                            out=xg[b][:, k, :], out_offset=None, in_=a["x"][:, :],
                            in_offset=bass.IndirectOffsetOnAxis(ap=cur[b][:, k:k + 1], axis=0)).then_inc(gathered[b], 16)
                over(pool, EG, R, 1, gather)

            @block.vector
            def _(dve):
                dve.wait_ge(consts, 128)

                def dot(j, c):
                    def one(k, o, h, v):
                        ins = dve.scalar_tensor_tensor(junk[:, o + k, :], h, 1.0, v[:, :], ALU.mult, ALU.mult,
                                                       accum_out=sc[c][:, o + k:o + k + 1])
                        if o and k == K - 1:
                            ins.then_inc(dots, 1)
                    return ([lambda k=k: one(k, 0, h_dst[:, ds((j * K + k) * D, D)], ai) for k in range(K)]
                            + [lambda k=k: one(k, K, hs[c][:, k, :], aj) for k in range(K)])

                def scores(j, b, i, between=()):
                    c = b % 2
                    step = Steps(dve, step_s, j * STATS, passed, between)
                    dve.wait_ge(gathered[b], 128 * (i + 1))
                    for k in range(2 * K):
                        last = moments(dve, ln[c], k, xg[b][:, k, :])
                    step(roots(dve, step, ln[c], last, 0, 2 * K))
                    minus_mean_over_root(dve, ln[c], 0, 2 * K).then_inc(stats, 1)
                    step.rest()

                def group(j, b, i):
                    c = b % 2
                    dve.wait_ge(relued, 2 * K * (j + 1))
                    wait(dve, copied, j - 1)
                    if there(j + 2, EG):
                        scores(j + 2, (b + 2) % R, i + (b + 2) // R, dot(j, c))
                    else:
                        for emit in dot(j, c):
                            emit()
                    dve.wait_ge(dots, j + 1)
                    dve.tensor_copy(si[:, ds(j * K, K)], sc[c][:, 0:K])
                    dve.tensor_copy(sj[:, ds(j * K, K)], sc[c][:, K:2 * K]).then_inc(copied, 1)

                scores(0, 0, 0)
                scores(1, 1, 0)
                over(dve, EG, R, 2, group)

            @block.scalar
            def _(act):
                act.wait_ge(consts, 128)

                def relu(j, b, i):
                    c = b % 2
                    act.wait_ge(stats, j + 1)
                    wait(act, dots, j - 1)
                    for k in range(2 * K):
                        o = h_dst[:, ds((j * K + k) * D, D)] if k < K else hs[c][:, k - K, :]
                        act.activation(o, xg[b][:, k, :], ACT.Relu, bias=ln[c].nmr[:, k:k + 1],
                                       scale=ln[c].rstd[:, k:k + 1]).then_inc(relued, 1)
                    act.wait_ge(hid_mm, j + 1)
                    act.activation(hid[c][:, :], bank[c][:, 0:GC], ACT.Silu, bias=b1[:, 0:1]).then_inc(hid_done, 1)

                over(act, EG, R, 1, relu)
                act.wait_ge(ew_mm, EG)
                act.activation(ew_t[:, :], bank[2][0:P, 0:ET], ACT.Sigmoid, bias=b2[:, 0:1])

            @block.tensor
            def _(pe):
                pe.wait_ge(consts, 128)

                def hidden(j, b, i):
                    pe.wait_ge(attr[b], 16 * (i + 1))
                    pe.matmul(bank[b][:, 0:GC], w1[:, :], at[b][:, :], start=True, stop=True).then_inc(hid_mm, 1)

                def weigh(j, b, i):
                    pe.wait_ge(hid_done, j + 1)
                    for k in range(K):
                        last = pe.matmul(bank[2][0:P, ds(j * K + k, 1)], hid[b][:, k * P:(k + 1) * P], w2[:, :],
                                         start=True, stop=True)
                    last.then_inc(ew_mm, 1)
                    if there(j + 2, EG):
                        hidden(j + 2, b, i + 1)

                hidden(0, 0, 0)
                hidden(1, 1, 0)
                over(pe, EG, 2, 2, weigh)


def softmax(nc, sem, sb, bank, ident, si, sj, dst_p, alpha):
    with ExitStack() as ctx:
        t_ = lambda name, shape: sb("s_" + name, shape, F32, ctx)
        key, e, same, gate, f, f2, bk, w = (t_(n, [P, ET]) for n in ("key", "e", "same", "gate", "f", "f2", "bk", "w"))
        gate_b = t_("gate_b", [P, ET])
        cols = t_("cols", [P, 1])
        row = {n: t_("row_" + n, [1, 128]) for n in
               ("k0", "kl", "cont", "on", "g_on", "g_cont", "onb", "g_onb", "g_contb", "edge", "run", "enter", "rev")}
        step_s, rows_s, cols_s, e1, e2 = (sem("s_" + n) for n in ("step", "rows", "cols", "e1", "e2"))
        counts = {"step": 0, "t": 0}
        jobs = []

        with nc.Block() as block:
            @block.vector
            def _(dve):
                step = Steps(dve, step_s, 0, None)

                def to_row(dst_row, col):
                    step(dve.tensor_copy(cols[:, :], col))
                    dve.sem_inc(rows_s, 1)
                    jobs.append("row")
                    dve.wait_ge(cols_s, len(jobs))
                    step(dve.tensor_copy(dst_row[0:1, 0:P], bank[0][0:1, 0:P]))

                def to_col(src_row):
                    dve.sem_inc(rows_s, 1)
                    jobs.append("col")
                    dve.wait_ge(cols_s, len(jobs))
                    step(dve.tensor_copy(cols[:, :], bank[1][0:P, 0:1]))

                r = {n: x[0:1, 0:P] for n, x in row.items()}
                step(dve.tensor_copy(key[:, :], dst_p[:, :]))
                step(dve.tensor_tensor(f[:, :], si[:, :], sj[:, :], ALU.add))
                step(dve.scalar_tensor_tensor(e[:, :], f[:, :], 0.01, f[:, :], ALU.mult, ALU.max))
                dve.memset(same[:, :], 1.0)
                step(dve.tensor_tensor(gate_b[:, 1:ET], key[:, 1:ET], key[:, 0:ET - 1], ALU.is_equal))
                step(dve.tensor_copy(same[:, 1:ET], gate_b[:, 1:ET]))
                step(dve.tensor_scalar(gate[:, :], same[:, :], 1.0, BIG, ALU.subtract, ALU.mult))
                step(dve.memset(gate_b[:, :], 0.0))
                step(dve.tensor_copy(gate_b[:, 0:ET - 1], gate[:, 1:ET]))
                to_row(row["k0"], key[:, 0:1])
                to_row(row["kl"], key[:, ET - 1:ET])
                step(dve.memset(r["cont"], 0.0))
                step(dve.tensor_tensor(row["cont"][0:1, 1:P], row["k0"][0:1, 1:P], row["kl"][0:1, 0:P - 1], ALU.is_equal))
                step(dve.tensor_tensor(r["edge"], r["k0"], r["kl"], ALU.is_equal))
                step(dve.tensor_tensor(r["on"], r["edge"], r["cont"], ALU.mult))
                step(dve.tensor_scalar(r["g_on"], r["on"], 1.0, BIG, ALU.subtract, ALU.mult))
                step(dve.tensor_scalar(r["g_cont"], r["cont"], 1.0, BIG, ALU.subtract, ALU.mult))
                step(dve.memset(r["g_contb"], -BIG))
                step(dve.tensor_copy(row["g_contb"][0:1, 0:P - 1], row["g_cont"][0:1, 1:P]))
                step(dve.tensor_scalar(r["onb"], r["edge"], 1.0, BIG, ALU.subtract, ALU.mult))
                step(dve.tensor_tensor(r["g_onb"], r["g_contb"], r["onb"], ALU.min))

                def back_max(x, res):
                    step(dve.tensor_tensor_scan(f2[:, ::-1], gate_b[:, ::-1], x[:, ::-1], -BIG, ALU.add, ALU.max))
                    to_row(row["edge"], f2[:, 0:1])
                    step(dve.tensor_tensor_scan(row["run"][0:1, P - 1::-1], row["g_onb"][0:1, P - 1::-1],
                                                row["edge"][0:1, P - 1::-1], -BIG, ALU.add, ALU.max))
                    step(dve.memset(r["enter"], -BIG))
                    step(dve.tensor_tensor(row["enter"][0:1, 0:P - 1], row["run"][0:1, 1:P], row["g_contb"][0:1, 0:P - 1], ALU.add))
                    to_col(row["enter"])
                    step(dve.tensor_tensor_scan(res[:, ::-1], gate_b[:, ::-1], x[:, ::-1], cols[:, 0:1], ALU.add, ALU.max))

                step(dve.tensor_tensor_scan(f[:, :], gate[:, :], e[:, :], -BIG, ALU.add, ALU.max))
                to_row(row["edge"], f[:, ET - 1:ET])
                step(dve.tensor_tensor_scan(r["run"], r["g_on"], r["edge"], -BIG, ALU.add, ALU.max))
                step(dve.memset(r["enter"], -BIG))
                step(dve.tensor_tensor(row["enter"][0:1, 1:P], row["run"][0:1, 0:P - 1], row["g_cont"][0:1, 1:P], ALU.add))
                to_col(row["enter"])
                step(dve.tensor_tensor_scan(f[:, :], gate[:, :], e[:, :], cols[:, 0:1], ALU.add, ALU.max))
                back_max(f, bk)
                dve.tensor_tensor(f[:, :], e[:, :], bk[:, :], ALU.subtract).then_inc(e1, 1)
                dve.wait_ge(e2, 1)
                step(dve.tensor_tensor_scan(f[:, :], same[:, :], w[:, :], 0.0, ALU.mult, ALU.add))
                to_row(row["edge"], f[:, ET - 1:ET])
                step(dve.tensor_tensor_scan(r["run"], r["on"], r["edge"], 0.0, ALU.mult, ALU.add))
                step(dve.memset(r["enter"], 0.0))
                step(dve.tensor_tensor(row["enter"][0:1, 1:P], row["run"][0:1, 0:P - 1], row["cont"][0:1, 1:P], ALU.mult))
                to_col(row["enter"])
                step(dve.tensor_tensor_scan(f[:, :], same[:, :], w[:, :], cols[:, 0:1], ALU.mult, ALU.add))
                back_max(f, bk)
                step(dve.reciprocal(f[:, :], bk[:, :]))
                step(dve.tensor_tensor(alpha[:, :], w[:, :], f[:, :], ALU.mult))

            @block.scalar
            def _(act):
                act.wait_ge(e1, 1)
                act.activation(w[:, :], f[:, :], ACT.Exp).then_inc(e2, 1)

            @block.tensor
            def _(pe):
                for n, kind in enumerate(jobs):
                    pe.wait_ge(rows_s, n + 1)
                    if kind == "row":
                        pe.transpose(bank[0][0:1, 0:P], cols[:, 0:1], ident[0:P, 0:P]).then_inc(cols_s, 1)
                    else:
                        pe.transpose(bank[1][0:P, 0:1], row["enter"][0:1, 0:P], ident[0:1, 0:1]).then_inc(cols_s, 1)


def scatter_by_source(nc, a, sem, sb, bank, agg0, h_dst, alpha, src_p):
    with ExitStack() as ctx:
        t_ = lambda name, shape, dt=F32: sb("b_" + name, shape, dt, ctx)
        key = t_("key", [P, ET])
        earlier = t_("earlier", [P, K, K, P])
        keyrow = [t_(f"keyrow{b}", [P, GC], I32) for b in range(2)]
        same = [t_(f"same{b}", [P, K, GC]) for b in range(2)]
        junk = t_("junk", [P, K, GC])
        cnt, pick, diff = ([t_(f"{n}{b}", [P, K]) for b in range(2)] for n in ("cnt", "pick", "diff"))
        spare = t_("spare", [P, K])
        idx = [t_(f"idx{b}", [P, K], I32) for b in range(2)]
        msg = [t_(f"msg{b}", [P, K, D]) for b in range(2)]
        tot = [t_(f"tot{b}", [P, K, D]) for b in range(2)]
        keys_in = [sem(f"b_keys_in{b}") for b in range(2)]
        made, step_s, msgs, summed, totals, indices, first = (
            sem("b_" + s) for s in ("made", "step", "msgs", "summed", "totals", "indices", "first"))
        added = sem("b_added", pool=True)
        passed = sem("passed")
        with nc.Block() as block:
            @block.sync
            def _(sp):
                def load_keys(j, b, i):
                    wait(sp, msgs, j - 1)
                    sp.dma_start(keyrow[b][:, :], a["src_p"][ds(j * K, K), :].rearrange("(o k) p -> o (k p)", o=1)
                                 .broadcast_to([P, GC])).then_inc(keys_in[b], 16)
                over(sp, EG, 2, 1, load_keys)

            @block.gpsimd
            def _(pool):
                pool.memset(earlier[:, :, :, :], 1.0).then_inc(made, 1)
                pool.wait_ge(made, 1)
                for k in range(K):
                    last = pool.affine_select(out=earlier[:, k, :, :], in_=earlier[:, k, :, :], compare_op=ALU.is_gt, fill=0.0,
                                              base=k * P, pattern=[[-P, K], [-1, P]], channel_multiplier=1)
                last.then_inc(made, 1)
                pool.iota(spare[:, :], pattern=[[P, K]], base=N, channel_multiplier=1,
                          allow_small_or_imprecise_dtypes=True).then_inc(made, 1)

                def scatter(j, b, i):
                    pool.wait_ge(indices, j + 1)
                    pool.sem_inc(passed, 1)
                    pool.wait_ge(totals, j + 1)
                    pool.sem_inc(passed, 1)
                    wait(pool, added, 64 * j)
                    pool.sem_inc(passed, 1)
                    for k in range(K):
                        pool.indirect_dma_start(
                            out=agg0[:, :], out_offset=bass.IndirectOffsetOnAxis(ap=idx[b][:, k:k + 1], axis=0),
                            in_=tot[b][:, k, :], in_offset=None, compute_op=ALU.add).then_inc(added, 16)
                over(pool, EG, 2, 1, scatter)
                pool.wait_ge(added, 64 * EG)

            @block.vector
            def _(dve):
                dve.tensor_copy(key[:, :], src_p[:, :]).then_inc(first, 1)
                dve.wait_ge(first, 1)
                dve.wait_ge(made, 3)

                def group(j, b, i):
                    step = Steps(dve, step_s, j * 4, passed)
                    wait(dve, summed, j - 1)
                    dve.wait_ge(keys_in[b], 16 * (i + 1))
                    for k in range(K):
                        t = j * K + k
                        dve.tensor_scalar(msg[b][:, k, :], h_dst[:, ds(t * D, D)], alpha[:, ds(t, 1)], None, ALU.mult)
                        last = dve.tensor_scalar(same[b][:, k, :], keyrow[b][:, :], key[:, ds(t, 1)], None, ALU.is_equal)
                    step(last)
                    dve.sem_inc(msgs, 1)
                    for k in range(K):
                        last = dve.scalar_tensor_tensor(junk[:, k, :], same[b][:, k, :], 1.0,
                                                        earlier[:, k, :, :].rearrange("p j q -> p (j q)"),
                                                        ALU.mult, ALU.mult, accum_out=cnt[b][:, k:k + 1])
                    step(last)
                    dve.tensor_scalar(pick[b][:, :], cnt[b][:, :], 0.5, None, ALU.is_lt)
                    step(dve.tensor_tensor(diff[b][:, :], key[:, ds(j * K, K)], spare[:, :], ALU.subtract))
                    step(dve.tensor_tensor(cnt[b][:, :], diff[b][:, :], pick[b][:, :], ALU.mult))
                    wait(dve, added, 64 * (j - 1))
                    dve.tensor_tensor(idx[b][:, :], cnt[b][:, :], spare[:, :], ALU.add).then_inc(indices, 1)
                over(dve, EG, 2, 1, group)

            @block.scalar
            def _(act):
                def sums_out(j, b, i):
                    act.wait_ge(summed, j + 1)
                    wait(act, added, 64 * (j - 1))
                    act.activation(tot[b][:, :, :].rearrange("p k d -> p (k d)"), bank[b][0:P, 0:K * D], ACT.Copy).then_inc(totals, 1)
                over(act, EG, 2, 1, sums_out)

            @block.tensor
            def _(pe):
                def sums(j, b, i):
                    pe.wait_ge(msgs, j + 1)
                    wait(pe, totals, j - 1)
                    for o in range(K):
                        for k in range(K):
                            last = pe.matmul(bank[b][0:P, o * D:(o + 1) * D], same[b][:, k, o * P:(o + 1) * P],
                                             msg[b][:, k, :], start=(k == 0), stop=(k == K - 1))
                    last.then_inc(summed, 1)
                over(pe, EG, 2, 1, sums)


def layer0_nodes(nc, a, sem, sb, bank, ident, agg0, x1, node_rows):
    with ExitStack() as ctx:
        t_ = lambda name, shape, dt=F32: sb("c_" + name, shape, dt, ctx)
        R = 6
        flat = lambda ap: ap[:, :, :].rearrange("p k d -> p (k d)")
        w = t_("w", [D, D])
        wi = t_("wi", [D, D])
        ag = [t_(f"ag{b}", [P, K, D]) for b in range(R)]
        x = [t_(f"x{b}", [P, K, D]) for b in range(R)]
        at = [t_(f"at{b}", [D, GC]) for b in range(2)]
        y = [t_(f"y{b}", [P, K, D]) for b in range(2)]
        z = [t_(f"z{b}", [P, K, D]) for b in range(R)]
        loaded = [sem(f"c_loaded{b}") for b in range(R)]
        stored = [sem(f"c_stored{b}") for b in range(R)]
        w_in, w_made, turned, turned_out, mm, act_done, sums = (
            sem("c_" + s) for s in ("w_in", "w_made", "turned", "turned_out", "mm", "act_done", "sums"))
        with nc.Block() as block:
            @block.sync
            def _(sp):
                sp.dma_start(w[:, :], a["L0_gnn_W"]).then_inc(w_in, 16)

                def load(g, b):
                    sp.dma_start(ag[b][:, :, :], node_rows(agg0, g)).then_inc(loaded[b], 16)
                    sp.dma_start(x[b][:, :, :], node_rows(a["x"], g)).then_inc(loaded[b], 16)

                def move(g, b, i):
                    sp.wait_ge(sums, g + 1)
                    sp.dma_start(node_rows(x1, g), z[b][:, :, :]).then_inc(stored[b], 16)
                    if there(g + R, NG):
                        load(g + R, b)

                for b in range(R):
                    load(b, b)
                over(sp, NG, R, R, move)
                for b in range(R):
                    sp.wait_ge(stored[b], 16 * (NG // R + (b < NG % R)))

            @block.tensor
            def _(pe):
                def turn(g, b, i):
                    pe.wait_ge(loaded[b], 32 * (i + 1))
                    for k in range(K):
                        last = pe.transpose(bank[b % 2][:, k * P:(k + 1) * P], ag[b][:, k, :], ident[0:P, 0:P])
                    last.then_inc(turned, 1)

                def product(g, b, i):
                    if there(g + 1, NG):
                        turn(g + 1, (b + 1) % R, i + (b + 1) // R)
                    pe.wait_ge(turned_out, g + 1)
                    wait(pe, act_done, g - 1)
                    for k in range(K):
                        last = pe.matmul(bank[2 + b % 2][0:P, k * D:(k + 1) * D], at[b % 2][:, k * P:(k + 1) * P], wi[:, :],
                                         start=True, stop=True)
                    last.then_inc(mm, 1)

                pe.wait_ge(w_made, 1)
                turn(0, 0, 0)
                over(pe, NG, R, 1, product)

            @block.vector
            def _(dve):
                dve.wait_ge(w_in, 16)
                dve.tensor_tensor(wi[:, :], w[:, :], ident[:, :], ALU.add).then_inc(w_made, 1)

                def evacuate(g, b, i):
                    dve.wait_ge(turned, g + 1)
                    wait(dve, mm, g - 1)
                    dve.tensor_copy(at[b % 2][:, :], bank[b % 2][:, 0:GC]).then_inc(turned_out, 1)
                over(dve, NG, R, 1, evacuate)

            @block.scalar
            def _(act):
                def gelu(g, b, i):
                    act.wait_ge(mm, g + 1)
                    wait(act, sums, g - 1)
                    act.activation(flat(y[b % 2]), bank[2 + b % 2][0:P, 0:K * D], ACT.Gelu).then_inc(act_done, 1)
                over(act, NG, R, 1, gelu)

            @block.gpsimd
            def _(pool):
                def add_rows(g, b, i):
                    pool.wait_ge(act_done, g + 1)
                    wait(pool, stored[b], 16 * i)
                    pool.tensor_tensor(z[b][:, :, :], y[b % 2][:, :, :], x[b][:, :, :], ALU.add).then_inc(sums, 1)
                over(pool, NG, R, 1, add_rows)


def edges(nc, a, sem, sb, bank, layer, ident, x, agg, src_t, key_t, prev_t, to_t, ew_t):
    with ExitStack() as ctx:
        nm = f"e{layer}_"
        t_ = lambda name, shape, dt=F32: sb(nm + name, shape, dt, ctx)
        R = 4
        four, two = range(R), range(2)
        xg = [t_(f"xg{b}", [P, K, D]) for b in four]
        from_i = [t_(f"from_i{b}", [P, K], I32) for b in four]
        to_i = [t_(f"to_i{b}", [P, K], I32) for b in two]
        keyrow = [t_(f"keyrow{b}", [P, GC], I32) for b in two]
        same = [t_(f"same{b}", [P, K, P]) for b in two]
        carry = [t_(f"carry{b}", [P, K, P]) for b in two]
        ln = [Stats(t_, f"ln{b}", K) for b in two]
        msg = [t_(f"msg{b}", [P, K, D + 1]) for b in two]
        run = [t_(f"run{b}", [P, K, D + 1]) for b in two]
        cnt = [t_(f"cnt{b}", [P, K]) for b in two]
        res = [t_(f"res{b}", [P, K, D]) for b in two]
        if layer == 1:
            h = [t_(f"h{b}", [P, K, D]) for b in two]
            ht = [t_(f"ht{b}", [D, GC]) for b in two]
            m = [t_(f"m{b}", [P, K, D]) for b in two]
            bias = t_("bias", [1, K * D])
            ones = t_("ones", [1, P])
        if layer != 3:
            w = t_("w", [D, D])
        if layer == 2:
            rt = [t_(f"rt{b}", [D, GC]) for b in two]
        gathered = [sem(f"{nm}gathered{b}", pool=True) for b in four]
        keys_in = [sem(f"{nm}keys_in{b}") for b in two]
        written = [sem(f"{nm}written{b}", pool=True) for b in two]
        passed = sem("passed")
        ready, from_set, to_set, step_s, stats, relued, matrices, run_mm, run_out, results = (
            sem(nm + s) for s in ("ready", "from_set", "to_set", "step", "stats", "relued", "matrices", "run_mm",
                                  "run_out", "results"))
        if layer != 3:
            consts, turned, turned_out, mm = (sem(nm + s) for s in ("consts", "turned", "turned_out", "mm"))
        if layer != 2:
            out_s = sem(nm + "out")
        if layer == 1:
            silued, msgs = sem(nm + "silued"), sem(nm + "msgs")
        run_at = lambda k: bank[4 + k % 2][0:P, 0:D + 1]
        flat = lambda ap: ap[:, :, :].rearrange("p k d -> p (k d)")
        with nc.Block() as block:
            @block.sync
            def _(sp):
                if layer == 1:
                    sp.dma_start(w[:, :], a["L1_gnn_agg_W"]).then_inc(consts, 16)
                    for k in range(K):
                        sp.dma_start(bias[:, k * D:(k + 1) * D], a["L1_gnn_agg_b"].rearrange("(o d) -> o d", o=1)).then_inc(consts, 16)
                if layer == 2:
                    sp.dma_start(w[:, :], a["w2t"]).then_inc(consts, 16)

                def load_keys(j, b, i):
                    wait(sp, matrices, j - 1)
                    sp.dma_start(keyrow[b][:, :], a["dst_rows"][ds(j * K, K), :].rearrange("(o k) p -> o (k p)", o=1)
                                 .broadcast_to([P, GC])).then_inc(keys_in[b], 16)
                over(sp, EG, 2, 1, load_keys)

            @block.gpsimd
            def _(pool):
                def gather(j, b):
                    wait(pool, relued, K * (j - R + 1))
                    pool.sem_inc(passed, 1)
                    pool.tensor_copy(from_i[b][:, :], src_t[:, ds(j * K, K)]).then_inc(from_set, 1)
                    pool.wait_ge(from_set, j + 1)
                    pool.sem_inc(passed, 1)
                    for k in range(K):
                        pool.indirect_dma_start(
                            out=xg[b][:, k, :], out_offset=None, in_=x[0:N, :],
                            in_offset=bass.IndirectOffsetOnAxis(ap=from_i[b][:, k:k + 1], axis=0)).then_inc(gathered[b], 16)

                def write(j, c):
                    pool.wait_ge(results, j + 1)
                    pool.sem_inc(passed, 1)
                    pool.tensor_copy(to_i[c][:, :], to_t[:, ds(j * K, K)]).then_inc(to_set, 1)
                    pool.wait_ge(to_set, j + 1)
                    pool.sem_inc(passed, 1)
                    for k in range(K):
                        to = bass.IndirectOffsetOnAxis(ap=to_i[c][:, k:k + 1], axis=0)
                        if layer == 2:
                            pool.indirect_dma_start(out=agg[:, :], out_offset=to, in_=res[c][:, k, :], in_offset=None,
                                                    compute_op=ALU.add).then_inc(written[c], 16)
                        else:
                            pool.indirect_dma_start(out=agg[:, :], out_offset=to, in_=res[c][:, k, :], in_offset=None,
                                                    bounds_check=N - 1, oob_is_err=False).then_inc(written[c], 16)

                def group(j, b, i):
                    if there(j + R, EG):
                        gather(j + R, b)
                    write(j, b % 2)

                for b in four:
                    gather(b, b)
                over(pool, EG, R, R, group)
                for c in two:
                    pool.wait_ge(written[c], 32 * EG)

            @block.vector
            def _(dve):
                for c in two:
                    dve.memset(msg[c][:, :, D:D + 1], 1.0)
                    dve.memset(run[c][:, :, :], 0.0)
                if layer == 1:
                    dve.memset(ones[:, :], 1.0)
                dve.memset(cnt[0][:, :], 0.0).then_inc(ready, 1)

                def normalize(j, b, i, between=()):
                    c = b % 2
                    step = Steps(dve, step_s, j * STATS, passed, between)
                    wait(dve, relued, K * (j - 1))
                    dve.wait_ge(gathered[b], 64 * (i + 1))
                    for k in range(K):
                        last = moments(dve, ln[c], k, xg[b][:, k, :])
                    step(roots(dve, step, ln[c], last, 0, K))
                    minus_mean_over_root(dve, ln[c], 0, K).then_inc(stats, 1)
                    step.rest()

                def compare(j, c):
                    def one(k, matrix, keys, last):
                        t = j * K + k
                        ins = dve.tensor_scalar(matrix[c][:, k, :], keyrow[c][:, k * P:(k + 1) * P], keys[:, ds(t, 1)], None, ALU.is_equal)
                        if last:
                            ins.then_inc(matrices, 1)
                    return [lambda k=k, m=m, y=y: one(k, m, y, k == K - 1 and m is carry)
                            for k in range(K) for m, y in ((same, key_t), (carry, prev_t))]

                def weigh(j, c):
                    dve.wait_ge(silued, j + 1)
                    for k in range(K):
                        last = dve.tensor_scalar(msg[c][:, k, 0:D], m[c][:, k, :], ew_t[:, ds(j * K + k, 1)], None, ALU.mult)
                    last.then_inc(msgs, 1)

                def means(j, c, half):
                    dve.wait_ge(run_out, K * (j + 1))
                    dve.tensor_scalar(cnt[c][:, :], run[c][:, :, D], 1.0, None, ALU.max).then_inc(out_s, 1)
                    dve.wait_ge(out_s, 2 * j + 1)
                    dve.reciprocal(cnt[c][:, :], cnt[c][:, :]).then_inc(out_s, 1)
                    dve.wait_ge(out_s, 2 * j + 2)
                    wait(dve, written[c], 64 * half)
                    for k in range(K):
                        last = dve.tensor_scalar(res[c][:, k, :], run[c][:, k, 0:D], cnt[c][:, k:k + 1], None, ALU.mult)
                    last.then_inc(results, 1)

                def group(j, b, i):
                    c = b % 2
                    half = 2 * i + b // 2
                    if layer == 1:
                        weigh(j, c)
                    if there(j + 1, EG):
                        dve.wait_ge(keys_in[1 - c], 16 * (2 * i + (b + 1) // 2 + 1))
                    if layer == 2:
                        wait(dve, run_mm, K * j)
                    if there(j + 2, EG):
                        normalize(j + 2, (b + 2) % R, i + (b + 2) // R, compare(j + 1, 1 - c))
                    elif there(j + 1, EG):
                        for emit in compare(j + 1, 1 - c):
                            emit()
                    if layer != 2:
                        means(j, c, half)

                normalize(0, 0, 0)
                dve.wait_ge(keys_in[0], 16)
                normalize(1, 1, 0, compare(0, 0))
                over(dve, EG, R, R, group)

            @block.scalar
            def _(act):
                act.wait_ge(ready, 1)

                def relu(j, b):
                    c = b % 2
                    act.wait_ge(stats, j + 1)
                    for k in range(K):
                        act.activation(h[c][:, k, :] if layer == 1 else msg[c][:, k, 0:D], xg[b][:, k, :], ACT.Relu,
                                       bias=ln[c].nmr[:, k:k + 1], scale=ln[c].rstd[:, k:k + 1]).then_inc(relued, 1)

                def evacuate(j, c):
                    act.wait_ge(turned, j + 1)
                    act.activation(ht[c][:, :], bank[c][:, 0:GC], ACT.Copy).then_inc(turned_out, 1)

                def silu(j, c):
                    act.wait_ge(mm, j + 1)
                    act.activation(flat(m[c]), bank[2 + c][0:P, 0:K * D], ACT.Silu).then_inc(silued, 1)

                def runs_out(j, c):
                    for k in range(K):
                        act.wait_ge(run_mm, K * j + k + 1)
                        act.activation(run[c][:, k, :], run_at(k), ACT.Copy).then_inc(run_out, 1)

                def products(j, c, half):
                    act.wait_ge(turned, j + 1)
                    act.activation(rt[c][:, :], bank[6][:, 0:GC], ACT.Copy).then_inc(turned_out, 1)
                    wait(act, written[c], 64 * half)
                    act.wait_ge(mm, j + 1)
                    act.activation(flat(res[c]), bank[7][0:P, 0:K * D], ACT.Copy).then_inc(results, 1)

                def group(j, b, i):
                    c = b % 2
                    if there(j + 1, EG):
                        relu(j + 1, (b + 1) % R)
                    runs_out(j, c)
                    if layer == 1 and there(j + 1, EG):
                        evacuate(j + 1, 1 - c)
                        silu(j + 1, 1 - c)
                    if layer == 2:
                        products(j, c, 2 * i + b // 2)

                relu(0, 0)
                if layer == 1:
                    evacuate(0, 0)
                    silu(0, 0)
                over(act, EG, R, R, group)

            @block.tensor
            def _(pe):
                pe.wait_ge(ready, 1)
                if layer != 3:
                    pe.wait_ge(consts, 16 * (1 + K) if layer == 1 else 16)

                def turn(j, c):
                    pe.wait_ge(relued, K * (j + 1))
                    for k in range(K):
                        last = pe.transpose(bank[c][:, k * P:(k + 1) * P], h[c][:, k, :], ident[0:P, 0:P])
                    last.then_inc(turned, 1)

                def linear(j, c):
                    pe.matmul(bank[2 + c][0:P, 0:K * D], ones[:, :], bias[:, :], start=True, stop=False)
                    pe.wait_ge(turned_out, j + 1)
                    for k in range(K):
                        last = pe.matmul(bank[2 + c][0:P, k * D:(k + 1) * D], ht[c][:, k * P:(k + 1) * P], w[:, :],
                                         start=False, stop=(k == K - 1))
                    last.then_inc(mm, 1)

                def sum_runs(j, c):
                    pe.wait_ge(matrices, j + 1)
                    if layer == 1:
                        pe.wait_ge(msgs, j + 1)
                    else:
                        pe.wait_ge(relued, K * (j + 1))
                    for k in range(K):
                        pe.matmul(run_at(k), same[c][:, k, :], msg[c][:, k, :], start=True, stop=False)
                        before = run[c][:, k - 1, :] if k else run[1 - c][:, K - 1, :]
                        wait(pe, run_out, K * j + k)
                        pe.matmul(run_at(k), carry[c][:, k, :], before, start=False, stop=True).then_inc(run_mm, 1)

                def times_w(j, c):
                    pe.wait_ge(run_out, K * (j + 1))
                    wait(pe, results, j)
                    for k in range(K):
                        last = pe.transpose(bank[6][:, k * P:(k + 1) * P], run[c][:, k, 0:D], ident[0:P, 0:P])
                    last.then_inc(turned, 1)
                    pe.wait_ge(turned_out, j + 1)
                    for k in range(K):
                        last = pe.matmul(bank[7][0:P, k * D:(k + 1) * D], rt[c][:, k * P:(k + 1) * P], w[:, :],
                                         start=True, stop=True)
                    last.then_inc(mm, 1)

                def group(j, b, i):
                    c = b % 2
                    if layer == 1 and there(j + 1, EG):
                        turn(j + 1, 1 - c)
                    sum_runs(j, c)
                    if layer == 2:
                        times_w(j, c)
                    if layer == 1 and there(j + 1, EG):
                        linear(j + 1, 1 - c)

                if layer == 1:
                    turn(0, 0)
                    linear(0, 0)
                over(pe, EG, R, R, group)


def bias_parts(dve, step, made, row, part, split, ones):
    dve.memset(ones[:, :], 0.0)
    step(dve.memset(split[:, :], 0.0))
    for p in (0, 32, 64):
        dve.memset(ones[p:p + 1, :], 1.0)
    for p in (0, 32, 64):
        step(dve.tensor_copy(split[p:p + 1, :], row[p:p + 1, :]))
    for p in (32, 64):
        step(dve.tensor_tensor(part[p:p + 1, :], row[p:p + 1, :], split[p:p + 1, :], ALU.subtract))
        step(dve.tensor_copy(split[p:p + 1, :], part[p:p + 1, :]))
    step(dve.tensor_tensor(part[64:65, :], part[64:65, :], split[64:65, :], ALU.subtract))
    dve.tensor_copy(split[64:65, :], part[64:65, :]).then_inc(made, 1)


def layer1_nodes(nc, a, sem, sb, bank, ident, x1, agg1, x2, x3, node_rows):
    with ExitStack() as ctx:
        t_ = lambda name, shape, dt=F32: sb("d_" + name, shape, dt, ctx)
        R = 10
        ring, two = range(R), range(2)
        wh, wa, w2, wr = (t_(n, [D, D]) for n in ("wh", "wa", "w2", "wr"))
        b1 = t_("b1", [D, 1])
        gain, shift = t_("gain", [P, K, D]), t_("shift", [P, K, D])
        b2 = t_("b2", [65, K * D])
        part = t_("part", [65, K * D])
        b2s = t_("b2s", [65, K * D], BF16)
        ones = t_("ones", [65, P], BF16)
        x = [t_(f"x{b}", [P, K, D]) for b in ring]
        ag = [t_(f"ag{b}", [P, K, D]) for b in ring]
        z = [t_(f"z{b}", [P, K, D]) for b in ring]
        h, yn = ([t_(f"{n}{b}", [P, K, D]) for b in two] for n in ("h", "yn"))
        ht, at, ut = ([t_(f"{n}{b}", [D, GC]) for b in two] for n in ("ht", "at", "ut"))
        early = [Stats(t_, f"early{b}", 2 * K) for b in two]
        ln = [Stats(t_, f"ln{b}", 2 * K) for b in two]
        loaded, stored = ([sem(f"d_{s}{b}") for b in ring] for s in ("loaded", "stored"))
        consts, made, made_s, first_s, step_s, normed, turned, evac, mm, silued, mo, stats, onormed, sums = (
            sem("d_" + s) for s in ("consts", "made", "made_s", "first_s", "step_s", "normed", "turned", "evac",
                                    "mm", "silued", "mo", "stats", "onormed", "sums"))
        passed = sem("passed")
        flat = lambda ap: ap.rearrange("p k d -> p (k d)")
        with nc.Block() as block:
            @block.sync
            def _(sp):
                row = lambda n: a[n].rearrange("(o d) -> o d", o=1)
                sp.dma_start(wh[:, :], a["L1_gnn_upd_W1"][0:D, :]).then_inc(consts, 16)
                sp.dma_start(wa[:, :], a["L1_gnn_upd_W1"][D:2 * D, :]).then_inc(consts, 16)
                sp.dma_start(w2[:, :], a["L1_gnn_upd_W2"]).then_inc(consts, 16)
                sp.dma_start(wr[:, :], a["L1_gnn_res_W"]).then_inc(consts, 16)
                sp.dma_start(b1[:, :], a["L1_gnn_upd_b1"].rearrange("(d o) -> d o", o=1)).then_inc(consts, 16)
                for k in range(K):
                    sp.dma_start(gain[:, k, :], row("L1_gnn_ln_g").broadcast_to([P, D])).then_inc(consts, 16)
                    sp.dma_start(shift[:, k, :], row("L1_gnn_ln_b").broadcast_to([P, D])).then_inc(consts, 16)
                    sp.dma_start(b2[:, k * D:(k + 1) * D], row("L1_gnn_upd_b2").broadcast_to([65, D])).then_inc(consts, 16)

                def load(g, b):
                    sp.dma_start(x[b][:, :, :], node_rows(x1, g)).then_inc(loaded[b], 16)
                    sp.dma_start(ag[b][:, :, :], node_rows(agg1, g)).then_inc(loaded[b], 16)

                def move(g, b, i):
                    sp.wait_ge(sums, 3 * (g + 1))
                    sp.dma_start(node_rows(x2, g), z[b][:, :, :]).then_inc(stored[b], 16)
                    sp.dma_start(node_rows(x3, g), z[b][:, :, :]).then_inc(stored[b], 16)
                    if there(g + R, NG):
                        load(g + R, b)

                for b in ring:
                    load(b, b)
                over(sp, NG, R, R, move)
                for b in ring:
                    sp.wait_ge(stored[b], 32 * (NG // R + (b < NG % R)))

            @block.vector
            def _(dve):
                dve.wait_ge(consts, 16 * (5 + 3 * K))
                step = Steps(dve, made_s, 0, None)
                bias_parts(dve, step, made, b2, part, b2s, ones)


                def x_moments(g, b, s):
                    return [lambda k=k: moments(dve, s, k, x[b][:, k, :]) for k in range(K)]

                def group(g, b, i):
                    c = b % 2
                    lo, between = (0 if there(g + 5, NG) else K), []
                    if there(g + 6, NG):
                        dve.wait_ge(loaded[(b + 6) % R], 32 * (i + (b + 6) // R + 1))
                        between = x_moments(g + 6, (b + 6) % R, ln[1 - c])
                    step = Steps(dve, step_s, g * STATS, passed, between)
                    wait(dve, normed, g + 4 if there(g + 3, NG) else NG)
                    dve.wait_ge(mo, g + 1)
                    for k in range(K):
                        last = moments(dve, ln[c], K + k, bank[6 + c][0:P, k * D:(k + 1) * D])
                    step(roots(dve, step, ln[c], last, lo, 2 * K))
                    minus_mean_over_root(dve, ln[c], lo, 2 * K).then_inc(stats, 1)
                    step.rest()

                for g in range(6):
                    dve.wait_ge(loaded[g], 32)
                for g in range(4):
                    for k in range(K):
                        last = moments(dve, early[g // 2], g % 2 * K + k, x[g][:, k, :])
                fifth, sixth = x_moments(4, 4, ln[1]), x_moments(5, 5, ln[0])
                for n, (s, between) in enumerate(((early[0], fifth[:-1]), (early[1], sixth[:-2]), (ln[1], sixth[-1:]))):
                    step = Steps(dve, first_s, n * STATS, passed, between)
                    step(roots(dve, step, s, last, 0, s.n if n < 2 else K))
                    minus_mean_over_root(dve, s, 0, s.n if n < 2 else K).then_inc(stats, 1)
                    step.rest()
                    last = (fifth[-1], sixth[-2], lambda: None)[n]()
                over(dve, NG, R, 6, group)

            @block.scalar
            def _(act):
                def normalize(g, b):
                    s, lo = (early[g // 2], g % 2 * K) if isinstance(g, int) and g < 4 else (ln[1 - b % 2], 0)
                    act.wait_ge(stats, max(g - 1, 1 + g // 2) if isinstance(g, int) else g - 1)
                    wait(act, turned, g - 1)
                    for k in range(K):
                        last = act.activation(h[b % 2][:, k, :], x[b][:, k, :], ACT.Relu,
                                              bias=s.nmr[:, lo + k:lo + k + 1], scale=s.rstd[:, lo + k:lo + k + 1])
                    last.then_inc(normed, 1)

                def evacuate(g, b):
                    c = b % 2
                    act.wait_ge(turned, g + 1)
                    wait(act, mo, g - 1)
                    act.activation(ht[c][:, :], bank[c][:, 0:GC], ACT.Copy)
                    act.activation(at[c][:, :], bank[2 + c][:, 0:GC], ACT.Copy).then_inc(evac, 1)

                def silu(g, b):
                    c = b % 2
                    act.wait_ge(mm, g + 1)
                    act.activation(ut[c][:, :], bank[4 + c][:, 0:GC], ACT.Silu, bias=b1[:, 0:1]).then_inc(silued, 1)

                def out_normalize(g, b):
                    c = b % 2
                    act.wait_ge(stats, g + 4)
                    wait(act, sums, 3 * (g - 1))
                    for k in range(K):
                        last = act.activation(yn[c][:, k, :], bank[6 + c][0:P, k * D:(k + 1) * D], ACT.Identity,
                                              bias=ln[c].nmr[:, K + k:K + k + 1], scale=ln[c].rstd[:, K + k:K + k + 1])
                    last.then_inc(onormed, 1)

                def group(g, b, i):
                    silu(g, b)
                    if there(g + 1, NG):
                        evacuate(g + 1, (b + 1) % R)
                    if there(g + 2, NG):
                        normalize(g + 2, (b + 2) % R)
                    if there(g - 2, NG):
                        out_normalize(g - 2, (b - 2) % R)

                act.wait_ge(consts, 16 * (5 + 3 * K))
                for g in two:
                    normalize(g, g)
                evacuate(0, 0)
                over(act, NG, R, 2, group)
                for g in (NG - 2, NG - 1):
                    out_normalize(g, g % R)

            @block.gpsimd
            def _(pool):
                pool.wait_ge(consts, 16 * (5 + 3 * K))

                def finish(g, b, i):
                    c = b % 2
                    pool.wait_ge(onormed, g + 1)
                    pool.tensor_tensor(yn[c][:, :, :], yn[c][:, :, :], gain[:, :, :], ALU.mult).then_inc(sums, 1)
                    wait(pool, stored[b], 32 * i)
                    pool.tensor_tensor(z[b][:, :, :], x[b][:, :, :], shift[:, :, :], ALU.add).then_inc(sums, 1)
                    pool.wait_ge(sums, 3 * g + 2)
                    pool.tensor_tensor(z[b][:, :, :], z[b][:, :, :], yn[c][:, :, :], ALU.add).then_inc(sums, 1)
                over(pool, NG, R, 2, finish)

            @block.tensor
            def _(pe):
                pe.wait_ge(consts, 16 * (5 + 3 * K))
                pe.wait_ge(made, 1)

                def turn(g, b):
                    c = b % 2
                    pe.wait_ge(normed, g + 1)
                    for k in range(K):
                        pe.transpose(bank[c][:, k * P:(k + 1) * P], h[c][:, k, :], ident[0:P, 0:P])
                    for k in range(K):
                        last = pe.transpose(bank[2 + c][:, k * P:(k + 1) * P], ag[b][:, k, :], ident[0:P, 0:P])
                    last.then_inc(turned, 1)

                def hidden(g, b):
                    c = b % 2
                    pe.wait_ge(evac, g + 1)
                    pe.matmul(bank[4 + c][:, 0:GC], wh[:, :], ht[c][:, :], start=True, stop=False)
                    pe.matmul(bank[4 + c][:, 0:GC], wa[:, :], at[c][:, :], start=False, stop=True).then_inc(mm, 1)

                def outer(g, b):
                    c = b % 2
                    o = bank[6 + c]
                    wait(pe, onormed, g - 1)
                    pe.matmul(o[0:P, 0:K * D], ones[:, :], b2s[:, :], start=True, stop=False)
                    for k in range(K):
                        pe.matmul(o[0:P, k * D:(k + 1) * D], ht[c][:, k * P:(k + 1) * P], wr[:, :], start=False, stop=False)
                    pe.wait_ge(silued, g + 1)
                    for k in range(K):
                        last = pe.matmul(o[0:P, k * D:(k + 1) * D], ut[c][:, k * P:(k + 1) * P], w2[:, :],
                                         start=False, stop=(k == K - 1))
                    last.then_inc(mo, 1)

                def group(g, b, i):
                    hidden(g, b)
                    if there(g + 1, NG):
                        turn(g + 1, (b + 1) % R)
                    if there(g - 1, NG):
                        outer(g - 1, (b - 1) % R)

                turn(0, 0)
                over(pe, NG, R, 2, group)
                outer(NG - 1, (NG - 1) % R)


def layer3_nodes(nc, a, sem, sb, bank, ident, x3, agg3, out, node_rows):
    with ExitStack() as ctx:
        t_ = lambda name, shape, dt=F32: sb("f_" + name, shape, dt, ctx)
        R = 8
        ring, two = range(R), range(2)
        w1 = t_("w1", [D, 2 * D])
        w2 = t_("w2", [D, 2, D])
        b1 = t_("b1", [D, 2])
        eps1 = t_("eps1", [P, 1])
        b2 = t_("b2", [65, K * D])
        part = t_("part", [65, K * D])
        b2s = t_("b2s", [65, K * D], BF16)
        ones = t_("ones", [65, P], BF16)
        x = [t_(f"x{b}", [P, K, D]) for b in ring]
        ag = [t_(f"ag{b}", [P, K, D]) for b in ring]
        z = [t_(f"z{b}", [P, K, D]) for b in ring]
        h, rn = ([t_(f"{n}{b}", [P, K, D]) for b in two] for n in ("h", "rn"))
        rt, ut, vt = ([t_(f"{n}{b}", [D, GC]) for b in two] for n in ("rt", "ut", "vt"))
        ln = [Stats(t_, f"ln{b}", K) for b in two]
        loaded, stored = ([sem(f"f_{s}{b}") for b in ring] for s in ("loaded", "stored"))
        consts, made, made_s, step_s, stats, hs, normed, turned, rst, mm, relued2, mo, results, sums = (
            sem("f_" + s) for s in ("consts", "made", "made_s", "step_s", "stats", "hs", "normed", "turned", "rst",
                                    "mm", "relued2", "mo", "results", "sums"))
        flat = lambda t: t[:, :, :].rearrange("p k d -> p (k d)")
        passed = sem("passed")
        n_consts = 16 * (4 + K + 1)
        with nc.Block() as block:
            @block.sync
            def _(sp):
                sp.dma_start(w1[:, :], a["L3_gnn_W1"]).then_inc(consts, 16)
                sp.dma_start(w2[:, :, :], a["L3_gnn_W2"].rearrange("(h q) d -> q h d", h=2)).then_inc(consts, 16)
                for h in two:
                    sp.dma_start(b1[:, h:h + 1], a["L3_gnn_b1"][h * D:(h + 1) * D].rearrange("(q o) -> q o", o=1)).then_inc(consts, 16)
                sp.dma_start(eps1[:, :], a["L3_gnn_eps"].rearrange("(o d) -> o d", o=1).broadcast_to([P, 1])).then_inc(consts, 16)
                for k in range(K):
                    sp.dma_start(b2[:, k * D:(k + 1) * D], a["L3_gnn_b2"].rearrange("(o d) -> o d", o=1).broadcast_to([65, D])).then_inc(consts, 16)

                def load(g, b):
                    sp.dma_start(x[b][:, :, :], node_rows(x3, g)).then_inc(loaded[b], 16)
                    sp.dma_start(ag[b][:, :, :], node_rows(agg3, g)).then_inc(loaded[b], 16)

                def move(g, b, i):
                    sp.wait_ge(sums, g + 1)
                    sp.dma_start(node_rows(out, g), z[b][:, :, :]).then_inc(stored[b], 16)
                    if there(g + R, NG):
                        load(g + R, b)

                for b in ring:
                    load(b, b)
                over(sp, NG, R, R, move)
                for b in ring:
                    sp.wait_ge(stored[b], 16 * (NG // R + (b < NG % R)))

            @block.vector
            def _(dve):
                dve.wait_ge(consts, n_consts)
                step = Steps(dve, made_s, 0, None)
                step(dve.tensor_scalar(eps1[:, :], eps1[:, :], 1.0, None, ALU.add))
                bias_parts(dve, step, made, b2, part, b2s, ones)


                def x_moments(g, b, s):
                    return [lambda k=k: moments(dve, s, k, x[b][:, k, :]) for k in range(K)]

                def combine(g, b):
                    dve.wait_ge(hs, g + 1)
                    wait(dve, turned, g - 1)
                    dve.scalar_tensor_tensor(flat(rn[b % 2]), flat(h[b % 2]), eps1[:, 0:1], flat(ag[b]),
                                             ALU.mult, ALU.add).then_inc(normed, 1)

                def statistics(g, s, last, between):
                    step = Steps(dve, step_s, g * STATS, passed, between)
                    step(roots(dve, step, s, last, 0, K))
                    minus_mean_over_root(dve, s, 0, K).then_inc(stats, 1)
                    step.rest()

                def group(g, b, i):
                    s, between = ln[1 - b % 2], []
                    if there(g + 4, NG):
                        dve.wait_ge(loaded[(b + 4) % R], 32 * (i + (b + 4) // R + 1))
                        between = x_moments(g + 4, (b + 4) % R, ln[b % 2])[1:]
                    if there(g + 3, NG):
                        statistics(g + 3, s, x_moments(g + 3, (b + 3) % R, s)[0](), between)
                    if there(g + 2, NG):
                        combine(g + 2, (b + 2) % R)

                for g in range(4):
                    dve.wait_ge(loaded[g], 32)
                for emit in x_moments(0, 0, ln[0]):
                    emit()
                second, third, fourth = (x_moments(g, g, ln[g % 2]) for g in (1, 2, 3))
                for emit in second[1:]:
                    emit()
                statistics(0, ln[0], second[0](), [])
                statistics(1, ln[1], third[0](), third[1:])
                combine(0, 0)
                statistics(2, ln[0], fourth[1](), fourth[2:])
                combine(1, 1)
                over(dve, NG, R, 4, group)

            @block.scalar
            def _(act):
                act.wait_ge(consts, n_consts)

                def normalize(g, b):
                    s = ln[b % 2]
                    act.wait_ge(stats, g + 1)
                    wait(act, normed, g - 1)
                    for k in range(K):
                        last = act.activation(h[b % 2][:, k, :], x[b][:, k, :], ACT.Relu,
                                              bias=s.nmr[:, k:k + 1], scale=s.rstd[:, k:k + 1])
                    last.then_inc(hs, 1)

                def evacuate(g, b):
                    c = b % 2
                    act.wait_ge(turned, g + 1)
                    wait(act, mm, g - 1)
                    act.activation(rt[c][:, :], bank[c][:, 0:GC], ACT.Copy).then_inc(rst, 1)

                def relu(g, b):
                    c = b % 2
                    act.wait_ge(mm, g + 1)
                    wait(act, mo, g - 1)
                    act.activation(ut[c][:, :], bank[2 + 2 * c][:, 0:GC], ACT.Relu, bias=b1[:, 0:1])
                    act.activation(vt[c][:, :], bank[3 + 2 * c][:, 0:GC], ACT.Relu, bias=b1[:, 1:2]).then_inc(relued2, 1)

                def result(g, b, i):
                    act.wait_ge(mo, g + 1)
                    wait(act, stored[b], 16 * i)
                    act.activation(flat(z[b]), bank[6 + b % 2][0:P, 0:K * D], ACT.Relu).then_inc(results, 1)

                def group(g, b, i):
                    relu(g, b)
                    if there(g + 1, NG):
                        evacuate(g + 1, (b + 1) % R)
                    if there(g - 1, NG):
                        result(g - 1, (b - 1) % R, i if b else i - 1)
                    if there(g + 3, NG):
                        normalize(g + 3, (b + 3) % R)

                for g in range(3):
                    normalize(g, g)
                evacuate(0, 0)
                over(act, NG, R, 3, group)
                result(NG - 1, (NG - 1) % R, (NG - 1) // R)

            @block.gpsimd
            def _(pool):
                def add_rows(g, b, i):
                    pool.wait_ge(results, g + 1)
                    pool.tensor_tensor(flat(z[b]), flat(z[b]), flat(x[b]), ALU.add).then_inc(sums, 1)
                over(pool, NG, R, 2, add_rows)

            @block.tensor
            def _(pe):
                pe.wait_ge(consts, n_consts)
                pe.wait_ge(made, 1)

                def turn(g, b):
                    c = b % 2
                    pe.wait_ge(normed, g + 1)
                    for k in range(K):
                        last = pe.transpose(bank[c][:, k * P:(k + 1) * P], rn[c][:, k, :], ident[0:P, 0:P])
                    last.then_inc(turned, 1)

                def hidden(g, b):
                    c = b % 2
                    pe.wait_ge(rst, g + 1)
                    wait(pe, relued2, g - 1)
                    pe.matmul(bank[2 + 2 * c][:, 0:GC], w1[:, 0:D], rt[c][:, :], start=True, stop=True)
                    pe.matmul(bank[3 + 2 * c][:, 0:GC], w1[:, D:2 * D], rt[c][:, :], start=True, stop=True).then_inc(mm, 1)

                def outer(g, b):
                    c = b % 2
                    o = bank[6 + c]
                    wait(pe, results, g - 1)
                    pe.matmul(o[0:P, 0:K * D], ones[:, :], b2s[:, :], start=True, stop=False)
                    pe.wait_ge(relued2, g + 1)
                    for k in range(K):
                        pe.matmul(o[0:P, k * D:(k + 1) * D], ut[c][:, k * P:(k + 1) * P], w2[:, 0, :], start=False, stop=False)
                    for k in range(K):
                        last = pe.matmul(o[0:P, k * D:(k + 1) * D], vt[c][:, k * P:(k + 1) * P], w2[:, 1, :],
                                         start=False, stop=(k == K - 1))
                    last.then_inc(mo, 1)

                def group(g, b, i):
                    hidden(g, b)
                    if there(g + 1, NG):
                        turn(g + 1, (b + 1) % R)
                    if there(g - 1, NG):
                        outer(g - 1, (b - 1) % R)

                turn(0, 0)
                over(pe, NG, R, 2, group)
                outer(NG - 1, (NG - 1) % R)


_INS = ['x', 'src', 'dst', 'L0_gnn_a_i', 'L0_gnn_a_j', 'L0_gnn_W', 'L1_gnn_agg_W', 'L1_gnn_agg_b', 'L1_gnn_edge_W1',
        'L1_gnn_edge_b1', 'L1_gnn_edge_W2', 'L1_gnn_edge_b2', 'L1_gnn_upd_W1', 'L1_gnn_upd_b1', 'L1_gnn_upd_W2',
        'L1_gnn_upd_b2', 'L1_gnn_ln_g', 'L1_gnn_ln_b', 'L1_gnn_res_W', 'L2_gnn_W', 'L3_gnn_eps', 'L3_gnn_W1',
        'L3_gnn_b1', 'L3_gnn_W2', 'L3_gnn_b2']


def kernel(**inputs):
    import numpy as _np
    import concourse.bacc as _bacc
    from concourse import mybir as _mybir
    from concourse.bass_utils import run_bass_kernel_spmd as _run

    nc = _bacc.Bacc("TRN2", target_bir_lowering=False, num_devices=1)
    laid = {name: _np.ascontiguousarray(inputs[name]) for name in _INS}
    src, dst = laid['src'], laid['dst']
    laid['src_t'] = _np.ascontiguousarray(src.reshape(ET, P).T)
    laid['dst_t'] = _np.ascontiguousarray(dst.reshape(ET, P).T)
    laid['dst_rows'] = _np.ascontiguousarray(dst.reshape(ET, P))
    laid['src_p'] = _np.ascontiguousarray(src.reshape(P, ET).T)
    laid['attr'] = _np.ascontiguousarray(_np.asarray(inputs['edge_attr_4']).T)
    laid['w2t'] = _np.ascontiguousarray(_np.asarray(inputs['L2_gnn_W']).T)
    arrays, aps = {}, {}
    for name, v in laid.items():
        arrays[f"in_{name}"] = v
        aps[name] = nc.dram_tensor(f"in_{name}", v.shape, _mybir.dt.from_np(v.dtype), kind="ExternalInput").ap()
    out = nc.dram_tensor("out_x", (N, D), F32, kind="ExternalOutput").ap()
    program(nc, aps, out)
    r = _run(nc, [arrays], core_ids=[0])
    return r.results[0]["out_x"]
```

```python
from contextlib import ExitStack, contextmanager

import concourse.bass as bass
from concourse import mybir

F32 = mybir.dt.float32
BF16 = mybir.dt.bfloat16
I32 = mybir.dt.int32
ALU = mybir.AluOpType
ACT = mybir.ActivationFunctionType

N = 50000
E = 25000
D = 128
P = 125
ET = E // P
K = 4
EG = ET // K
NG = N // (P * K)
GC = P * K
EPS = 1e-5
BIG = 1e38
W = 3
DUMP = W * K * P
SKIP = 1 << 24
FILL = 16


def ds(start, size):
    return bass.ds(start, size)


class Steps:

    def __init__(self, eng, sem, base, passed, between=()):
        self.eng, self.sem, self.value, self.passed, self.between = eng, sem, base, passed, list(between)

    def __call__(self, ins):
        ins.then_inc(self.sem, 1)
        self.value = self.value + 1
        if self.between:
            self.between.pop(0)()
        self.eng.wait_ge(self.sem, self.value)

    def rest(self):
        for emit in self.between:
            emit()


STATS = 14
MAGIC = 0x5F3759DF


class Stats:

    def __init__(self, t_, name, n):
        self.n = n
        self.st, self.mv = t_(name + "_st", [P, n, 6]), t_(name + "_mv", [P, n, 2])
        self.v, self.a, self.y, self.nmr = (t_(f"{name}_{s}", [P, n]) for s in ("v", "a", "y", "nmr"))
        self.mean, self.rstd = self.mv[:, :, 0], self.y


def moments(dve, s, k, rows):
    return dve.bn_stats(s.st[:, k, :], rows)


def roots(dve, step, s, last, lo, hi):
    step(last)
    dve.sem_inc(step.passed, 1)
    for k in range(lo, hi):
        last = dve.bn_aggr(s.mv[:, k, :], s.st[:, k, :])
    step(last)
    v, a, y = (x[:, lo:hi] for x in (s.v, s.a, s.y))
    step(dve.tensor_scalar(v, s.mv[:, lo:hi, 1], EPS, None, ALU.add))
    step(dve.tensor_scalar(a.bitcast(I32), v.bitcast(I32), 1, None, ALU.logical_shift_right))
    step(dve.tensor_scalar(y.bitcast(I32), a.bitcast(I32), -1.0, float(MAGIC), ALU.mult, ALU.add))
    for n in range(3):
        step(dve.scalar_tensor_tensor(a, y, -0.5, y, ALU.mult, ALU.mult))
        step(dve.tensor_tensor(a, a, v, ALU.mult))
        last = dve.scalar_tensor_tensor(y, a, 1.5, y, ALU.add, ALU.mult)
        if n < 2:
            step(last)
    return last


def minus_mean_over_root(dve, s, lo, hi):
    return dve.scalar_tensor_tensor(s.nmr[:, lo:hi], s.mv[:, lo:hi, 0], -1.0, s.y[:, lo:hi], ALU.mult, ALU.mult)


def over(eng, n, unroll, ahead, body):
    loops = (n - ahead) // unroll
    for g in range(unroll):
        body(g, g, 0)
    with eng.Fori(1, loops) as i:
        for b in range(unroll):
            body(unroll * i + b, b, i)
    for g in range(unroll * loops, n):
        body(g, g % unroll, g // unroll)


def wait(eng, s, value):
    if not isinstance(value, int) or value > 0:
        eng.wait_ge(s, value)


def there(g, n):
    return not isinstance(g, int) or 0 <= g < n


def program(nc, a, out):
    with ExitStack() as whole:
        bank = [whole.enter_context(nc.psum_tensor(f"bank{i}", [128, 512], F32)) for i in range(8)]

        def sb(name, shape, dt=F32, ctx=whole):
            return ctx.enter_context(nc.sbuf_tensor(name, shape, dt))

        def dram(name, rows):
            return nc.dram_tensor(name, (rows, D), F32, kind="Internal").ap()

        agg0 = dram("agg0", N + DUMP)
        agg1 = dram("agg1", N)
        x1 = dram("x1", N)
        x2 = dram("x2", N)
        x3 = dram("x3", N + DUMP)
        means3 = dram("means3", E + 1)
        ends = nc.dram_tensor("ends", (N, 1), I32, kind="Internal").ap()

        ident = sb("ident", [128, 128])
        dst_t = sb("dst_t", [P, ET], I32)
        src_t = sb("src_t", [P, ET], I32)
        key_t = sb("key_t", [P, ET])
        prev_t = sb("prev_t", [P, ET])
        end_t = sb("end_t", [P, ET], I32)
        add_t = sb("add_t", [P, ET], I32)
        row_t = sb("row_t", [P, ET], I32)
        ends_t = sb("ends_t", [P, NG * K], I32)
        ew_t = sb("ew_t", [P, ET])

        node_rows = lambda ap, g: ap[ds(g * GC, GC), :].rearrange("(p k) d -> p k d", k=K)

        with semaphores(nc, whole) as sem:
            prepare(nc, a, sem, sb, bank, ident, dst_t, src_t, key_t, prev_t, end_t, add_t, row_t)
            with ExitStack() as ctx:
                esb = lambda name, shape, dt=F32: sb(name, shape, dt, ctx)
                h_dst = esb("h_dst", [P, ET * D])
                si = esb("si", [P, ET])
                sj = esb("sj", [P, ET])
                alpha = esb("alpha", [P, ET])
                src_p = esb("src_p", [P, ET], I32)
                dst_p = esb("dst_p", [P, ET], I32)
                edge_rows(nc, a, sem, sb, bank, agg0, agg1, x3, means3, ends, h_dst, si, sj, src_p, dst_p, ew_t)
                earlier = esb("earlier", [P, K, K, P])
                spare = esb("spare_rows", [P, K])
                softmax(nc, sem, sb, bank, ident, si, sj, dst_p, alpha, earlier, spare)
                scatter_by_source(nc, a, sem, sb, bank, agg0, h_dst, alpha, src_p, earlier, spare, end_t, row_t, ends)
            layer0_nodes(nc, a, sem, sb, bank, ident, agg0, x1, node_rows, end_t, row_t, ends)
        with semaphores(nc, whole) as sem:
            edges(nc, a, sem, sb, bank, 1, ident, x1, agg1, src_t, key_t, prev_t, end_t, ew_t)
            layer1_nodes(nc, a, sem, sb, bank, ident, x1, agg1, x2, x3, node_rows)
        with semaphores(nc, whole, last=True) as sem:
            edges(nc, a, sem, sb, bank, 2, ident, x2, x3, src_t, key_t, prev_t, add_t, ew_t)
            edges(nc, a, sem, sb, bank, 3, ident, x3, means3, src_t, key_t, prev_t, None, ew_t, ends, ends_t)
            layer3_nodes(nc, a, sem, sb, bank, ident, x3, means3, ends_t, out, node_rows)


@contextmanager
def semaphores(nc, whole, last=False):
    with ExitStack() as ctx:
        known, kept = {}, {}

        def sem(name, pool=False):
            mine = kept if pool else known
            if name not in mine:
                mine[name] = (whole if pool else ctx).enter_context(nc.semaphore(name))
            return mine[name]
        yield sem
        if last:
            return
        with nc.Block() as block:
            def clear(eng, part):
                for s in list(known.values())[part::5]:
                    eng.sem_clear(s)

            @block.sync
            def _(sp):
                clear(sp, 0)

            @block.gpsimd
            def _(pool):
                clear(pool, 1)

            @block.vector
            def _(dve):
                clear(dve, 2)

            @block.scalar
            def _(act):
                clear(act, 3)

            @block.tensor
            def _(pe):
                clear(pe, 4)


def prepare(nc, a, sem, sb, bank, ident, dst_t, src_t, key_t, prev_t, end_t, add_t, row_t):
    with ExitStack() as ctx:
        loaded, made, step_s = sem("p_loaded"), sem("p_made"), sem("p_step")
        nxt = sb("nxt", [P, ET], F32, ctx)
        nxt_i = sb("nxt_i", [P, ET], I32, ctx)
        prev_i = sb("prev_i", [P, ET], I32, ctx)
        spares = -(-ET // (W * K))
        spare = sb("spare", [P, spares * W * K], F32, ctx)
        isend = sb("isend", [P, ET], F32, ctx)
        tmp = sb("tmp", [P, ET], F32, ctx)
        with nc.Block() as block:
            @block.sync
            def _(sp):
                sp.dma_start(dst_t[:, :], a["dst_t"]).then_inc(loaded, 16)
                sp.dma_start(src_t[:, :], a["src_t"]).then_inc(loaded, 16)
                sp.dma_start(nxt_i[0:P - 1, :], a["dst_t"][1:P, :]).then_inc(loaded, 16)
                sp.dma_start(nxt_i[P - 1:P, 0:ET - 1], a["dst_t"][0:1, 1:ET]).then_inc(loaded, 16)
                sp.dma_start(nxt_i[P - 1:P, ET - 1:ET], a["dst_t"][P - 1:P, ET - 1:ET]).then_inc(loaded, 16)
                sp.dma_start(prev_i[:, 1:ET], a["dst_t"][P - 1:P, 0:ET - 1].broadcast_to([P, ET - 1])).then_inc(loaded, 16)

            @block.gpsimd
            def _(pool):
                pool.memset(ident[:, :], 0.0).then_inc(made, 1)
                pool.wait_ge(made, 1)
                pool.affine_select(out=ident[:, :], in_=ident[:, :], compare_op=ALU.not_equal, fill=1.0,
                                   base=0, pattern=[[-1, 128]], channel_multiplier=1).then_inc(made, 1)
                pool.iota(row_t[:, :], pattern=[[GC, EG], [1, K]], base=0, channel_multiplier=K)
                pool.iota(spare[:, :], pattern=[[0, spares], [P, W * K]], base=N,
                          channel_multiplier=1, allow_small_or_imprecise_dtypes=True).then_inc(made, 1)

            @block.vector
            def _(dve):
                step = Steps(dve, step_s, 0, None)
                dve.wait_ge(loaded, 96)
                step(dve.tensor_copy(key_t[:, :], dst_t[:, :]))
                step(dve.tensor_copy(nxt[:, :], nxt_i[:, :]))
                dve.tensor_copy(prev_t[:, 1:ET], prev_i[:, 1:ET])
                step(dve.memset(prev_t[:, 0:1], -1.0))
                dve.wait_ge(made, 3)
                step(dve.tensor_scalar(tmp[:, :], prev_t[:, :], 1.0, ident[0:P, P - 1:P], ALU.add, ALU.mult))
                step(dve.tensor_scalar(prev_t[:, :], tmp[:, :], 1.0, None, ALU.subtract))
                step(dve.tensor_tensor(isend[:, :], key_t[:, :], nxt[:, :], ALU.not_equal))
                step(dve.tensor_tensor(isend[:, ET - 1:ET], isend[:, ET - 1:ET], ident[0:P, P - 1:P], ALU.max))
                step(dve.scalar_tensor_tensor(tmp[:, :], key_t[:, :], float(SKIP), isend[:, :], ALU.subtract, ALU.mult))
                step(dve.tensor_scalar(end_t[:, :], tmp[:, :], float(SKIP), None, ALU.add))
                step(dve.tensor_tensor(tmp[:, :], key_t[:, :], spare[:, 0:ET], ALU.subtract))
                step(dve.tensor_tensor(nxt[:, :], tmp[:, :], isend[:, :], ALU.mult))
                step(dve.tensor_tensor(add_t[:, :], nxt[:, :], spare[:, 0:ET], ALU.add))


def edge_rows(nc, a, sem, sb, bank, agg0, agg1, x3, means3, ends, h_dst, si, sj, src_p, dst_p, ew_t):
    with ExitStack() as ctx:
        t_ = lambda name, shape, dt=F32: sb("a_" + name, shape, dt, ctx)
        zeros = t_("zeros", [P, FILL * D])
        none = t_("none", [P, N // P], I32)
        R = 4
        xg = [t_(f"xg{b}", [P, 2 * K, D]) for b in range(R)]
        hs = [t_(f"hs{b}", [P, K, D]) for b in range(2)]
        cur = [t_(f"cur{b}", [P, 2 * K], I32) for b in range(R)]
        ln = [Stats(t_, f"ln{b}", 2 * K) for b in range(2)]
        junk = t_("junk", [P, 2 * K, D])
        sc = [t_(f"sc{b}", [P, 2 * K]) for b in range(2)]
        ai = t_("ai", [P, D])
        aj = t_("aj", [P, D])
        w1 = t_("w1", [4, D])
        b1 = t_("b1", [D, 1])
        w2 = t_("w2", [D, 1])
        b2 = t_("b2", [P, 1])
        at = [t_(f"at{b}", [4, GC]) for b in range(2)]
        hid = [t_(f"hid{b}", [D, GC]) for b in range(2)]
        consts, zeroed, filled = sem("a_consts"), sem("a_zeroed"), sem("a_filled")
        gathered = [sem(f"a_gathered{b}", pool=True) for b in range(R)]
        attr = [sem(f"a_attr{b}") for b in range(2)]
        staged, stats, relued, dots, copied, step_s, hid_mm, hid_done, ew_mm = (
            sem("a_" + s) for s in ("staged", "stats", "relued", "dots", "copied", "step", "hid_mm", "hid_done", "ew_mm"))
        passed = sem("passed")
        fills = N // (P * FILL)
        assert fills * P * FILL == N and 2 * fills == EG
        with nc.Block() as block:
            @block.sync
            def _(sp):
                row = lambda n: a[n].rearrange("(o d) -> o d", o=1)
                sp.dma_start(src_p[:, :], a["src"].rearrange("(p t) -> p t", t=ET)).then_inc(consts, 16)
                sp.dma_start(dst_p[:, :], a["dst"].rearrange("(p t) -> p t", t=ET)).then_inc(consts, 16)
                sp.dma_start(ai[:, :], row("L0_gnn_a_i").broadcast_to([P, D])).then_inc(consts, 16)
                sp.dma_start(aj[:, :], row("L0_gnn_a_j").broadcast_to([P, D])).then_inc(consts, 16)
                sp.dma_start(w1[:, :], a["L1_gnn_edge_W1"]).then_inc(consts, 16)
                sp.dma_start(b1[:, :], a["L1_gnn_edge_b1"].rearrange("(d o) -> d o", o=1)).then_inc(consts, 16)
                sp.dma_start(w2[:, :], a["L1_gnn_edge_W2"]).then_inc(consts, 16)
                sp.dma_start(b2[:, :], row("L1_gnn_edge_b2").broadcast_to([P, 1])).then_inc(consts, 16)
                sp.wait_ge(zeroed, 1)
                sp.dma_start(means3[E:E + 1, :], zeros[0:1, 0:D]).then_inc(filled, 16)
                sp.dma_start(ends[:, :].rearrange("(p r) o -> p (r o)", p=P), none[:, :]).then_inc(filled, 16)
                for agg in (agg0, x3):
                    sp.dma_start(agg[N:N + DUMP, :].rearrange("(p r) d -> p (r d)", r=DUMP // P), zeros[:, 0:DUMP // P * D]).then_inc(filled, 16)

                def supply(j, b, i):
                    wait(sp, hid_mm, j - 1)
                    sp.dma_start(at[b][:, :], a["attr"][:, ds(j * GC, GC)]).then_inc(attr[b], 16)
                    agg = (agg0, agg1)[b]
                    sp.dma_start(agg[ds(i * P * FILL, P * FILL), :].rearrange("(p r) d -> p (r d)", r=FILL), zeros[:, :]).then_inc(filled, 16)
                over(sp, EG, 2, 1, supply)
                sp.wait_ge(filled, (2 * fills + 4) * 16)

            @block.gpsimd
            def _(pool):
                pool.iota(none[:, :], pattern=[[0, N // P]], base=E, channel_multiplier=0)
                pool.memset(zeros[:, :], 0.0).then_inc(zeroed, 1)
                pool.wait_ge(consts, 128)

                def gather(j, b, i):
                    wait(pool, relued, 2 * K * (j - R + 1))
                    pool.sem_inc(passed, 1)
                    pool.tensor_copy(cur[b][:, 0:K], dst_p[:, ds(j * K, K)]).then_inc(staged, 1)
                    pool.tensor_copy(cur[b][:, K:2 * K], src_p[:, ds(j * K, K)]).then_inc(staged, 1)
                    pool.wait_ge(staged, 2 * j + 2)
                    pool.sem_inc(passed, 1)
                    for k in range(2 * K):
                        pool.indirect_dma_start(
                            out=xg[b][:, k, :], out_offset=None, in_=a["x"][:, :],
                            in_offset=bass.IndirectOffsetOnAxis(ap=cur[b][:, k:k + 1], axis=0)).then_inc(gathered[b], 16)
                over(pool, EG, R, 1, gather)

            @block.vector
            def _(dve):
                dve.wait_ge(consts, 128)

                def dot(j, c):
                    def one(k, o, h, v):
                        ins = dve.scalar_tensor_tensor(junk[:, o + k, :], h, 1.0, v[:, :], ALU.mult, ALU.mult,
                                                       accum_out=sc[c][:, o + k:o + k + 1])
                        if o and k == K - 1:
                            ins.then_inc(dots, 1)
                    return ([lambda k=k: one(k, 0, h_dst[:, ds((j * K + k) * D, D)], ai) for k in range(K)]
                            + [lambda k=k: one(k, K, hs[c][:, k, :], aj) for k in range(K)])

                def scores(j, b, i, between=()):
                    c = b % 2
                    step = Steps(dve, step_s, j * STATS, passed, between)
                    dve.wait_ge(gathered[b], 128 * (i + 1))
                    for k in range(2 * K):
                        last = moments(dve, ln[c], k, xg[b][:, k, :])
                    step(roots(dve, step, ln[c], last, 0, 2 * K))
                    minus_mean_over_root(dve, ln[c], 0, 2 * K).then_inc(stats, 1)
                    step.rest()

                def group(j, b, i):
                    c = b % 2
                    dve.wait_ge(relued, 2 * K * (j + 1))
                    wait(dve, copied, j - 1)
                    if there(j + 2, EG):
                        scores(j + 2, (b + 2) % R, i + (b + 2) // R, dot(j, c))
                    else:
                        for emit in dot(j, c):
                            emit()
                    dve.wait_ge(dots, j + 1)
                    dve.tensor_copy(si[:, ds(j * K, K)], sc[c][:, 0:K])
                    dve.tensor_copy(sj[:, ds(j * K, K)], sc[c][:, K:2 * K]).then_inc(copied, 1)

                scores(0, 0, 0)
                scores(1, 1, 0)
                over(dve, EG, R, 2, group)

            @block.scalar
            def _(act):
                act.wait_ge(consts, 128)

                def relu(j, b, i):
                    c = b % 2
                    act.wait_ge(stats, j + 1)
                    wait(act, dots, j - 1)
                    for k in range(2 * K):
                        o = h_dst[:, ds((j * K + k) * D, D)] if k < K else hs[c][:, k - K, :]
                        act.activation(o, xg[b][:, k, :], ACT.Relu, bias=ln[c].nmr[:, k:k + 1],
                                       scale=ln[c].rstd[:, k:k + 1]).then_inc(relued, 1)
                    act.wait_ge(hid_mm, j + 1)
                    act.activation(hid[c][:, :], bank[c][:, 0:GC], ACT.Silu, bias=b1[:, 0:1]).then_inc(hid_done, 1)

                over(act, EG, R, 1, relu)
                act.wait_ge(ew_mm, EG)
                act.activation(ew_t[:, :], bank[2][0:P, 0:ET], ACT.Sigmoid, bias=b2[:, 0:1])

            @block.tensor
            def _(pe):
                pe.wait_ge(consts, 128)

                def hidden(j, b, i):
                    pe.wait_ge(attr[b], 16 * (i + 1))
                    pe.matmul(bank[b][:, 0:GC], w1[:, :], at[b][:, :], start=True, stop=True).then_inc(hid_mm, 1)

                def weigh(j, b, i):
                    pe.wait_ge(hid_done, j + 1)
                    for k in range(K):
                        last = pe.matmul(bank[2][0:P, ds(j * K + k, 1)], hid[b][:, k * P:(k + 1) * P], w2[:, :],
                                         start=True, stop=True)
                    last.then_inc(ew_mm, 1)
                    if there(j + 2, EG):
                        hidden(j + 2, b, i + 1)

                hidden(0, 0, 0)
                hidden(1, 1, 0)
                over(pe, EG, 2, 2, weigh)


def softmax(nc, sem, sb, bank, ident, si, sj, dst_p, alpha, earlier, spare):
    with ExitStack() as ctx:
        t_ = lambda name, shape: sb("s_" + name, shape, F32, ctx)
        key, e, same, gate, f, f2, bk, w = (t_(n, [P, ET]) for n in ("key", "e", "same", "gate", "f", "f2", "bk", "w"))
        gate_b = t_("gate_b", [P, ET])
        cols = t_("cols", [P, 1])
        row = {n: t_("row_" + n, [1, 128]) for n in
               ("k0", "kl", "cont", "on", "g_on", "g_cont", "onb", "g_onb", "g_contb", "edge", "run", "enter", "rev")}
        step_s, rows_s, cols_s, e1, e2, made = (sem("s_" + n) for n in ("step", "rows", "cols", "e1", "e2", "made"))
        counts = {"step": 0, "t": 0}
        jobs = []

        with nc.Block() as block:
            @block.gpsimd
            def _(pool):
                pool.memset(earlier[:, :, :, :], 1.0).then_inc(made, 1)
                pool.wait_ge(made, 1)
                for k in range(K):
                    last = pool.affine_select(out=earlier[:, k, :, :], in_=earlier[:, k, :, :], compare_op=ALU.is_gt, fill=0.0,
                                              base=k * P, pattern=[[-P, K], [-1, P]], channel_multiplier=1)
                last.then_inc(made, 1)
                pool.iota(spare[:, :], pattern=[[P, K]], base=N, channel_multiplier=1,
                          allow_small_or_imprecise_dtypes=True).then_inc(made, 1)

            @block.vector
            def _(dve):
                step = Steps(dve, step_s, 0, None)

                def to_row(dst_row, col):
                    step(dve.tensor_copy(cols[:, :], col))
                    dve.sem_inc(rows_s, 1)
                    jobs.append("row")
                    dve.wait_ge(cols_s, len(jobs))
                    step(dve.tensor_copy(dst_row[0:1, 0:P], bank[0][0:1, 0:P]))

                def to_col(src_row):
                    dve.sem_inc(rows_s, 1)
                    jobs.append("col")
                    dve.wait_ge(cols_s, len(jobs))
                    step(dve.tensor_copy(cols[:, :], bank[1][0:P, 0:1]))

                r = {n: x[0:1, 0:P] for n, x in row.items()}
                step(dve.tensor_copy(key[:, :], dst_p[:, :]))
                step(dve.tensor_tensor(f[:, :], si[:, :], sj[:, :], ALU.add))
                step(dve.scalar_tensor_tensor(e[:, :], f[:, :], 0.01, f[:, :], ALU.mult, ALU.max))
                dve.memset(same[:, :], 1.0)
                step(dve.tensor_tensor(gate_b[:, 1:ET], key[:, 1:ET], key[:, 0:ET - 1], ALU.is_equal))
                step(dve.tensor_copy(same[:, 1:ET], gate_b[:, 1:ET]))
                step(dve.tensor_scalar(gate[:, :], same[:, :], 1.0, BIG, ALU.subtract, ALU.mult))
                step(dve.memset(gate_b[:, :], 0.0))
                step(dve.tensor_copy(gate_b[:, 0:ET - 1], gate[:, 1:ET]))
                to_row(row["k0"], key[:, 0:1])
                to_row(row["kl"], key[:, ET - 1:ET])
                step(dve.memset(r["cont"], 0.0))
                step(dve.tensor_tensor(row["cont"][0:1, 1:P], row["k0"][0:1, 1:P], row["kl"][0:1, 0:P - 1], ALU.is_equal))
                step(dve.tensor_tensor(r["edge"], r["k0"], r["kl"], ALU.is_equal))
                step(dve.tensor_tensor(r["on"], r["edge"], r["cont"], ALU.mult))
                step(dve.tensor_scalar(r["g_on"], r["on"], 1.0, BIG, ALU.subtract, ALU.mult))
                step(dve.tensor_scalar(r["g_cont"], r["cont"], 1.0, BIG, ALU.subtract, ALU.mult))
                step(dve.memset(r["g_contb"], -BIG))
                step(dve.tensor_copy(row["g_contb"][0:1, 0:P - 1], row["g_cont"][0:1, 1:P]))
                step(dve.tensor_scalar(r["onb"], r["edge"], 1.0, BIG, ALU.subtract, ALU.mult))
                step(dve.tensor_tensor(r["g_onb"], r["g_contb"], r["onb"], ALU.min))

                def back_max(x, res):
                    step(dve.tensor_tensor_scan(f2[:, ::-1], gate_b[:, ::-1], x[:, ::-1], -BIG, ALU.add, ALU.max))
                    to_row(row["edge"], f2[:, 0:1])
                    step(dve.tensor_tensor_scan(row["run"][0:1, P - 1::-1], row["g_onb"][0:1, P - 1::-1],
                                                row["edge"][0:1, P - 1::-1], -BIG, ALU.add, ALU.max))
                    step(dve.memset(r["enter"], -BIG))
                    step(dve.tensor_tensor(row["enter"][0:1, 0:P - 1], row["run"][0:1, 1:P], row["g_contb"][0:1, 0:P - 1], ALU.add))
                    to_col(row["enter"])
                    step(dve.tensor_tensor_scan(res[:, ::-1], gate_b[:, ::-1], x[:, ::-1], cols[:, 0:1], ALU.add, ALU.max))

                step(dve.tensor_tensor_scan(f[:, :], gate[:, :], e[:, :], -BIG, ALU.add, ALU.max))
                to_row(row["edge"], f[:, ET - 1:ET])
                step(dve.tensor_tensor_scan(r["run"], r["g_on"], r["edge"], -BIG, ALU.add, ALU.max))
                step(dve.memset(r["enter"], -BIG))
                step(dve.tensor_tensor(row["enter"][0:1, 1:P], row["run"][0:1, 0:P - 1], row["g_cont"][0:1, 1:P], ALU.add))
                to_col(row["enter"])
                step(dve.tensor_tensor_scan(f[:, :], gate[:, :], e[:, :], cols[:, 0:1], ALU.add, ALU.max))
                back_max(f, bk)
                dve.tensor_tensor(f[:, :], e[:, :], bk[:, :], ALU.subtract).then_inc(e1, 1)
                dve.wait_ge(e2, 1)
                step(dve.tensor_tensor_scan(f[:, :], same[:, :], w[:, :], 0.0, ALU.mult, ALU.add))
                to_row(row["edge"], f[:, ET - 1:ET])
                step(dve.tensor_tensor_scan(r["run"], r["on"], r["edge"], 0.0, ALU.mult, ALU.add))
                step(dve.memset(r["enter"], 0.0))
                step(dve.tensor_tensor(row["enter"][0:1, 1:P], row["run"][0:1, 0:P - 1], row["cont"][0:1, 1:P], ALU.mult))
                to_col(row["enter"])
                step(dve.tensor_tensor_scan(f[:, :], same[:, :], w[:, :], cols[:, 0:1], ALU.mult, ALU.add))
                back_max(f, bk)
                step(dve.reciprocal(f[:, :], bk[:, :]))
                step(dve.tensor_tensor(alpha[:, :], w[:, :], f[:, :], ALU.mult))

            @block.scalar
            def _(act):
                act.wait_ge(e1, 1)
                act.activation(w[:, :], f[:, :], ACT.Exp).then_inc(e2, 1)

            @block.tensor
            def _(pe):
                for n, kind in enumerate(jobs):
                    pe.wait_ge(rows_s, n + 1)
                    if kind == "row":
                        pe.transpose(bank[0][0:1, 0:P], cols[:, 0:1], ident[0:P, 0:P]).then_inc(cols_s, 1)
                    else:
                        pe.transpose(bank[1][0:P, 0:1], row["enter"][0:1, 0:P], ident[0:1, 0:1]).then_inc(cols_s, 1)


class Place:

    def __init__(self, nc, sem, t_, name, n, end_t, row_t, ends):
        self.n, self.end_t, self.row_t, self.ends = n, end_t, row_t, ends
        self.to, self.row = ([t_(f"{m}{b}", [P, n], I32) for b in range(2)] for m in ("place_to", "place_row"))
        self.placed = [sem(f"{name}placed{b}", pool=True) for b in range(2)]
        self.places = sem(name + "places")

    def set(self, dve, g, b, half, t):
        wait(dve, self.placed[b % 2], 16 * self.n * half)
        dve.tensor_copy(self.to[b % 2][:, :], self.end_t[:, ds(t, self.n)])
        dve.tensor_copy(self.row[b % 2][:, :], self.row_t[:, ds(t, self.n)]).then_inc(self.places, 1)

    def write(self, pool, g, b, passed):
        pool.wait_ge(self.places, g + 1)
        pool.sem_inc(passed, 1)
        for k in range(self.n):
            pool.indirect_dma_start(
                out=self.ends[:, :], out_offset=bass.IndirectOffsetOnAxis(ap=self.to[b % 2][:, k:k + 1], axis=0),
                in_=self.row[b % 2][:, k:k + 1], in_offset=None, bounds_check=N - 1, oob_is_err=False).then_inc(self.placed[b % 2], 16)

    def end(self, pool, steps):
        for c in range(2):
            pool.wait_ge(self.placed[c], 16 * self.n * (steps // 2))


def scatter_by_source(nc, a, sem, sb, bank, agg0, h_dst, alpha, src_p, earlier, spare, end_t, row_t, ends):
    with ExitStack() as ctx:
        t_ = lambda name, shape, dt=F32: sb("b_" + name, shape, dt, ctx)
        key = t_("key", [P, ET])
        keyrow = [t_(f"keyrow{b}", [P, GC], I32) for b in range(2)]
        same = [t_(f"same{b}", [P, K, GC]) for b in range(2)]
        junk = t_("junk", [P, K, GC])
        cnt, pick, diff = ([t_(f"{n}{b}", [P, K]) for b in range(2)] for n in ("cnt", "pick", "diff"))
        idx = [t_(f"idx{b}", [P, K], I32) for b in range(2)]
        msg = [t_(f"msg{b}", [P, K, D]) for b in range(2)]
        tot = [t_(f"tot{b}", [P, K, D]) for b in range(2)]
        keys_in = [sem(f"b_keys_in{b}") for b in range(2)]
        step_s, msgs, summed, totals, indices, first = (
            sem("b_" + s) for s in ("step", "msgs", "summed", "totals", "indices", "first"))
        added = sem("b_added", pool=True)
        place = Place(nc, sem, t_, "b_", K // 2, end_t, row_t, ends)
        passed = sem("passed")
        with nc.Block() as block:
            @block.sync
            def _(sp):
                def load_keys(j, b, i):
                    wait(sp, msgs, j - 1)
                    sp.dma_start(keyrow[b][:, :], a["src_p"][ds(j * K, K), :].rearrange("(o k) p -> o (k p)", o=1)
                                 .broadcast_to([P, GC])).then_inc(keys_in[b], 16)
                over(sp, EG, 2, 1, load_keys)

            @block.gpsimd
            def _(pool):
                def scatter(j, b, i):
                    place.write(pool, j, b, passed)
                    pool.wait_ge(indices, j + 1)
                    pool.sem_inc(passed, 1)
                    pool.wait_ge(totals, j + 1)
                    pool.sem_inc(passed, 1)
                    wait(pool, added, 64 * j)
                    pool.sem_inc(passed, 1)
                    for k in range(K):
                        pool.indirect_dma_start(
                            out=agg0[:, :], out_offset=bass.IndirectOffsetOnAxis(ap=idx[b][:, k:k + 1], axis=0),
                            in_=tot[b][:, k, :], in_offset=None, compute_op=ALU.add).then_inc(added, 16)
                over(pool, EG, 2, 1, scatter)
                pool.wait_ge(added, 64 * EG)
                place.end(pool, EG)

            @block.vector
            def _(dve):
                dve.tensor_copy(key[:, :], src_p[:, :]).then_inc(first, 1)
                dve.wait_ge(first, 1)

                def group(j, b, i):
                    place.set(dve, j, b, i, j * K)
                    step = Steps(dve, step_s, j * 4, passed)
                    wait(dve, summed, j - 1)
                    dve.wait_ge(keys_in[b], 16 * (i + 1))
                    for k in range(K):
                        t = j * K + k
                        dve.tensor_scalar(msg[b][:, k, :], h_dst[:, ds(t * D, D)], alpha[:, ds(t, 1)], None, ALU.mult)
                        last = dve.tensor_scalar(same[b][:, k, :], keyrow[b][:, :], key[:, ds(t, 1)], None, ALU.is_equal)
                    step(last)
                    dve.sem_inc(msgs, 1)
                    for k in range(K):
                        last = dve.scalar_tensor_tensor(junk[:, k, :], same[b][:, k, :], 1.0,
                                                        earlier[:, k, :, :].rearrange("p j q -> p (j q)"),
                                                        ALU.mult, ALU.mult, accum_out=cnt[b][:, k:k + 1])
                    step(last)
                    dve.tensor_scalar(pick[b][:, :], cnt[b][:, :], 0.5, None, ALU.is_lt)
                    step(dve.tensor_tensor(diff[b][:, :], key[:, ds(j * K, K)], spare[:, :], ALU.subtract))
                    step(dve.tensor_tensor(cnt[b][:, :], diff[b][:, :], pick[b][:, :], ALU.mult))
                    wait(dve, added, 64 * (j - 1))
                    dve.tensor_tensor(idx[b][:, :], cnt[b][:, :], spare[:, :], ALU.add).then_inc(indices, 1)
                over(dve, EG, 2, 1, group)

            @block.scalar
            def _(act):
                def sums_out(j, b, i):
                    act.wait_ge(summed, j + 1)
                    wait(act, added, 64 * (j - 1))
                    act.activation(tot[b][:, :, :].rearrange("p k d -> p (k d)"), bank[b][0:P, 0:K * D], ACT.Copy).then_inc(totals, 1)
                over(act, EG, 2, 1, sums_out)

            @block.tensor
            def _(pe):
                def sums(j, b, i):
                    pe.wait_ge(msgs, j + 1)
                    wait(pe, totals, j - 1)
                    for o in range(K):
                        for k in range(K):
                            last = pe.matmul(bank[b][0:P, o * D:(o + 1) * D], same[b][:, k, o * P:(o + 1) * P],
                                             msg[b][:, k, :], start=(k == 0), stop=(k == K - 1))
                    last.then_inc(summed, 1)
                over(pe, EG, 2, 1, sums)


def layer0_nodes(nc, a, sem, sb, bank, ident, agg0, x1, node_rows, end_t, row_t, ends):
    with ExitStack() as ctx:
        t_ = lambda name, shape, dt=F32: sb("c_" + name, shape, dt, ctx)
        R = 6
        flat = lambda ap: ap[:, :, :].rearrange("p k d -> p (k d)")
        w = t_("w", [D, D])
        wi = t_("wi", [D, D])
        ag = [t_(f"ag{b}", [P, K, D]) for b in range(R)]
        x = [t_(f"x{b}", [P, K, D]) for b in range(R)]
        at = [t_(f"at{b}", [D, GC]) for b in range(2)]
        y = [t_(f"y{b}", [P, K, D]) for b in range(2)]
        z = [t_(f"z{b}", [P, K, D]) for b in range(R)]
        loaded = [sem(f"c_loaded{b}") for b in range(R)]
        stored = [sem(f"c_stored{b}") for b in range(R)]
        w_in, w_made, turned, turned_out, mm, act_done, sums = (
            sem("c_" + s) for s in ("w_in", "w_made", "turned", "turned_out", "mm", "act_done", "sums"))
        passed = sem("passed")
        place = Place(nc, sem, t_, "c_", 1, end_t, row_t, ends)
        assert NG == 2 * EG and K == 4
        with nc.Block() as block:
            @block.sync
            def _(sp):
                sp.dma_start(w[:, :], a["L0_gnn_W"]).then_inc(w_in, 16)

                def load(g, b):
                    sp.dma_start(ag[b][:, :, :], node_rows(agg0, g)).then_inc(loaded[b], 16)
                    sp.dma_start(x[b][:, :, :], node_rows(a["x"], g)).then_inc(loaded[b], 16)

                def move(g, b, i):
                    sp.wait_ge(sums, g + 1)
                    sp.dma_start(node_rows(x1, g), z[b][:, :, :]).then_inc(stored[b], 16)
                    if there(g + R, NG):
                        load(g + R, b)

                for b in range(R):
                    load(b, b)
                over(sp, NG, R, R, move)
                for b in range(R):
                    sp.wait_ge(stored[b], 16 * (NG // R + (b < NG % R)))

            @block.tensor
            def _(pe):
                def turn(g, b, i):
                    pe.wait_ge(loaded[b], 32 * (i + 1))
                    for k in range(K):
                        last = pe.transpose(bank[b % 2][:, k * P:(k + 1) * P], ag[b][:, k, :], ident[0:P, 0:P])
                    last.then_inc(turned, 1)

                def product(g, b, i):
                    if there(g + 1, NG):
                        turn(g + 1, (b + 1) % R, i + (b + 1) // R)
                    pe.wait_ge(turned_out, g + 1)
                    wait(pe, act_done, g - 1)
                    for k in range(K):
                        last = pe.matmul(bank[2 + b % 2][0:P, k * D:(k + 1) * D], at[b % 2][:, k * P:(k + 1) * P], wi[:, :],
                                         start=True, stop=True)
                    last.then_inc(mm, 1)

                pe.wait_ge(w_made, 1)
                turn(0, 0, 0)
                over(pe, NG, R, 1, product)

            @block.vector
            def _(dve):
                dve.wait_ge(w_in, 16)
                dve.tensor_tensor(wi[:, :], w[:, :], ident[:, :], ALU.add).then_inc(w_made, 1)

                def evacuate(g, b, i):
                    dve.wait_ge(turned, g + 1)
                    wait(dve, mm, g - 1)
                    dve.tensor_copy(at[b % 2][:, :], bank[b % 2][:, 0:GC]).then_inc(turned_out, 1)

                def add_rows(g, b, i):
                    dve.wait_ge(act_done, g + 1)
                    wait(dve, stored[b], 16 * i)
                    dve.tensor_tensor(flat(z[b]), flat(y[b % 2]), flat(x[b]), ALU.add).then_inc(sums, 1)

                def group(g, b, i):
                    place.set(dve, g, b, R // 2 * i + b // 2, 2 * g + 2 - b % 2)
                    evacuate(g, b, i)
                    if there(g - 1, NG):
                        add_rows(g - 1, (b - 1) % R, i if b else i - 1)
                over(dve, NG, R, 1, group)
                add_rows(NG - 1, (NG - 1) % R, (NG - 1) // R)

            @block.scalar
            def _(act):
                def gelu(g, b, i):
                    act.wait_ge(mm, g + 1)
                    wait(act, sums, g - 1)
                    act.activation(flat(y[b % 2]), bank[2 + b % 2][0:P, 0:K * D], ACT.Gelu).then_inc(act_done, 1)
                over(act, NG, R, 1, gelu)

            @block.gpsimd
            def _(pool):
                over(pool, NG, 2, 1, lambda g, b, i: place.write(pool, g, b, passed))
                place.end(pool, NG)


def edges(nc, a, sem, sb, bank, layer, ident, x, agg, src_t, key_t, prev_t, to_t, ew_t, ends=None, ends_t=None):
    with ExitStack() as ctx:
        nm = f"e{layer}_"
        t_ = lambda name, shape, dt=F32: sb(nm + name, shape, dt, ctx)
        R = 6
        LAG = 2 if layer == 2 else 1
        B = 3 if layer == 3 else 2
        ring, three, two = range(R), range(W), range(2)
        xg = [t_(f"xg{b}", [P, K, D]) for b in ring]
        from_i = [t_(f"from_i{b}", [P, K], I32) for b in ring]
        to_i = [t_(f"to_i{b}", [P, K], I32) for b in three]
        keyrow = [t_(f"keyrow{b}", [P, GC], I32) for b in two]
        same = [t_(f"same{b}", [P, K, P]) for b in range(B)]
        carry = [t_(f"carry{b}", [P, K, P]) for b in range(B)]
        ln = [Stats(t_, f"ln{b}", 2 * K) for b in three] if layer == 3 else [Stats(t_, f"ln{b}", K) for b in two]
        msg = [t_(f"msg{b}", [P, K, D + 1]) for b in three]
        run = [t_(f"run{b}", [P, K, D + 1]) for b in range(B)]
        cnt = [t_(f"cnt{b}", [P, K]) for b in two]
        res = [t_(f"res{b}", [P, K, D]) for b in three]
        if layer == 1:
            h = [t_(f"h{b}", [P, K, D]) for b in two]
            ht = [t_(f"ht{b}", [D, GC]) for b in two]
            m = [t_(f"m{b}", [P, K, D]) for b in two]
            bias, part = t_("bias", [65, D]), t_("part", [65, D])
            split, ones = t_("split", [65, D], BF16), t_("ones", [65, P], BF16)
        if layer != 3:
            w = t_("w", [D, D])
        if layer == 2:
            rt = [t_(f"rt{b}", [D, GC]) for b in two]
        gathered = [sem(f"{nm}gathered{b}", pool=True) for b in ring]
        keys_in = [sem(f"{nm}keys_in{b}") for b in two]
        written = [sem(f"{nm}written{b}", pool=layer != 3) for b in three]
        passed = sem("passed")
        ready, from_set, to_set, step_s, stats, relued, matrices, run_mm, run_out, results = (
            sem(nm + s) for s in ("ready", "from_set", "to_set", "step", "stats", "relued", "matrices", "run_mm",
                                  "run_out", "results"))
        consts = sem(nm + "consts")
        if layer != 3:
            turned, turned_out, mm = (sem(nm + s) for s in ("turned", "turned_out", "mm"))
        if layer != 2:
            out_s = sem(nm + "out")
        if layer == 1:
            silued, msgs, made, made_s = (sem(nm + s) for s in ("silued", "msgs", "made", "made_s"))
        n_consts = 32 if layer == 1 else 16
        run_at = lambda k: bank[4 + k % 2][0:P, 0:D + 1]
        flat = lambda ap: ap[:, :, :].rearrange("p k d -> p (k d)")
        with nc.Block() as block:
            @block.sync
            def _(sp):
                if layer == 1:
                    sp.dma_start(bias[:, :], a["L1_gnn_agg_b"].rearrange("(o d) -> o d", o=1).broadcast_to([65, D])).then_inc(consts, 16)
                    sp.dma_start(w[:, :], a["L1_gnn_agg_W"]).then_inc(consts, 16)
                if layer == 2:
                    sp.dma_start(w[:, :], a["w2t"]).then_inc(consts, 16)

                def load_keys(j, b, i):
                    wait(sp, matrices, j - 1)
                    sp.dma_start(keyrow[b][:, :], a["dst_rows"][ds(j * K, K), :].rearrange("(o k) p -> o (k p)", o=1)
                                 .broadcast_to([P, GC])).then_inc(keys_in[b], 16)

                def store(j, b):
                    sp.wait_ge(results, j + 1)
                    sp.dma_start(agg[ds(j * GC, GC), :].rearrange("(p k) d -> p k d", k=K), res[b % W][:, :, :]).then_inc(written[b % W], 16)

                def move(j, b, i):
                    load_keys(j, b % 2, None)
                    if there(j - 5, EG):
                        store(j - 5, (b - 5) % R)

                if layer == 3:
                    sp.dma_start(ends_t[:, :].rearrange("p (g k) -> p g k", k=K), ends.rearrange("(g p k) o -> p g (k o)", p=P, k=K)).then_inc(consts, 16)
                    over(sp, EG, R, 1, move)
                    for j in range(EG - 5, EG):
                        store(j, j % R)
                    sp.wait_ge(consts, 16)
                    for s in three:
                        sp.wait_ge(written[s], 16 * len(range(s, EG, W)))
                else:
                    over(sp, EG, 2, 1, load_keys)

            @block.gpsimd
            def _(pool):
                def gather(j, b):
                    wait(pool, relued, K * (j - R + 1))
                    pool.sem_inc(passed, 1)
                    pool.wait_ge(from_set, j + 1)
                    pool.sem_inc(passed, 1)
                    for k in range(K):
                        pool.indirect_dma_start(
                            out=xg[b][:, k, :], out_offset=None, in_=x[0:N, :],
                            in_offset=bass.IndirectOffsetOnAxis(ap=from_i[b][:, k:k + 1], axis=0)).then_inc(gathered[b], 16)

                def write(j, b):
                    pool.wait_ge(to_set, j + 1)
                    pool.sem_inc(passed, 1)
                    pool.wait_ge(results, j + 1)
                    pool.sem_inc(passed, 1)
                    for k in range(K):
                        to = bass.IndirectOffsetOnAxis(ap=to_i[b % W][:, k:k + 1], axis=0)
                        if layer == 2:
                            pool.indirect_dma_start(out=agg[:, :], out_offset=to, in_=res[b % W][:, k, :], in_offset=None,
                                                    compute_op=ALU.add).then_inc(written[b % W], 16)
                        else:
                            pool.indirect_dma_start(out=agg[:, :], out_offset=to, in_=res[b % W][:, k, :], in_offset=None,
                                                    bounds_check=N - 1, oob_is_err=False).then_inc(written[b % W], 16)

                def group(j, b, i):
                    if there(j + R, EG):
                        gather(j + R, b)
                    if layer != 3 and there(j - LAG, EG):
                        write(j - LAG, (b - LAG) % R)

                for b in ring:
                    gather(b, b)
                over(pool, EG, R, R, group)
                if layer != 3:
                    for j in range(EG - LAG, EG):
                        write(j, j % R)
                    for s in three:
                        pool.wait_ge(written[s], 64 * len(range(s, EG, W)))

            @block.vector
            def _(dve):
                def set_from(j, b):
                    dve.tensor_copy(from_i[b][:, :], src_t[:, ds(j * K, K)]).then_inc(from_set, 1)

                def set_to(j, b, i):
                    wait(dve, written[b % W], 64 * (2 * i + b // W))
                    dve.tensor_copy(to_i[b % W][:, :], to_t[:, ds(j * K, K)]).then_inc(to_set, 1)

                def normalize(j, b, i, between=()):
                    c = b % 2
                    step = Steps(dve, step_s, j * STATS, passed, between)
                    wait(dve, relued, K * (j - 1))
                    dve.wait_ge(gathered[b], 64 * (i + 1))
                    for k in range(K):
                        last = moments(dve, ln[c], k, xg[b][:, k, :])
                    step(roots(dve, step, ln[c], last, 0, K))
                    minus_mean_over_root(dve, ln[c], 0, K).then_inc(stats, 1)
                    step.rest()

                def pair_moments(c, i):
                    dve.wait_ge(gathered[c % R], 64 * (i + c // R + 1))
                    for k in range(K):
                        last = moments(dve, ln[(c + 1) // 2 % W], (0 if c % 2 else K) + k, xg[c % R][:, k, :])
                    return last

                def pair_roots(q, s, last, lo, hi, between):
                    step = Steps(dve, step_s, q * STATS, passed, between)
                    step(roots(dve, step, s, last, lo, hi))
                    minus_mean_over_root(dve, s, lo, hi).then_inc(stats, 1)
                    step.rest()

                def compare(j, b):
                    def one(k, matrix, keys, last):
                        t = j * K + k
                        ins = dve.tensor_scalar(matrix[b % B][:, k, :], keyrow[b % 2][:, k * P:(k + 1) * P], keys[:, ds(t, 1)], None, ALU.is_equal)
                        if last:
                            ins.then_inc(matrices, 1)
                        return ins
                    return [lambda k=k, m=m, y=y: one(k, m, y, k == K - 1 and m is carry)
                            for k in range(K) for m, y in ((same, key_t), (carry, prev_t))]

                def weigh(j, b):
                    dve.wait_ge(silued, j + 1)
                    for k in range(K):
                        last = dve.tensor_scalar(msg[b % W][:, k, 0:D], m[b % 2][:, k, :], ew_t[:, ds(j * K + k, 1)], None, ALU.mult)
                    last.then_inc(msgs, 1)

                def means(j, b):
                    c = b % 2
                    dve.wait_ge(run_out, K * (j + 1))
                    dve.tensor_scalar(cnt[c][:, :], run[b % B][:, :, D], 1.0, None, ALU.max).then_inc(out_s, 1)
                    dve.wait_ge(out_s, 2 * j + 1)
                    dve.reciprocal(cnt[c][:, :], cnt[c][:, :]).then_inc(out_s, 1)
                    dve.wait_ge(out_s, 2 * j + 2)
                    for k in range(K):
                        last = dve.tensor_scalar(res[b % W][:, k, :], run[b % B][:, k, 0:D], cnt[c][:, k:k + 1], None, ALU.mult)
                    last.then_inc(results, 1)

                def group(j, b, i):
                    if there(j + R + 1, EG):
                        set_from(j + R + 1, (b + 1) % R)
                    if there(j + 1, EG):
                        dve.wait_ge(keys_in[(b + 1) % 2], 16 * (R // 2 * i + (b + 1) // 2 + 1))
                    if layer == 2:
                        wait(dve, run_mm, K * j)
                    between = compare(j + 1, b + 1) if there(j + 1, EG) else []
                    if layer == 3:
                        last = pair_moments(b + 4, i) if there(j + 4, EG) else None
                    if layer == 3 and b % 2 == 0 and there(j + 3, EG):
                        last = last or between.pop(0)()
                        pair_roots(R // 2 * i + (b + 4) // 2, ln[(b + 4) // 2 % W], last, 0, 2 * K if there(j + 4, EG) else K, between)
                    elif layer != 3 and there(j + 3, EG):
                        normalize(j + 3, (b + 3) % R, i + (b + 3) // R, between)
                    else:
                        for emit in between:
                            emit()
                    if layer != 3:
                        set_to(j, b, i)
                    if layer == 1:
                        means(j, b)
                    if layer == 3 and there(j - 1, EG):
                        before, i_before = (b - 1) % R, i if b else i - 1
                        wait(dve, written[before % W], 16 * (2 * i_before + before // W))
                        means(j - 1, before)
                    if layer == 1 and there(j + 1, EG):
                        weigh(j + 1, (b + 1) % R)

                for b in ring:
                    set_from(b, b)
                for msg_b in msg:
                    dve.memset(msg_b[:, :, D:D + 1], 1.0)
                for run_b in run:
                    last = dve.memset(run_b[:, :, :], 0.0)
                last.then_inc(ready, 1)
                if layer == 1:
                    dve.wait_ge(consts, n_consts)
                    bias_parts(dve, Steps(dve, made_s, 0, None), made, bias, part, split, ones)
                if layer == 3:
                    pair_roots(0, ln[0], pair_moments(0, 0), K, 2 * K, [])
                    set_from(R, 0)
                    for b in (1, 2):
                        last = pair_moments(b, 0)
                    dve.wait_ge(keys_in[0], 16)
                    pair_roots(1, ln[1], last, 0, 2 * K, compare(0, 0))
                    pair_moments(3, 0)
                else:
                    normalize(0, 0, 0)
                    set_from(R, 0)
                    dve.wait_ge(keys_in[0], 16)
                    normalize(1, 1, 0, compare(0, 0))
                    normalize(2, 2, 0)
                if layer == 1:
                    weigh(0, 0)
                over(dve, EG, R, R, group)
                if layer == 3:
                    dve.wait_ge(written[(EG - 1) % W], 16 * ((EG - 1) // W))
                    means(EG - 1, (EG - 1) % R)

            @block.scalar
            def _(act):
                act.wait_ge(ready, 1)

                def relu(j, c, i, k):
                    if layer == 3:
                        s, n, value = ln[(c + 1) // 2 % W], (0 if c % 2 else K) + k, R // 2 * i + (c + 1) // 2 + 1
                    else:
                        s, n, value = ln[c % 2], k, j + 1
                    if k == 0:
                        act.wait_ge(stats, value)
                    act.activation(h[c % 2][:, k, :] if layer == 1 else msg[c % W][:, k, 0:D], xg[c % R][:, k, :], ACT.Relu,
                                   bias=s.nmr[:, n:n + 1], scale=s.rstd[:, n:n + 1]).then_inc(relued, 1)

                def run_copy(j, b, k):
                    if layer == 3 and k == 0:
                        wait(act, results, j - B + 1)
                    act.wait_ge(run_mm, K * j + k + 1)
                    act.activation(run[b % B][:, k, :], run_at(k), ACT.Copy).then_inc(run_out, 1)

                def evacuate(j, b):
                    act.wait_ge(turned, j + 1)
                    if layer == 1:
                        act.activation(ht[b % 2][:, :], bank[b % 2][:, 0:GC], ACT.Copy).then_inc(turned_out, 1)
                    else:
                        act.activation(rt[b % 2][:, :], bank[6][:, 0:GC], ACT.Copy).then_inc(turned_out, 1)

                def silu(j, b):
                    act.wait_ge(mm, j + 1)
                    act.activation(flat(m[b % 2]), bank[2 + b % 2][0:P, 0:K * D], ACT.Silu).then_inc(silued, 1)

                def products(j, b, i):
                    wait(act, written[b % W], 64 * (2 * i + b // W))
                    act.wait_ge(mm, j + 1)
                    act.activation(flat(res[b % W]), bank[7][0:P, 0:K * D], ACT.Copy).then_inc(results, 1)

                def group(j, b, i):
                    before, b_before, i_before = j - 1, (b - 1) % R, (i if b else i - 1)
                    if layer == 2 and there(before, EG):
                        evacuate(before, b_before)
                    for k in range(K):
                        if there(j + 2, EG):
                            relu(j + 2, b + 2, i, k)
                        run_copy(j, b, k)
                    if layer == 1 and there(j + 1, EG):
                        silu(j + 1, (b + 1) % R)
                    if layer == 1 and there(j + 2, EG):
                        evacuate(j + 2, (b + 2) % R)
                    if layer == 2 and there(before, EG):
                        products(before, b_before, i_before)

                for j in two:
                    for k in range(K):
                        relu(j, j, 0, k)
                if layer == 1:
                    evacuate(0, 0)
                    silu(0, 0)
                    evacuate(1, 1)
                over(act, EG, R, R, group)
                if layer == 2:
                    evacuate(EG - 1, (EG - 1) % R)
                    products(EG - 1, (EG - 1) % R, (EG - 1) // R)

            @block.tensor
            def _(pe):
                pe.wait_ge(ready, 1)
                if layer != 3:
                    pe.wait_ge(consts, n_consts)
                if layer == 1:
                    pe.wait_ge(made, 1)

                def turn(j, b):
                    pe.wait_ge(relued, K * (j + 1))
                    for k in range(K):
                        last = pe.transpose(bank[b % 2][:, k * P:(k + 1) * P], h[b % 2][:, k, :], ident[0:P, 0:P])
                    last.then_inc(turned, 1)

                def linear(j, b, k):
                    o = bank[2 + b % 2]
                    if k == 0:
                        put_bias(pe, o, ones, split)
                        pe.wait_ge(turned_out, j + 1)
                    ins = pe.matmul(o[0:P, k * D:(k + 1) * D], ht[b % 2][:, k * P:(k + 1) * P], w[:, :],
                                    start=False, stop=(k == K - 1))
                    if k == K - 1:
                        ins.then_inc(mm, 1)

                def turn_runs(j, b):
                    pe.wait_ge(run_out, K * (j + 1))
                    for k in range(K):
                        last = pe.transpose(bank[6][:, k * P:(k + 1) * P], run[b % B][:, k, 0:D], ident[0:P, 0:P])
                    last.then_inc(turned, 1)

                def times_w(j, b, k):
                    if k == 0:
                        wait(pe, results, j)
                        pe.wait_ge(turned_out, j + 1)
                    ins = pe.matmul(bank[7][0:P, k * D:(k + 1) * D], rt[b % 2][:, k * P:(k + 1) * P], w[:, :],
                                    start=True, stop=True)
                    if k == K - 1:
                        ins.then_inc(mm, 1)

                def group(j, b, i):
                    c = b % 2
                    if layer == 2 and there(j - 1, EG):
                        turn_runs(j - 1, (b - 1) % R)
                    pe.wait_ge(matrices, j + 1)
                    if layer == 1:
                        pe.wait_ge(msgs, j + 1)
                    else:
                        pe.wait_ge(relued, K * (j + 1))
                    for k in range(K):
                        pe.matmul(run_at(k), same[b % B][:, k, :], msg[b % W][:, k, :], start=True, stop=False)
                        if layer == 1 and there(j + 1, EG):
                            linear(j + 1, (b + 1) % R, k)
                        if layer == 2 and there(j - 1, EG):
                            times_w(j - 1, (b - 1) % R, k)
                        before = run[b % B][:, k - 1, :] if k else run[(b - 1) % B][:, K - 1, :]
                        wait(pe, run_out, K * j + k)
                        pe.matmul(run_at(k), carry[b % B][:, k, :], before, start=False, stop=True).then_inc(run_mm, 1)
                    if layer == 1 and there(j + 2, EG):
                        turn(j + 2, (b + 2) % R)

                if layer == 1:
                    turn(0, 0)
                    turn(1, 1)
                    for k in range(K):
                        linear(0, 0, k)
                over(pe, EG, R, R, group)
                if layer == 2:
                    turn_runs(EG - 1, (EG - 1) % R)
                    for k in range(K):
                        times_w(EG - 1, (EG - 1) % R, k)


def bias_parts(dve, step, made, row, part, split, ones):
    dve.memset(ones[:, :], 0.0)
    step(dve.memset(split[:, :], 0.0))
    for p in (0, 32, 64):
        dve.memset(ones[p:p + 1, :], 1.0)
    for p in (0, 32, 64):
        step(dve.tensor_copy(split[p:p + 1, :], row[p:p + 1, :]))
    for p in (32, 64):
        step(dve.tensor_tensor(part[p:p + 1, :], row[p:p + 1, :], split[p:p + 1, :], ALU.subtract))
        step(dve.tensor_copy(split[p:p + 1, :], part[p:p + 1, :]))
    step(dve.tensor_tensor(part[64:65, :], part[64:65, :], split[64:65, :], ALU.subtract))
    dve.tensor_copy(split[64:65, :], part[64:65, :]).then_inc(made, 1)


def put_bias(pe, o, ones, split):
    pe.matmul(o[0:P, 0:K * D].rearrange("p (k d) -> p k d", k=K), ones[:, :],
              split[:, :].rearrange("p (o d) -> p o d", o=1).broadcast_to([65, K, D]), start=True, stop=False)


def layer1_nodes(nc, a, sem, sb, bank, ident, x1, agg1, x2, x3, node_rows):
    with ExitStack() as ctx:
        t_ = lambda name, shape, dt=F32: sb("d_" + name, shape, dt, ctx)
        R = 10
        ring, two = range(R), range(2)
        wh, wa, w2, wr = (t_(n, [D, D]) for n in ("wh", "wa", "w2", "wr"))
        b1 = t_("b1", [D, 1])
        gain, shift = t_("gain", [P, K, D]), t_("shift", [P, K, D])
        b2 = t_("b2", [65, D])
        part = t_("part", [65, D])
        b2s = t_("b2s", [65, D], BF16)
        ones = t_("ones", [65, P], BF16)
        x = [t_(f"x{b}", [P, K, D]) for b in ring]
        ag = [t_(f"ag{b}", [P, K, D]) for b in ring]
        z = [t_(f"z{b}", [P, K, D]) for b in ring]
        h, yn = ([t_(f"{n}{b}", [P, K, D]) for b in two] for n in ("h", "yn"))
        at, ut = ([t_(f"{n}{b}", [D, GC]) for b in two] for n in ("at", "ut"))
        H = 5
        ht = [t_(f"ht{b}", [D, GC]) for b in range(H)]
        early = [Stats(t_, f"early{b}", 2 * K) for b in two]
        ln = [Stats(t_, f"ln{b}", 2 * K) for b in two]
        loaded, stored = ([sem(f"d_{s}{b}") for b in ring] for s in ("loaded", "stored"))
        consts, b2_in, gains_in, made, made_s, first_s, step_s, normed, turned, evac, mm, silued, mo, stats, onormed, sums = (
            sem("d_" + s) for s in ("consts", "b2_in", "gains_in", "made", "made_s", "first_s", "step_s", "normed", "turned", "evac",
                                    "mm", "silued", "mo", "stats", "onormed", "sums"))
        passed = sem("passed")
        flat = lambda ap: ap.rearrange("p k d -> p (k d)")
        with nc.Block() as block:
            @block.sync
            def _(sp):
                def load(g, b):
                    sp.dma_start(x[b][:, :, :], node_rows(x1, g)).then_inc(loaded[b], 16)
                    sp.dma_start(ag[b][:, :, :], node_rows(agg1, g)).then_inc(loaded[b], 16)

                def move(g, b, i):
                    sp.wait_ge(sums, 3 * (g + 1))
                    sp.dma_start(node_rows(x2, g), z[b][:, :, :]).then_inc(stored[b], 16)
                    sp.dma_start(node_rows(x3, g), z[b][:, :, :]).then_inc(stored[b], 16)
                    if there(g + R, NG):
                        load(g + R, b)

                row = lambda n, to: a[n].rearrange("(o d) -> o d", o=1).broadcast_to([to, D])
                for b in range(4):
                    load(b, b)
                sp.dma_start(b2[:, :], row("L1_gnn_upd_b2", 65)).then_inc(b2_in, 16)
                sp.dma_start(b1[:, :], a["L1_gnn_upd_b1"].rearrange("(d o) -> d o", o=1)).then_inc(consts, 16)
                sp.dma_start(wh[:, :], a["L1_gnn_upd_W1"][0:D, :]).then_inc(consts, 16)
                sp.dma_start(wa[:, :], a["L1_gnn_upd_W1"][D:2 * D, :]).then_inc(consts, 16)
                sp.dma_start(w2[:, :], a["L1_gnn_upd_W2"]).then_inc(consts, 16)
                sp.dma_start(wr[:, :], a["L1_gnn_res_W"]).then_inc(consts, 16)
                for b in (4, 5):
                    load(b, b)
                for k in range(K):
                    sp.dma_start(gain[:, k, :], row("L1_gnn_ln_g", P)).then_inc(gains_in, 16)
                    sp.dma_start(shift[:, k, :], row("L1_gnn_ln_b", P)).then_inc(gains_in, 16)
                for b in range(6, R):
                    load(b, b)
                over(sp, NG, R, R, move)
                for b in ring:
                    sp.wait_ge(stored[b], 32 * (NG // R + (b < NG % R)))

            @block.vector
            def _(dve):
                def x_moments(g, b, s):
                    return [lambda k=k: moments(dve, s, k, x[b][:, k, :]) for k in range(K)]

                def group(g, b, i):
                    c = b % 2
                    lo, between = (0 if there(g + 5, NG) else K), []
                    if there(g + 6, NG):
                        dve.wait_ge(loaded[(b + 6) % R], 32 * (i + (b + 6) // R + 1))
                        between = x_moments(g + 6, (b + 6) % R, ln[1 - c])
                    step = Steps(dve, step_s, g * STATS, passed, between)
                    wait(dve, normed, g + 4 if there(g + 3, NG) else NG)
                    dve.wait_ge(mo, g + 1)
                    for k in range(K):
                        last = moments(dve, ln[c], K + k, bank[6 + c][0:P, k * D:(k + 1) * D])
                    step(roots(dve, step, ln[c], last, lo, 2 * K))
                    minus_mean_over_root(dve, ln[c], lo, 2 * K).then_inc(stats, 1)
                    step.rest()

                for g in range(4):
                    dve.wait_ge(loaded[g], 32)
                for g in range(4):
                    for k in range(K):
                        last = moments(dve, early[g // 2], g % 2 * K + k, x[g][:, k, :])
                fifth, sixth = x_moments(4, 4, ln[1]), x_moments(5, 5, ln[0])

                def first_stats(n, s, blocks, last, between):
                    step = Steps(dve, first_s, n * STATS, passed, between)
                    step(roots(dve, step, s, last, 0, blocks))
                    minus_mean_over_root(dve, s, 0, blocks).then_inc(stats, 1)
                    step.rest()

                first_stats(0, early[0], 2 * K, last, [])
                dve.wait_ge(b2_in, 16)
                bias_parts(dve, Steps(dve, made_s, 0, None), made, b2, part, b2s, ones)
                for g in (4, 5):
                    dve.wait_ge(loaded[g], 32)
                first_stats(1, early[1], 2 * K, fifth[0](), fifth[1:] + sixth[:-1])
                first_stats(2, ln[1], K, sixth[-1](), [])
                over(dve, NG, R, 6, group)

            @block.scalar
            def _(act):
                def normalize(g, b):
                    s, lo = (early[g // 2], g % 2 * K) if isinstance(g, int) and g < 4 else (ln[1 - b % 2], 0)
                    act.wait_ge(stats, max(g - 1, 1 + g // 2) if isinstance(g, int) else g - 1)
                    wait(act, turned, g - 1)
                    for k in range(K):
                        last = act.activation(h[b % 2][:, k, :], x[b][:, k, :], ACT.Relu,
                                              bias=s.nmr[:, lo + k:lo + k + 1], scale=s.rstd[:, lo + k:lo + k + 1])
                    last.then_inc(normed, 1)

                def evacuate(g, b):
                    c = b % 2
                    act.wait_ge(turned, g + 1)
                    act.activation(ht[b % H][:, :], bank[c][:, 0:GC], ACT.Copy)
                    act.activation(at[c][:, :], bank[2 + c][:, 0:GC], ACT.Copy).then_inc(evac, 1)

                def silu(g, b):
                    c = b % 2
                    act.wait_ge(mm, g + 1)
                    act.activation(ut[c][:, :], bank[4 + c][:, 0:GC], ACT.Silu, bias=b1[:, 0:1]).then_inc(silued, 1)

                def out_normalize(g, b):
                    c = b % 2
                    act.wait_ge(stats, g + 4)
                    wait(act, sums, 3 * (g - 1))
                    for k in range(K):
                        last = act.activation(yn[c][:, k, :], bank[6 + c][0:P, k * D:(k + 1) * D], ACT.Identity,
                                              bias=ln[c].nmr[:, K + k:K + k + 1], scale=ln[c].rstd[:, K + k:K + k + 1])
                    last.then_inc(onormed, 1)

                def group(g, b, i):
                    silu(g, b)
                    if there(g + 1, NG):
                        evacuate(g + 1, (b + 1) % R)
                    if there(g + 2, NG):
                        normalize(g + 2, (b + 2) % R)
                    if there(g - 2, NG):
                        out_normalize(g - 2, (b - 2) % R)

                for g in two:
                    normalize(g, g)
                act.wait_ge(consts, 16 * 5)
                evacuate(0, 0)
                over(act, NG, R, 2, group)
                for g in (NG - 2, NG - 1):
                    out_normalize(g, g % R)

            @block.gpsimd
            def _(pool):
                pool.wait_ge(gains_in, 32 * K)

                def finish(g, b, i):
                    c = b % 2
                    pool.wait_ge(onormed, g + 1)
                    pool.tensor_tensor(yn[c][:, :, :], yn[c][:, :, :], gain[:, :, :], ALU.mult).then_inc(sums, 1)
                    wait(pool, stored[b], 32 * i)
                    pool.tensor_tensor(z[b][:, :, :], x[b][:, :, :], shift[:, :, :], ALU.add).then_inc(sums, 1)
                    pool.wait_ge(sums, 3 * g + 2)
                    pool.tensor_tensor(z[b][:, :, :], z[b][:, :, :], yn[c][:, :, :], ALU.add).then_inc(sums, 1)
                over(pool, NG, R, 2, finish)

            @block.tensor
            def _(pe):

                def turn(g, b):
                    c = b % 2
                    pe.wait_ge(normed, g + 1)
                    for k in range(K):
                        pe.transpose(bank[c][:, k * P:(k + 1) * P], h[c][:, k, :], ident[0:P, 0:P])
                    for k in range(K):
                        last = pe.transpose(bank[2 + c][:, k * P:(k + 1) * P], ag[b][:, k, :], ident[0:P, 0:P])
                    last.then_inc(turned, 1)

                def hidden(g, b):
                    c = b % 2
                    pe.wait_ge(evac, g + 1)
                    pe.matmul(bank[4 + c][:, 0:GC], wh[:, :], ht[b % H][:, :], start=True, stop=False)
                    pe.matmul(bank[4 + c][:, 0:GC], wa[:, :], at[c][:, :], start=False, stop=True).then_inc(mm, 1)

                def outer(g, b):
                    c = b % 2
                    o = bank[6 + c]
                    wait(pe, onormed, g - 1)
                    put_bias(pe, o, ones, b2s)
                    for k in range(K):
                        pe.matmul(o[0:P, k * D:(k + 1) * D], ht[b % H][:, k * P:(k + 1) * P], wr[:, :], start=False, stop=False)
                    pe.wait_ge(silued, g + 1)
                    for k in range(K):
                        last = pe.matmul(o[0:P, k * D:(k + 1) * D], ut[c][:, k * P:(k + 1) * P], w2[:, :],
                                         start=False, stop=(k == K - 1))
                    last.then_inc(mo, 1)

                def group(g, b, i):
                    hidden(g, b)
                    if there(g + 1, NG):
                        turn(g + 1, (b + 1) % R)
                    if there(g - 1, NG):
                        outer(g - 1, (b - 1) % R)

                turn(0, 0)
                pe.wait_ge(consts, 16 * 5)
                pe.wait_ge(made, 1)
                over(pe, NG, R, 2, group)
                outer(NG - 1, (NG - 1) % R)


def layer3_nodes(nc, a, sem, sb, bank, ident, x3, means3, ends_t, out, node_rows):
    with ExitStack() as ctx:
        t_ = lambda name, shape, dt=F32: sb("f_" + name, shape, dt, ctx)
        R, A = 12, 6
        ring, short, two = range(R), range(A), range(2)
        w1 = t_("w1", [D, 2 * D])
        w2 = t_("w2", [D, 2, D])
        b1 = t_("b1", [D, 2])
        eps1 = t_("eps1", [P, 1])
        b2 = t_("b2", [65, D])
        part = t_("part", [65, D])
        b2s = t_("b2s", [65, D], BF16)
        ones = t_("ones", [65, P], BF16)
        x = [t_(f"x{b}", [P, K, D]) for b in ring]
        ag = [t_(f"ag{b}", [P, K, D]) for b in short]
        index = [t_(f"index{b}", [P, K], I32) for b in short]
        z = [t_(f"z{b}", [P, K, D]) for b in short]
        h, rn = ([t_(f"{n}{b}", [P, K, D]) for b in two] for n in ("h", "rn"))
        rt, ut, vt = ([t_(f"{n}{b}", [D, GC]) for b in two] for n in ("rt", "ut", "vt"))
        ln = [Stats(t_, f"ln{b}", 2 * K) for b in two]
        loaded = [sem(f"f_loaded{b}") for b in ring]
        stored = [sem(f"f_stored{b}") for b in short]
        gathered = [sem(f"f_gathered{b}", pool=True) for b in short]
        consts, rows_in, indices, made, made_s, step_s, stats, hs, normed, turned, rst, mm, relued2, mo, results, sums = (
            sem("f_" + s) for s in ("consts", "rows_in", "indices", "made", "made_s", "step_s", "stats", "hs", "normed",
                                    "turned", "rst", "mm", "relued2", "mo", "results", "sums"))
        flat = lambda t: t[:, :, :].rearrange("p k d -> p (k d)")
        passed = sem("passed")
        n_consts = 16 * 4
        with nc.Block() as block:
            @block.sync
            def _(sp):
                def load(g, c):
                    sp.dma_start(x[c][:, :, :], node_rows(x3, g)).then_inc(loaded[c], 16)

                def move(g, c, i):
                    sp.wait_ge(sums, g + 1)
                    sp.dma_start(node_rows(out, g), z[c % A][:, :, :]).then_inc(stored[c % A], 16)
                    if there(g + R, NG):
                        load(g + R, c)

                for b in range(4):
                    load(b, b)
                sp.dma_start(eps1[:, :], a["L3_gnn_eps"].rearrange("(o d) -> o d", o=1).broadcast_to([P, 1])).then_inc(rows_in, 16)
                sp.dma_start(b2[:, :], a["L3_gnn_b2"].rearrange("(o d) -> o d", o=1).broadcast_to([65, D])).then_inc(rows_in, 16)
                sp.dma_start(w1[:, :], a["L3_gnn_W1"]).then_inc(consts, 16)
                sp.dma_start(w2[:, :, :], a["L3_gnn_W2"].rearrange("(h q) d -> q h d", h=2)).then_inc(consts, 16)
                for h_ in two:
                    sp.dma_start(b1[:, h_:h_ + 1], a["L3_gnn_b1"][h_ * D:(h_ + 1) * D].rearrange("(q o) -> q o", o=1)).then_inc(consts, 16)
                for b in range(4, R):
                    load(b, b)
                over(sp, NG, R, R, move)
                for b in short:
                    sp.wait_ge(stored[b], 16 * len(range(b, NG, A)))

            @block.gpsimd
            def _(pool):
                def gather(g, b):
                    wait(pool, normed, g - A + 1)
                    pool.sem_inc(passed, 1)
                    pool.wait_ge(indices, g + 1)
                    pool.sem_inc(passed, 1)
                    for k in range(K):
                        pool.indirect_dma_start(
                            out=ag[b][:, k, :], out_offset=None, in_=means3[:, :],
                            in_offset=bass.IndirectOffsetOnAxis(ap=index[b][:, k:k + 1], axis=0)).then_inc(gathered[b], 16)

                for b in short:
                    gather(b, b)

                def next_group(g, b, i):
                    if there(g + A, NG):
                        gather(g + A, b)
                over(pool, NG, A, A, next_group)

            @block.vector
            def _(dve):
                def pair_moments(q, c):
                    return [lambda n=n: moments(dve, ln[c // 2 % 2], n, x[(c + n // K) % R][:, n % K, :])
                            for n in range(2 * K)]

                def wait_loaded(c, i):
                    for n in two:
                        dve.wait_ge(loaded[(c + n) % R], 16 * (i + (c + n) // R + 1))

                def set_index(g, c):
                    dve.tensor_copy(index[c % A][:, :], ends_t[:, ds(g * K, K)]).then_inc(indices, 1)

                def combine(g, c, i):
                    dve.wait_ge(hs, g + 1)
                    dve.wait_ge(gathered[c % A], 64 * (R // A * i + c // A + 1))
                    wait(dve, turned, g - 1)
                    dve.scalar_tensor_tensor(flat(rn[c % 2]), flat(h[c % 2]), eps1[:, 0:1], flat(ag[c % A]),
                                             ALU.mult, ALU.add).then_inc(normed, 1)
                    if there(g + A, NG):
                        set_index(g + A, c)

                def add_rows(g, c):
                    dve.wait_ge(results, g + 1)
                    dve.tensor_tensor(flat(z[c % A]), flat(z[c % A]), flat(x[c % R]), ALU.add).then_inc(sums, 1)

                def statistics(q, c, last, between):
                    s = ln[c // 2 % 2]
                    step = Steps(dve, step_s, q * STATS, passed, between)
                    step(roots(dve, step, s, last, 0, 2 * K))
                    minus_mean_over_root(dve, s, 0, 2 * K).then_inc(stats, 1)
                    step.rest()

                def pair(q, b, i):
                    g, c, between = 2 * q, 2 * b, []
                    for n in two:
                        if there(g - 4 + n, NG):
                            between.append(lambda n=n: add_rows(g - 4 + n, c - 4 + n))
                    if there(q + 3, NG // 2):
                        wait_loaded(c + 6, i)
                        between += pair_moments(q + 3, c + 6)[1:]
                    if there(q + 2, NG // 2):
                        statistics(q + 2, c + 4, pair_moments(q + 2, c + 4)[0](), between)
                    else:
                        for emit in between:
                            emit()
                    for n in two:
                        if there(g + 2 + n, NG):
                            combine(g + 2 + n, c + 2 + n, i)

                for b in short:
                    set_index(b, b)
                wait_loaded(0, 0)
                for emit in pair_moments(0, 0):
                    last = emit()
                statistics(0, 0, last, [])
                step = Steps(dve, made_s, 0, None)
                dve.wait_ge(rows_in, 32)
                step(dve.tensor_scalar(eps1[:, :], eps1[:, :], 1.0, None, ALU.add))
                bias_parts(dve, step, made, b2, part, b2s, ones)
                wait_loaded(2, 0)
                for emit in pair_moments(1, 2):
                    last = emit()
                wait_loaded(4, 0)
                statistics(1, 2, last, pair_moments(2, 4)[1:])
                for g in two:
                    combine(g, g, 0)
                over(dve, NG // 2, R // 2, 4, pair)
                for g in range(NG - 4, NG):
                    add_rows(g, g)

            @block.scalar
            def _(act):
                def normalize(g, c, i):
                    s, lo = ln[c // 2 % 2], c % 2 * K
                    act.wait_ge(stats, R // 2 * i + c // 2 + 1)
                    wait(act, normed, g - 1)
                    for k in range(K):
                        last = act.activation(h[c % 2][:, k, :], x[c % R][:, k, :], ACT.Relu,
                                              bias=s.nmr[:, lo + k:lo + k + 1], scale=s.rstd[:, lo + k:lo + k + 1])
                    last.then_inc(hs, 1)

                def evacuate(g, c):
                    act.wait_ge(turned, g + 1)
                    wait(act, mm, g - 1)
                    act.activation(rt[c % 2][:, :], bank[c % 2][:, 0:GC], ACT.Copy).then_inc(rst, 1)

                def relu(g, c):
                    act.wait_ge(mm, g + 1)
                    wait(act, mo, g - 1)
                    act.activation(ut[c % 2][:, :], bank[2 + 2 * (c % 2)][:, 0:GC], ACT.Relu, bias=b1[:, 0:1])
                    act.activation(vt[c % 2][:, :], bank[3 + 2 * (c % 2)][:, 0:GC], ACT.Relu, bias=b1[:, 1:2]).then_inc(relued2, 1)

                def result(g, c, i):
                    act.wait_ge(mo, g + 1)
                    wait(act, stored[c % A], 16 * (R // A * i + c // A))
                    act.activation(flat(z[c % A]), bank[6 + c % 2][0:P, 0:K * D], ACT.Relu).then_inc(results, 1)

                def group(g, c, i):
                    relu(g, c)
                    if there(g + 1, NG):
                        evacuate(g + 1, c + 1)
                    if there(g - 1, NG):
                        result(g - 1, c - 1, i)
                    if there(g + 3, NG):
                        normalize(g + 3, c + 3, i)

                for g in range(3):
                    normalize(g, g, 0)
                evacuate(0, 0)
                act.wait_ge(consts, n_consts)
                over(act, NG, R, 3, group)
                result(NG - 1, (NG - 1) % R, (NG - 1) // R)

            @block.tensor
            def _(pe):
                def turn(g, b):
                    pe.wait_ge(normed, g + 1)
                    for k in range(K):
                        last = pe.transpose(bank[b % 2][:, k * P:(k + 1) * P], rn[b % 2][:, k, :], ident[0:P, 0:P])
                    last.then_inc(turned, 1)

                def hidden(g, b):
                    pe.wait_ge(rst, g + 1)
                    wait(pe, relued2, g - 1)
                    pe.matmul(bank[2 + 2 * b][:, 0:GC], w1[:, 0:D], rt[b][:, :], start=True, stop=True)
                    pe.matmul(bank[3 + 2 * b][:, 0:GC], w1[:, D:2 * D], rt[b][:, :], start=True, stop=True).then_inc(mm, 1)

                def outer(g, b):
                    o = bank[6 + b]
                    wait(pe, results, g - 1)
                    put_bias(pe, o, ones, b2s)
                    pe.wait_ge(relued2, g + 1)
                    for k in range(K):
                        pe.matmul(o[0:P, k * D:(k + 1) * D], ut[b][:, k * P:(k + 1) * P], w2[:, 0, :], start=False, stop=False)
                    for k in range(K):
                        last = pe.matmul(o[0:P, k * D:(k + 1) * D], vt[b][:, k * P:(k + 1) * P], w2[:, 1, :],
                                         start=False, stop=(k == K - 1))
                    last.then_inc(mo, 1)

                def group(g, b, i):
                    hidden(g, b)
                    if there(g + 1, NG):
                        turn(g + 1, b + 1)
                    if there(g - 1, NG):
                        outer(g - 1, (b - 1) % 2)

                turn(0, 0)
                pe.wait_ge(consts, n_consts)
                pe.wait_ge(made, 1)
                over(pe, NG, 2, 2, group)
                outer(NG - 1, (NG - 1) % 2)


_INS = ['x', 'src', 'dst', 'L0_gnn_a_i', 'L0_gnn_a_j', 'L0_gnn_W', 'L1_gnn_agg_W', 'L1_gnn_agg_b', 'L1_gnn_edge_W1',
        'L1_gnn_edge_b1', 'L1_gnn_edge_W2', 'L1_gnn_edge_b2', 'L1_gnn_upd_W1', 'L1_gnn_upd_b1', 'L1_gnn_upd_W2',
        'L1_gnn_upd_b2', 'L1_gnn_ln_g', 'L1_gnn_ln_b', 'L1_gnn_res_W', 'L2_gnn_W', 'L3_gnn_eps', 'L3_gnn_W1',
        'L3_gnn_b1', 'L3_gnn_W2', 'L3_gnn_b2']


def kernel(**inputs):
    import numpy as _np
    import concourse.bacc as _bacc
    from concourse import mybir as _mybir
    from concourse.bass_utils import run_bass_kernel_spmd as _run

    nc = _bacc.Bacc("TRN2", target_bir_lowering=False, num_devices=1)
    laid = {name: _np.ascontiguousarray(inputs[name]) for name in _INS}
    src, dst = laid['src'], laid['dst']
    laid['src_t'] = _np.ascontiguousarray(src.reshape(ET, P).T)
    laid['dst_t'] = _np.ascontiguousarray(dst.reshape(ET, P).T)
    laid['dst_rows'] = _np.ascontiguousarray(dst.reshape(ET, P))
    laid['src_p'] = _np.ascontiguousarray(src.reshape(P, ET).T)
    laid['attr'] = _np.ascontiguousarray(_np.asarray(inputs['edge_attr_4']).T)
    laid['w2t'] = _np.ascontiguousarray(_np.asarray(inputs['L2_gnn_W']).T)
    arrays, aps = {}, {}
    for name, v in laid.items():
        arrays[f"in_{name}"] = v
        aps[name] = nc.dram_tensor(f"in_{name}", v.shape, _mybir.dt.from_np(v.dtype), kind="ExternalInput").ap()
    out = nc.dram_tensor("out_x", (N, D), F32, kind="ExternalOutput").ap()
    program(nc, aps, out)
    r = _run(nc, [arrays], core_ids=[0])
    return r.results[0]["out_x"]
```
